# Optimizing a Trainium2 kernel written in Bass

```python
import numpy as np
import jax
import jax.numpy as jnp

def _softmax(x, axis=-1):
    return jax.nn.softmax(x, axis=axis)

def _gelu(x):
    return jax.nn.gelu(x, approximate=True)

def _silu(x):
    return jax.nn.silu(x)

def _sigmoid(x):
    return jax.nn.sigmoid(x)

def _layernorm(x, axis=-1, eps=1e-05):
    m = jnp.mean(x, axis=axis, keepdims=True)
    v = jnp.var(x, axis=axis, keepdims=True)
    return (x - m) / jnp.sqrt(v + eps)

def _scatter_add(tgt, idx, src, axis=0):
    return tgt.at[idx].add(src)

def _segment_sum(src, seg, n):
    return jax.ops.segment_sum(src, seg, n)
kernel_name = 'mk_gps_d1_gnn_r8_30fe5f'

def setup_inputs(seed: int=0):
    np.random.seed(seed)
    _w = jnp.asarray

    def _rec_inputs():
        import jax
        import jax.numpy as jnp
        _gk = jax.random.key(seed)
        x = -0.0002117 + 1 * jax.random.normal(jax.random.fold_in(_gk, 1), (12500, 256), jnp.float32)
        _s = jax.random.randint(jax.random.fold_in(_gk, 2), (100000,), 0, 12500, jnp.int32)
        _d = jax.random.randint(jax.random.fold_in(_gk, 3), (100000,), 0, 12500, jnp.int32)
        _loop = jnp.arange(12500, dtype=jnp.int32)
        src = jnp.concatenate([_s, _d, _loop])
        dst = jnp.concatenate([_d, _s, _loop])
        _o = jnp.argsort(dst, stable=True)
        src = src[_o]
        dst = dst[_o]
        edge_weight = jax.random.uniform(jax.random.fold_in(_gk, 12), (212500,), jnp.float32, 0.0, 1)
        return (x, src, dst, edge_weight)
    x, src, dst, edge_weight = _rec_inputs()

    def _L0_gnn_setup():
        import jax, jax.numpy as jnp
        import numpy as np
        N = 12500
        E = 400000
        D_IN = 256
        D_OUT = 256
        key = jax.random.key(seed)
        k = jax.random.split(key, 8)
        stdv = 1.0 / np.sqrt(D_OUT)
        x = jax.random.normal(k[0], (N, D_IN), dtype=jnp.float32)
        edge_row = jax.random.randint(k[1], (E,), 0, N, dtype=jnp.int32)
        edge_col = jax.random.randint(k[2], (E,), 0, N, dtype=jnp.int32)
        edge_val = jax.random.uniform(k[3], (E,), dtype=jnp.float32)
        weight_l = jax.random.uniform(k[4], (D_IN, D_OUT), minval=-stdv, maxval=stdv, dtype=jnp.float32)
        bias_l = jax.random.uniform(k[5], (D_OUT,), minval=-stdv, maxval=stdv, dtype=jnp.float32)
        weight_r = jax.random.uniform(k[6], (D_IN, D_OUT), minval=-stdv, maxval=stdv, dtype=jnp.float32)
        bias_r = jax.random.uniform(k[7], (D_OUT,), minval=-stdv, maxval=stdv, dtype=jnp.float32)
        return {'x': x, 'edge_row': edge_row, 'edge_col': edge_col, 'edge_val': edge_val, 'weight_l': weight_l, 'bias_l': bias_l, 'weight_r': weight_r, 'bias_r': bias_r}
    _L0_gnn_all = _L0_gnn_setup()
    _L0_gnn_in = {k: v for k, v in _L0_gnn_all.items() if k in ('weight_l', 'bias_l', 'weight_r', 'bias_r')}
    del _L0_gnn_all

    def _L0_mix_setup():
        import jax, jax.numpy as jnp
        import numpy as np
        B, N, C, H = (8, 2048, 256, 8)
        D = C // H
        GH = C // 4
        key = jax.random.key(seed)
        ks = jax.random.split(key, 6)
        s = 0.02
        return {'x': jax.random.normal(ks[0], (B, N, C), dtype=jnp.float32), 'Wqkv': jax.random.normal(ks[1], (C, 3 * C), dtype=jnp.float32) * s, 'Wproj': jax.random.normal(ks[2], (C, C), dtype=jnp.float32) * s, 'bproj': jnp.zeros((C,), dtype=jnp.float32), 'ln_g': jnp.ones((C,), dtype=jnp.float32), 'ln_b': jnp.zeros((C,), dtype=jnp.float32), 'Wg1': jax.random.normal(ks[3], (C, GH), dtype=jnp.float32) * s, 'bg1': jnp.zeros((GH,), dtype=jnp.float32), 'Wg2': jax.random.normal(ks[4], (GH, C), dtype=jnp.float32) * s, 'bg2': jnp.zeros((C,), dtype=jnp.float32)}
    _L0_mix_all = _L0_mix_setup()
    _L0_mix_in = {k: v for k, v in _L0_mix_all.items() if k in ('Wqkv', 'Wproj', 'bproj', 'ln_g', 'ln_b', 'Wg1', 'bg1', 'Wg2', 'bg2')}
    del _L0_mix_all

    def _L0_ffn_setup():
        import jax, jax.numpy as jnp
        import numpy as np
        E = 8
        K = 2
        D = 256
        H = 512
        DOUT = 256
        EPS = 1e-05
        key = jax.random.key(seed)
        ks = jax.random.split(key, 9)
        s = 0.02
        return {'x': jax.random.normal(ks[0], (4, 1024, D), jnp.float32), 'gamma': 1.0 + 0.05 * jax.random.normal(ks[1], (D,), jnp.float32), 'beta': 0.05 * jax.random.normal(ks[2], (D,), jnp.float32), 'Wr': 0.01 * jax.random.normal(ks[3], (D, E), jnp.float32), 'br': jnp.zeros((E,), jnp.float32), 'W1': s * jax.random.normal(ks[4], (E, D, H), jnp.float32), 'b1': s * jax.random.normal(ks[5], (E, H), jnp.float32), 'W2': s * jax.random.normal(ks[6], (E, H, DOUT), jnp.float32), 'b2': s * jax.random.normal(ks[7], (E, DOUT), jnp.float32)}
    _L0_ffn_all = _L0_ffn_setup()
    _L0_ffn_in = {k: v for k, v in _L0_ffn_all.items() if k in ('gamma', 'beta', 'Wr', 'br', 'W1', 'b1', 'W2', 'b2')}
    del _L0_ffn_all
    return {'x': x, 'src': src, 'dst': dst, 'edge_weight': edge_weight, 'L0_gnn_weight_l': _L0_gnn_in['weight_l'], 'L0_gnn_bias_l': _L0_gnn_in['bias_l'], 'L0_gnn_weight_r': _L0_gnn_in['weight_r'], 'L0_gnn_bias_r': _L0_gnn_in['bias_r'], 'L0_mix_Wqkv': _L0_mix_in['Wqkv'], 'L0_mix_Wproj': _L0_mix_in['Wproj'], 'L0_mix_bproj': _L0_mix_in['bproj'], 'L0_mix_ln_g': _L0_mix_in['ln_g'], 'L0_mix_ln_b': _L0_mix_in['ln_b'], 'L0_mix_Wg1': _L0_mix_in['Wg1'], 'L0_mix_bg1': _L0_mix_in['bg1'], 'L0_mix_Wg2': _L0_mix_in['Wg2'], 'L0_mix_bg2': _L0_mix_in['bg2'], 'L0_ffn_gamma': _L0_ffn_in['gamma'], 'L0_ffn_beta': _L0_ffn_in['beta'], 'L0_ffn_Wr': _L0_ffn_in['Wr'], 'L0_ffn_br': _L0_ffn_in['br'], 'L0_ffn_W1': _L0_ffn_in['W1'], 'L0_ffn_b1': _L0_ffn_in['b1'], 'L0_ffn_W2': _L0_ffn_in['W2'], 'L0_ffn_b2': _L0_ffn_in['b2']}

def reference(x, src, dst, edge_weight, L0_gnn_weight_l, L0_gnn_bias_l, L0_gnn_weight_r, L0_gnn_bias_r, L0_mix_Wqkv, L0_mix_Wproj, L0_mix_bproj, L0_mix_ln_g, L0_mix_ln_b, L0_mix_Wg1, L0_mix_bg1, L0_mix_Wg2, L0_mix_bg2, L0_ffn_gamma, L0_ffn_beta, L0_ffn_Wr, L0_ffn_br, L0_ffn_W1, L0_ffn_b1, L0_ffn_W2, L0_ffn_b2):
    import jax
    import jax.numpy as jnp

    def _L0_gnn_ref(x, edge_row, edge_col, edge_val, weight_l, bias_l, weight_r, bias_r):
        import jax, jax.numpy as jnp
        import numpy as np
        N = 12500
        E = 400000
        D_IN = 256
        D_OUT = 256
        h = x @ weight_l
        msgs = edge_val[:, None] * h[edge_col]
        agg = jax.ops.segment_sum(msgs, edge_row, num_segments=N)
        out = agg + bias_l
        out = out + x @ weight_r + bias_r
        return out

    def _L0_mix_ref(x, Wqkv, Wproj, bproj, ln_g, ln_b, Wg1, bg1, Wg2, bg2):
        import jax, jax.numpy as jnp
        import numpy as np
        B, N, C, H = (8, 2048, 256, 8)
        D = C // H
        GH = C // 4
        b, n, c = x.shape
        h, d = (H, D)
        qkv = (x @ Wqkv).reshape(b, n, 3, h, d)
        q, k, v = (qkv[:, :, 0], qkv[:, :, 1], qkv[:, :, 2])
        k = jax.nn.softmax(k, axis=1)
        context = jnp.einsum('bnhd,bnhv->bhdv', k, v)
        out = jnp.einsum('bnhd,bhdv->bnhv', q, context).reshape(b, n, c)
        mu = jnp.mean(x, axis=-1, keepdims=True)
        var = jnp.var(x, axis=-1, keepdims=True)
        xn = (x - mu) * jax.lax.rsqrt(var + 1e-05) * ln_g + ln_b
        hgate = jax.nn.gelu(xn @ Wg1 + bg1, approximate=False)
        gate = jax.nn.sigmoid(hgate @ Wg2 + bg2)
        return out * gate @ Wproj + bproj

    def _L0_ffn_ref(x, gamma, beta, Wr, br, W1, b1, W2, b2):
        import jax, jax.numpy as jnp
        import numpy as np
        E = 8
        K = 2
        D = 256
        H = 512
        DOUT = 256
        EPS = 1e-05
        mu = jnp.mean(x, axis=-1, keepdims=True)
        var = jnp.mean(jnp.square(x - mu), axis=-1, keepdims=True)
        xn = (x - mu) * jax.lax.rsqrt(var + EPS) * gamma + beta
        logits = jnp.einsum('bsd,de->bse', xn, Wr) + br
        top_vals, top_idx = jax.lax.top_k(logits, K)
        w = jax.nn.softmax(top_vals, axis=-1)
        w_full = jnp.einsum('bsk,bske->bse', w, jax.nn.one_hot(top_idx, E, dtype=w.dtype))
        y = jnp.zeros(x.shape[:-1] + (DOUT,), x.dtype)
        for e in range(E):
            h = jax.nn.gelu(jnp.einsum('bsd,dh->bsh', xn, W1[e]) + b1[e], approximate=False)
            y_e = jnp.einsum('bsh,hd->bsd', h, W2[e]) + b2[e]
            y = y + y_e * w_full[..., e, None]
        return y
    xn = _layernorm(x, axis=-1)
    x = x + _L0_gnn_ref(xn, src, dst, edge_weight, L0_gnn_weight_l, L0_gnn_bias_l, L0_gnn_weight_r, L0_gnn_bias_r) + _L0_mix_ref(xn[None], L0_mix_Wqkv, L0_mix_Wproj, L0_mix_bproj, L0_mix_ln_g, L0_mix_ln_b, L0_mix_Wg1, L0_mix_bg1, L0_mix_Wg2, L0_mix_bg2)[0]
    x = x + _L0_ffn_ref(_layernorm(x, axis=-1)[None], L0_ffn_gamma, L0_ffn_beta, L0_ffn_Wr, L0_ffn_br, L0_ffn_W1, L0_ffn_b1, L0_ffn_W2, L0_ffn_b2)[0]
    return x

_drawn_inputs = setup_inputs


def setup_inputs(seed=0):
    import zlib

    import numpy as np

    out = dict(_drawn_inputs(seed))
    spreads = {'L0_mix_bproj': (0.0, 0.8),
     'L0_mix_ln_g': (1.0, 0.6),
     'L0_mix_ln_b': (0.0, 0.8),
     'L0_mix_bg1': (0.0, 0.8),
     'L0_mix_bg2': (0.0, 0.8),
     'L0_ffn_br': (0.0, 0.541)}
    factors = {'L0_gnn_bias_l': 18.228,
     'L0_gnn_bias_r': 17.957,
     'L0_mix_Wqkv': 8.0,
     'L0_mix_Wproj': 8.0,
     'L0_mix_Wg1': 8.0,
     'L0_mix_Wg2': 8.0,
     'L0_ffn_gamma': 57.103,
     'L0_ffn_beta': 53.655,
     'L0_ffn_b1': 64.0,
     'L0_ffn_b2': 47.234}
    for name, (base, spread) in spreads.items():
        noise = np.random.default_rng([zlib.crc32(name.encode()), seed]).standard_normal(out[name].shape)
        drawn = base * np.exp(spread * noise) if base else spread * noise
        out[name] = jnp.asarray(drawn.astype(out[name].dtype))
    for name, factor in factors.items():
        out[name] = (out[name] * factor).astype(out[name].dtype)
    return out
```

```python
from contextlib import ExitStack

import numpy as np

import concourse.bass as bass
from concourse import mybir

F32 = mybir.dt.float32
I32 = mybir.dt.int32
U32 = mybir.dt.uint32
ALU = mybir.AluOpType
ACT = mybir.ActivationFunctionType
AX_X = mybir.AxisListType.X

P = 128
N, D = 12500, 256
E = 212500
NH, HD = 8, 32
GH = 64
NE, HID = 8, 512
EPS = 1e-5

TILES = -(-N // P)
LAST = N - (TILES - 1) * P
PAIRS = TILES // 2
NPAD = TILES * P
HALF = D // P
HC = HID // P

CHUNK_GROUP = 16
EROWS = -(-E // P)
GROUPS = -(-EROWS // CHUNK_GROUP)
CHUNKS = GROUPS * CHUNK_GROUP
ETILES = CHUNKS // P
EFULL = E // P
NACC = 4
TRASH = NPAD
AGG_ROWS = NPAD + P
assert TILES % 2 == 0 and CHUNKS % P == 0 and CHUNK_GROUP % NACC == 0
TAIL_GROUPS = GROUPS - 2 * PAIRS
assert TAIL_GROUPS >= 1


def build(nc, t, scratch, out):
    with ExitStack() as ctx:
        def sb(name, shape, dt=F32):
            return ctx.enter_context(nc.sbuf_tensor(name, shape, dt))

        def sem(name):
            return ctx.enter_context(nc.semaphore(name))

        ident = sb("ident", [P, P])
        prior = sb("prior", [P, P])
        trash = sb("trash", [P, 1])
        iota8 = sb("iota8", [P, NE])
        ones = sb("ones", [P, P])
        zeros = sb("zeros", [P, 512])
        gscale = sb("gscale", [P, TILES])
        srcf = sb("srcf", [P, CHUNKS])
        wtf = sb("wtf", [P, CHUNKS])
        dsti = sb("dsti", [P, CHUNKS], I32)
        psum = [ctx.enter_context(nc.psum_tensor(f"bank{i}", [P, 512], F32)) for i in range(8)]

        setup_phase(nc, ctx, t, scratch, psum, ident, prior, trash, iota8, ones, zeros, srcf, wtf, dsti)
        with ExitStack() as mid:
            kmax = mid.enter_context(nc.sbuf_tensor("kmax", [P, D], F32))
            wk = mid.enter_context(nc.sbuf_tensor("wk", [P, HALF, D], F32))
            norm_phase(nc, t, scratch, psum, ident, gscale, kmax, wk)
            edge_mix_phase(nc, t, scratch, psum, ident, prior, trash, ones, zeros, gscale,
                           srcf, wtf, dsti, kmax, wk)
        wfull = sb("wfull", [P, TILES, NE])
        route_phase(nc, t, scratch, psum, ident, ones, iota8, wfull)
        expert_phase(nc, t, scratch, out, psum, ident, ones, wfull)


def setup_phase(nc, outer, t, scratch, psum, ident, prior, trash, iota8, ones, zeros, srcf, wtf, dsti):
    with ExitStack() as ctx:
        def sem(name):
            return ctx.enter_context(nc.semaphore(name))
        raw = {k: ctx.enter_context(nc.sbuf_tensor(f"raw_{k}", [P, ETILES, P], dt))
               for k, dt in (("src", I32), ("dst", I32), ("wt", F32))}
        flt = {k: ctx.enter_context(nc.sbuf_tensor(f"flt_{k}", [P, ETILES, P], F32)) for k in ("src", "dst")}
        s_clear = sem("setup_clear")
        s_load = sem("setup_load")
        s_const = sem("setup_const")
        s_pool = sem("setup_pool")
        s_flt = sem("setup_flt")
        s_turn = sem("setup_turn")
        s_taken = sem("setup_taken")
        s_zeroed = sem("setup_zeroed")
        s_tail = sem("setup_tail")
        dram = {"src": t["src"], "dst": t["dst"], "wt": t["edge_weight"]}
        block = ctx.enter_context(nc.Block())
        full_tiles = EFULL // P
        rest_rows = EFULL - full_tiles * P
        rest = E - EFULL * P

        @block.sync
        def _(sp):
            sp.wait_ge(s_clear, 4)
            for k, a in dram.items():
                sp.dma_start(raw[k][:, 0:full_tiles, :],
                             a[0:full_tiles * P * P].rearrange("(t c p) -> c t p", c=P, p=P)).then_inc(s_load, 16)
                sp.dma_start(raw[k][0:rest_rows, full_tiles, :],
                             a[full_tiles * P * P:EFULL * P].rearrange("(c p) -> c p", p=P)).then_inc(s_load, 16)
                sp.dma_start(raw[k][rest_rows:rest_rows + 1, full_tiles, 0:rest],
                             a[EFULL * P:E].rearrange("(a p) -> a p", a=1)).then_inc(s_load, 16)
            for acc in scratch["agg"]:
                v = acc.rearrange("(a p) d -> p a d", p=P)
                rows = AGG_ROWS // P
                for a in range(0, rows, 2):
                    n = min(2, rows - a)
                    sp.dma_start(v[:, a:a + n, :], zeros[:, 0:n * D].rearrange("p (a d) -> p a d", a=n)).then_inc(s_zeroed, 16)
            sp.wait_ge(s_zeroed, 16 * NACC * (-(-(AGG_ROWS // P) // 2)))

        @block.vector
        def _(dve):
            nc.vector.memset(raw["src"][:, full_tiles, :], 0).then_inc(s_clear, 1)
            nc.vector.memset(raw["dst"][:, full_tiles, :], 0).then_inc(s_clear, 1)
            nc.vector.memset(raw["wt"][:, full_tiles, :], 0.0).then_inc(s_clear, 1)
            nc.vector.memset(zeros[:], 0.0).then_inc(s_clear, 1)
            nc.vector.memset(ones[:], 1.0).then_inc(s_const, 1)
            dve.wait_ge(s_load, 16 * 9)
            nc.vector.tensor_copy(flt["src"][:], raw["src"][:]).then_inc(s_flt, 1)
            nc.vector.tensor_copy(flt["dst"][:], raw["dst"][:]).then_inc(s_flt, 1)
            n = 0
            for i in range(ETILES):
                for dst in (srcf, dsti, wtf):
                    dve.wait_ge(s_turn, n + 1)
                    nc.vector.tensor_copy(dst[:, i * P:(i + 1) * P], psum[n % 4][:, 0:P]).then_inc(s_taken, 1)
                    n += 1

        @block.gpsimd
        def _(pool):
            pool.wait_ge(s_const, 1)
            nc.gpsimd.affine_select(out=ident[:], in_=ones[:], compare_op=ALU.is_equal, fill=0.0, base=0,
                                    pattern=[[-1, P]], channel_multiplier=1).then_inc(s_const, 1)
            nc.gpsimd.iota(prior[:], pattern=[[0, P]], base=TRASH, channel_multiplier=1,
                           allow_small_or_imprecise_dtypes=True).then_inc(s_pool, 1)
            nc.gpsimd.iota(trash[:], pattern=[[0, 1]], base=TRASH, channel_multiplier=1,
                           allow_small_or_imprecise_dtypes=True)
            nc.gpsimd.iota(iota8[:], pattern=[[1, NE]], base=0, channel_multiplier=0,
                           allow_small_or_imprecise_dtypes=True)
            pool.wait_ge(s_pool, 1)
            nc.gpsimd.affine_select(out=prior[:], in_=prior[:], compare_op=ALU.is_ge, fill=0.0, base=-1,
                                    pattern=[[-1, P]], channel_multiplier=1).then_inc(s_pool, 1)

        @block.tensor
        def _(pe):
            pe.wait_ge(s_const, 2)
            pe.wait_ge(s_flt, 2)
            n = 0
            for i in range(ETILES):
                for a in (flt["src"], flt["dst"], raw["wt"]):
                    if n >= 4:
                        pe.wait_ge(s_taken, n - 3)
                    nc.tensor.transpose(psum[n % 4][:, 0:P], a[:, i, :], ident[:]).then_inc(s_turn, 1)
                    n += 1


def first(i):
    return isinstance(i, int) and i == 0


def norm_phase(nc, t, scratch, psum, ident, gscale, kmax, wk):
    with ExitStack() as ctx:
        def sb(name, shape, dt=F32):
            return ctx.enter_context(nc.sbuf_tensor(name, shape, dt))

        def sem(name):
            return ctx.enter_context(nc.semaphore(name))

        xin = sb("xin", [P, 2, D])
        xnr = sb("xnr", [P, 2, D])
        xnT = sb("xnT", [P, 2, HALF, P])
        hrow = sb("hrow", [P, 2, D])
        stat = sb("stat", [P, 2, 6])
        mv = sb("mv", [P, 2, 2])
        vare = sb("vare", [P, 2])
        std = sb("std", [P, 2])
        varall = sb("varall", [P, TILES])
        rstd = sb("rstd", [P, TILES])
        gvar = sb("gvar", [P, TILES])
        gstd = sb("gstd", [P, TILES])
        wl = sb("wl", [P, HALF, D])
        s_w = sem("n_weights")
        s_in = [sem(f"n_x_loaded{s}") for s in range(2)]
        s_step = sem("n_step")
        s_xn = sem("n_xn")
        s_T = sem("n_turned")
        s_xT = sem("n_xnT")
        s_hk = sem("n_hk")
        s_h = sem("n_h")
        s_max = sem("n_kmax")
        s_xst = [sem(f"n_xn_stored{s}") for s in range(2)]
        s_Tst = [sem(f"n_xnT_stored{s}") for s in range(2)]
        s_hst = [sem(f"n_h_stored{s}") for s in range(2)]
        s_std = sem("n_std")
        s_pad = sem("n_pad")
        s_fin = sem("n_gate_variance")
        s_gstd = sem("n_gate_std")
        T = [psum[0], psum[1]]
        H = [psum[2], psum[3]]
        K = [psum[4], psum[5]]
        block = ctx.enter_context(nc.Block())
        x = t["x"]

        @block.sync
        def _(sp):
            wkd = t["L0_mix_Wqkv"][:, D:2 * D].rearrange("(a p) n -> p a n", p=P)
            sp.dma_start(wl[:], t["L0_gnn_weight_l"].rearrange("(a p) n -> p a n", p=P)).then_inc(s_w, 16)
            sp.dma_start(wk[:], wkd).then_inc(s_w, 16)

            def load(i, s, last=False):
                if not first(i):
                    sp.wait_ge(s_xn, 2 * i + s - 1)
                if last:
                    sp.wait_ge(s_pad, 1)
                    sp.dma_start(xin[0:LAST, s, :], x[(TILES - 1) * P:N, :]).then_inc(s_in[s], 16)
                else:
                    sp.dma_start(xin[:, s, :], x[bass.ds(i * 2 * P + s * P, P), :]).then_inc(s_in[s], 16)

            load(0, 0)
            load(0, 1)
            with sp.Fori(1, PAIRS - 1) as i:
                load(i, 0)
                load(i, 1)
            load(PAIRS - 1, 0)
            load(PAIRS - 1, 1, last=True)

        @block.vector
        def _(dve):
            nc.vector.memset(kmax[:], -3.0e38).then_inc(s_max, 1)

            def normalise(i, s):
                n = 2 * i + s
                dve.wait_ge(s_in[s], 16 * i + 16)
                nc.vector.bn_stats(stat[:, s, :], xin[:, s, :]).then_inc(s_step, 1)
                dve.wait_ge(s_step, 4 * n + 1)
                dve.nop(nofuse=True)
                nc.vector.bn_aggr(mv[:, s, :], stat[:, s, :]).then_inc(s_step, 1)
                dve.wait_ge(s_step, 4 * n + 2)
                nc.vector.tensor_scalar(vare[:, s:s + 1], mv[:, s, 1:2], EPS, None, ALU.add).then_inc(s_step, 1)
                nc.vector.tensor_copy(varall[:, bass.ds(n, 1)], mv[:, s, 1:2])
                dve.wait_ge(s_std, n + 1)
                dve.nop(nofuse=True)
                nc.vector.reciprocal(rstd[:, bass.ds(n, 1)], std[:, s:s + 1]).then_inc(s_step, 1)
                dve.wait_ge(s_step, 4 * n + 4)
                if not first(i):
                    dve.wait_ge(s_T, n - 1)
                if not first(i):
                    dve.wait_ge(s_xst[s], 16 * i)
                nc.vector.tensor_scalar(xnr[:, s, :], xin[:, s, :], mv[:, s, 0:1], rstd[:, bass.ds(n, 1)],
                                        ALU.subtract, ALU.mult).then_inc(s_xn, 1)

            def maximum(i, s, rows=P):
                n = 2 * i + s
                dve.wait_ge(s_hk, n + 1)
                dve.wait_ge(s_max, n + 1)
                nc.vector.tensor_tensor(kmax[0:rows, :], kmax[0:rows, :], K[s][0:rows, 0:D],
                                        ALU.max).then_inc(s_max, 1)

            normalise(0, 0)
            normalise(0, 1)
            maximum(0, 0)
            maximum(0, 1)
            with dve.Fori(1, PAIRS - 1) as i:
                normalise(i, 0)
                normalise(i, 1)
                maximum(i, 0)
                maximum(i, 1)
            dve.wait_ge(s_xn, 2 * (PAIRS - 1))
            nc.vector.memset(xin[:, 1, :], 0.0).then_inc(s_pad, 1)
            normalise(PAIRS - 1, 0)
            normalise(PAIRS - 1, 1)
            maximum(PAIRS - 1, 0)
            maximum(PAIRS - 1, 1, rows=LAST)
            dve.wait_ge(s_xn, TILES)
            nc.vector.tensor_tensor(gvar[:], rstd[:], rstd[:], ALU.mult).then_inc(s_fin, 1)
            dve.wait_ge(s_fin, 1)
            nc.vector.tensor_tensor(gvar[:], gvar[:], varall[:], ALU.mult).then_inc(s_fin, 1)
            dve.wait_ge(s_fin, 2)
            nc.vector.tensor_scalar(gvar[:], gvar[:], EPS, None, ALU.add).then_inc(s_fin, 1)
            dve.wait_ge(s_gstd, 1)
            nc.vector.reciprocal(gscale[:], gstd[:])

        @block.gpsimd
        def _(pool):
            def store(i, s):
                n = 2 * i + s
                rows = bass.ds(i * 2 * P + s * P, P)
                for ready, src, dst, done in ((s_xn, xnr[:, s, :], scratch["xn"], s_xst),
                                              (s_xT, xnT[:, s, :, :].rearrange("p a c -> p (a c)"), scratch["xnT"], s_Tst),
                                              (s_h, hrow[:, s, :], scratch["h"], s_hst)):
                    pool.wait_ge(ready, n + 1)
                    pool.nop(nofuse=True)
                    pool.dma_start(dst[rows, :], src).then_inc(done[s], 16)
            store(0, 0)
            store(0, 1)
            with pool.Fori(1, PAIRS) as i:
                store(i, 0)
                store(i, 1)
            for done in (s_xst, s_Tst, s_hst):
                for s in range(2):
                    pool.wait_ge(done[s], 16 * PAIRS)

        @block.tensor
        def _(pe):
            pe.wait_ge(s_w, 32)

            def turn(i, s):
                n = 2 * i + s
                pe.wait_ge(s_xn, n + 1)
                if not first(i):
                    pe.wait_ge(s_xT, n - 1)
                for a in range(HALF):
                    last = nc.tensor.transpose(T[s][:, a * P:(a + 1) * P], xnr[:, s, a * P:(a + 1) * P], ident[:])
                last.then_inc(s_T, 1)

            def product(i, s):
                n = 2 * i + s
                pe.wait_ge(s_xT, n + 1)
                if not first(i):
                    pe.wait_ge(s_h, n - 1)
                if not first(i):
                    pe.wait_ge(s_max, n - 1)
                for bank, w in ((H[s], wl), (K[s], wk)):
                    for a in range(HALF):
                        last = nc.tensor.matmul(bank[:, 0:D], xnT[:, s, a, :], w[:, a, :],
                                                start=(a == 0), stop=(a == HALF - 1))
                last.then_inc(s_hk, 1)

            turn(0, 0)
            turn(0, 1)
            product(0, 0)
            product(0, 1)
            with pe.Fori(1, PAIRS) as i:
                turn(i, 0)
                turn(i, 1)
                product(i, 0)
                product(i, 1)

        @block.scalar
        def _(act):

            def unload(i, s):
                n = 2 * i + s
                act.wait_ge(s_T, n + 1)
                if not first(i):
                    act.wait_ge(s_hk, n - 1)
                if not first(i):
                    act.wait_ge(s_Tst[s], 16 * i)
                nc.scalar.copy(xnT[:, s, :, :].rearrange("p a c -> p (a c)"), T[s][:, 0:D]).then_inc(s_xT, 1)

            def emit(i, s):
                n = 2 * i + s
                act.wait_ge(s_hk, n + 1)
                if not first(i):
                    act.wait_ge(s_hst[s], 16 * i)
                nc.scalar.copy(hrow[:, s, :], H[s][:, 0:D]).then_inc(s_h, 1)

            def deviation(i, s):
                n = 2 * i + s
                act.wait_ge(s_step, 4 * n + 3)
                nc.scalar.activation(std[:, s:s + 1], vare[:, s:s + 1], ACT.Sqrt).then_inc(s_std, 1)

            deviation(0, 0)
            deviation(0, 1)
            unload(0, 0)
            unload(0, 1)
            emit(0, 0)
            emit(0, 1)
            with act.Fori(1, PAIRS) as i:
                deviation(i, 0)
                deviation(i, 1)
                unload(i, 0)
                unload(i, 1)
                emit(i, 0)
                emit(i, 1)
            act.wait_ge(s_fin, 3)
            nc.scalar.activation(gstd[:], gvar[:], ACT.Sqrt).then_inc(s_gstd, 1)


def edge_mix_phase(nc, t, scratch, psum, ident, prior, trash, ones, zeros, gscale, srcf, wtf, dsti, kmax, wk):
    with ExitStack() as ctx:
        def sb(name, shape, dt=F32):
            return ctx.enter_context(nc.sbuf_tensor(name, shape, dt))

        def sem(name):
            return ctx.enter_context(nc.semaphore(name))

        scol = sb("scol", [P, CHUNK_GROUP])
        gidx = sb("gidx", [P, CHUNK_GROUP], I32)
        sidx = sb("sidx", [P, CHUNK_GROUP], I32)
        rows = sb("rows", [P, CHUNK_GROUP, D])
        Emat = sb("Emat", [P, 2, P])
        seen = sb("seen", [P, 2, P])
        seen_sum = sb("seen_sum", [P, 2])
        msg = sb("msg", [P, NACC, D])
        B = [psum[0], psum[1]]
        M = [psum[2], psum[3]]
        s_gidx = sem("e_gather_rows_known")
        s_scol = sem("e_targets_staged")
        s_rows = [sem(f"e_rows_gathered{j}") for j in range(CHUNK_GROUP)]
        s_B = sem("e_targets_spread")
        s_E = sem("e_matrix")
        s_sidx = sem("e_add_rows_known")
        s_sum = sem("e_sums")
        s_msg = sem("e_message")
        s_add = [sem(f"e_added{r}") for r in range(NACC)]

        wq = sb("wq", [P, HALF, D])
        wqT = sb("wqT", [P, HALF, D])
        wv = sb("wv", [P, HALF, D])
        wproj = sb("wproj", [P, HALF, D])
        wr = sb("wr", [P, HALF, D])
        wg1 = sb("wg1", [P, HALF, GH])
        wg1s = sb("wg1s", [P, HALF, GH])
        wg2 = sb("wg2", [GH, D])
        lng = sb("lng", [P, HALF])
        lnb = sb("lnb", [P, HALF])
        lnb_all = sb("lnb_all", [P, HALF, P])
        bg1 = sb("bg1", [1, GH])
        bg2 = sb("bg2", [P, HALF])
        bg2h = sb("bg2h", [P, HALF])
        brows = sb("brows", [1, 3, D])
        bsum = sb("bsum", [1, D])
        hbias = sb("hbias", [P, GH])
        kcol = sb("kcol", [P, HALF])
        nmax = sb("nmax", [1, D])
        xr = sb("xr", [P, 2, D])
        xT = sb("xT", [P, 2, HALF, P])
        ek = sb("ek", [P, 2, D])
        GTs = sb("GTs", [P, HALF, D])
        rden = sb("rden", [P, HALF])
        cm = sb("cm", [P, HALF, D])
        M1 = sb("M1", [P, HALF, D])
        hp = sb("hp", [P, 2, GH])
        hg = sb("hg", [P, 2, GH])
        hgT = sb("hgT", [GH, 2, P])
        tg = sb("tg", [P, HALF, 2 * P])
        oT = sb("oT", [P, HALF, 2 * P])
        x1 = sb("x1", [P, 2, D])
        s_w = sem("m_weights")
        s_prep = sem("m_prep")
        s_pprep = sem("m_prep_tensor")
        s_x2 = [sem(f"m_tile_loaded{s}") for s in range(2)]
        s_k = sem("m_k")
        s_ek = sem("m_exp_k")
        s_gt = sem("m_gt")
        s_ctx = sem("m_context")
        s_cv = sem("m_context_vector")
        s_x3 = sem("m_pair_loaded")
        s_hg = sem("m_gate_hidden")
        s_hp = sem("m_gate_hidden_scaled")
        s_ge = sem("m_gelu")
        s_ht = sem("m_gelu_turned")
        s_hgt = sem("m_gelu_turned_out")
        s_gp = sem("m_gate")
        s_th = sem("m_tanh")
        s_op = sem("m_attention_out")
        s_o = sem("m_gated")
        s_p = sem("m_projected")
        s_x1 = sem("m_x1")
        s_x1st = sem("m_x1_stored")
        block = ctx.enter_context(nc.Block())
        LASTP = PAIRS - 1

        def halves(a):
            return a.rearrange("(a p) n -> p a n", p=P)

        def column(a):
            return a.rearrange("(a p) -> p a", p=P)

        def row(a):
            return a.rearrange("(a n) -> a n", a=1)

        def pair_rows(a, i):
            return a[bass.ds(i * 2 * P, 2 * P), :].rearrange("(a p) d -> p a d", p=P)

        weights = [(wq[:], halves(t["L0_mix_Wqkv"][:, 0:D])), (wv[:], halves(t["L0_mix_Wqkv"][:, 2 * D:3 * D])),
                   (wproj[:], halves(t["L0_mix_Wproj"])), (wr[:], halves(t["L0_gnn_weight_r"])),
                   (wg1[:], halves(t["L0_mix_Wg1"])), (wg2[:], t["L0_mix_Wg2"]),
                   (lng[:], column(t["L0_mix_ln_g"])), (lnb[:], column(t["L0_mix_ln_b"])),
                   (bg1[:], row(t["L0_mix_bg1"])), (bg2[:], column(t["L0_mix_bg2"])),
                   (brows[:, 0, :], row(t["L0_gnn_bias_l"])), (brows[:, 1, :], row(t["L0_gnn_bias_r"])),
                   (brows[:, 2, :], row(t["L0_mix_bproj"]))]
        WEIGHTS = 16 * len(weights)

        @block.sync
        def _(sp):
            for dst, src in weights:
                sp.dma_start(dst, src, allow_slow_non_contiguous=True).then_inc(s_w, 16)

            def load_tile(i, s):
                n = 2 * i + s
                if not first(i):
                    sp.wait_ge(s_gt, n - 1)
                at = bass.ds(i * 2 * P + s * P, P)
                sp.dma_start(xr[:, s, :], scratch["xn"][at, :]).then_inc(s_x2[s], 16)
                sp.dma_start(xT[:, s, :, :].rearrange("p a c -> p (a c)"), scratch["xnT"][at, :]).then_inc(s_x2[s], 16)

            def load_pair(i, last=False):
                sp.dma_start(xT[:].rearrange("p s a c -> p s (a c)"), pair_rows(scratch["xnT"], i)).then_inc(s_x3, 16)
                if last:
                    sp.dma_start(xr[:, 0, :], t["x"][(TILES - 2) * P:(TILES - 1) * P, :]).then_inc(s_x3, 16)
                    sp.dma_start(xr[0:LAST, 1, :], t["x"][(TILES - 1) * P:N, :]).then_inc(s_x3, 16)
                else:
                    sp.dma_start(xr[:], pair_rows(t["x"], i)).then_inc(s_x3, 16)

            def store_pair(i):
                sp.wait_ge(s_x1, i + 1)
                sp.dma_start(pair_rows(scratch["x1"], i), x1[:]).then_inc(s_x1st, 16)

            load_tile(0, 0)
            load_tile(0, 1)
            with sp.Fori(1, PAIRS) as i:
                load_tile(i, 0)
                load_tile(i, 1)
            sp.wait_ge(s_gt, TILES)
            load_pair(0)
            with sp.Fori(0, LASTP - 1) as i:
                store_pair(i)
                load_pair(i + 1)
            store_pair(LASTP - 1)
            load_pair(LASTP, last=True)
            store_pair(LASTP)
            sp.wait_ge(s_x1st, 16 * PAIRS)

        @block.gpsimd
        def _(pool):
            def gather(j):
                pool.indirect_dma_start(rows[:, j, :], None, scratch["h"][:, :],
                                        bass.IndirectOffsetOnAxis(ap=gidx[:, j:j + 1], axis=0)).then_inc(s_rows[j], 16)

            def group(g, last=False):
                for j in range(CHUNK_GROUP):
                    n = CHUNK_GROUP * g + j
                    r = j % NACC
                    uses = (CHUNK_GROUP // NACC) * g + j // NACC
                    pool.wait_ge(s_sidx, n + 1)
                    pool.wait_ge(s_msg, n + 1)
                    if not (first(g) and j < NACC):
                        pool.wait_ge(s_add[r], 16 * uses)
                    pool.nop(nofuse=True)
                    pool.indirect_dma_start(scratch["agg"][r][:, :],
                                            bass.IndirectOffsetOnAxis(ap=sidx[:, j:j + 1], axis=0),
                                            msg[:, r, :], None, compute_op=ALU.add).then_inc(s_add[r], 16)
                    if not last:
                        pool.wait_ge(s_gidx, n + CHUNK_GROUP + 1)
                        pool.nop(nofuse=True)
                        gather(j)

            pool.wait_ge(s_gidx, CHUNK_GROUP)
            for j in range(CHUNK_GROUP):
                gather(j)
            group(0)
            with pool.Fori(1, GROUPS - 1) as g:
                group(g)
            group(GROUPS - 1, last=True)
            for r in range(NACC):
                pool.wait_ge(s_add[r], 16 * CHUNKS // NACC)

        @block.vector
        def _(dve):
            nc.vector.tensor_copy(gidx[:], dsti[:, 0:CHUNK_GROUP]).then_inc(s_gidx, CHUNK_GROUP)
            nc.vector.tensor_copy(scol[:], srcf[:, 0:CHUNK_GROUP]).then_inc(s_scol, CHUNK_GROUP)
            nc.vector.memset(cm[:], 0.0).then_inc(s_prep, 1)
            dve.wait_ge(s_pprep, 1)
            nc.vector.tensor_reduce(kcol[:], psum[4][:, 0:D].rearrange("p (a c) -> p a c", a=HALF), AX_X,
                                    ALU.max).then_inc(s_prep, 1)
            dve.wait_ge(s_w, WEIGHTS)
            for a in range(HALF):
                nc.vector.tensor_scalar(wg1s[:, a, :], wg1[:, a, :], lng[:, a:a + 1], None, ALU.mult)
                nc.vector.tensor_scalar(lnb_all[:, a, :], ones[:], lnb[:, a:a + 1], None, ALU.mult)
            nc.vector.tensor_scalar(bg2h[:], bg2[:], 0.5, None, ALU.mult)
            nc.vector.tensor_tensor(bsum[:], brows[:, 0, :], brows[:, 1, :], ALU.add).then_inc(s_prep, 1)
            dve.wait_ge(s_prep, 3)
            nc.vector.tensor_tensor(bsum[:], bsum[:], brows[:, 2, :], ALU.add).then_inc(s_prep, 1)
            dve.wait_ge(s_pprep, 2)
            nc.vector.tensor_scalar(nmax[:], psum[5][0:1, 0:D], -1.0, None, ALU.mult).then_inc(s_prep, 1)
            dve.wait_ge(s_pprep, 3)
            nc.vector.tensor_copy(hbias[:], psum[6][:, 0:GH]).then_inc(s_prep, 1)
            nc.vector.tensor_copy(wqT[:].rearrange("p a n -> p (a n)"), psum[7][:, :]).then_inc(s_prep, 1)

            def edge(g, j, last):
                n = CHUNK_GROUP * g + j
                s = j % 2
                dve.wait_ge(s_B, n + 1)
                if not (first(g) and j < 2):
                    dve.wait_ge(s_sum, n - 1)
                nc.vector.tensor_scalar(Emat[:, s, :], B[s][:, 0:P], srcf[:, bass.ds(n, 1)], wtf[:, bass.ds(n, 1)],
                                        ALU.is_equal, ALU.mult)
                nc.vector.scalar_tensor_tensor(out=seen[:, s, :], in0=B[s][:, 0:P], scalar=srcf[:, bass.ds(n, 1)],
                                               in1=prior[:], op0=ALU.is_equal, op1=ALU.mult,
                                               accum_out=seen_sum[:, s:s + 1]).then_inc(s_E, 1)
                dve.wait_ge(s_E, n + 1)
                if not first(g):
                    dve.wait_ge(s_add[j % NACC], 16 * ((CHUNK_GROUP // NACC) * (g - 1) + j // NACC + 1))
                nc.vector.tensor_scalar(sidx[:, j:j + 1], seen_sum[:, s:s + 1], trash[:, 0:1],
                                        srcf[:, bass.ds(n, 1)], ALU.min, ALU.max).then_inc(s_sidx, 1)
                if not last:
                    nc.vector.tensor_copy(scol[:, j:j + 1], srcf[:, bass.ds(n + CHUNK_GROUP, 1)]).then_inc(s_scol, 1)
                    dve.wait_ge(s_rows[j], 16 * (g + 1))
                    nc.vector.tensor_copy(gidx[:, j:j + 1], dsti[:, bass.ds(n + CHUNK_GROUP, 1)]).then_inc(s_gidx, 1)

            def gate_scale(i):
                dve.wait_ge(s_hg, i + 1)
                if not first(i):
                    dve.wait_ge(s_ge, i)
                for s in range(2):
                    last = nc.vector.scalar_tensor_tensor(out=hp[:, s, :], in0=psum[4][:, s * GH:(s + 1) * GH],
                                                          scalar=gscale[:, bass.ds(2 * i + s, 1)], in1=hbias[:],
                                                          op0=ALU.mult, op1=ALU.add)
                last.then_inc(s_hp, 1)

            def gate_apply(i):
                dve.wait_ge(s_th, i + 1)
                dve.wait_ge(s_op, i + 1)
                if not first(i):
                    dve.wait_ge(s_p, i)
                nc.vector.scalar_tensor_tensor(out=oT[:].rearrange("p a c -> p (a c)"),
                                               in0=tg[:].rearrange("p a c -> p (a c)"), scalar=1.0,
                                               in1=psum[6][:, :], op0=ALU.add, op1=ALU.mult).then_inc(s_o, 1)

            def residual(i, last=False):
                dve.wait_ge(s_p, i + 1)
                dve.wait_ge(s_x3, 32 * (i + 1) + 16 * last)
                if not first(i):
                    dve.wait_ge(s_x1st, 16 * i)
                nc.vector.tensor_tensor(x1[:].rearrange("p a d -> p (a d)"), xr[:].rearrange("p a d -> p (a d)"),
                                        psum[7][:, :], ALU.add).then_inc(s_x1, 1)

            def group(g, steps, last=False):
                for j in range(CHUNK_GROUP):
                    edge(g, j, last)
                    for at, what in steps:
                        if at == j:
                            what()

            def mix_steps(i, last=False):
                return [(1, lambda: gate_scale(i)), (9, lambda: gate_apply(i)), (13, lambda: residual(i, last))]

            group(0, [])
            with dve.Fori(1, PAIRS) as g:
                group(g, [])
            dve.wait_ge(s_gt, TILES)
            nc.vector.tensor_copy(GTs[:].rearrange("p a n -> p (a n)"), psum[5][:, :]).then_inc(s_cv, 1)
            nc.vector.reciprocal(rden[:], psum[6][:, 0:HALF]).then_inc(s_cv, 1)
            dve.wait_ge(s_cv, 2)
            dve.wait_ge(s_ctx, 1)
            for a in range(HALF):
                for q in range(P // HD):
                    v = a * P + q * HD
                    blk = slice(q * HD, (q + 1) * HD)
                    last = nc.vector.tensor_scalar(cm[blk, a, v:v + HD], psum[4][blk, a * D + v:a * D + v + HD],
                                                   rden[blk, a:a + 1], 0.5, ALU.mult, ALU.mult)
            last.then_inc(s_cv, 1)
            dve.wait_ge(s_ctx, 2)
            nc.vector.tensor_copy(M1[:].rearrange("p a n -> p (a n)"), psum[7][:, :]).then_inc(s_cv, 1)
            group(PAIRS, mix_steps(0))
            with dve.Fori(1, LASTP) as i:
                group(PAIRS + i, mix_steps(i))
            group(PAIRS + LASTP, mix_steps(LASTP, last=True))
            if TAIL_GROUPS > 1:
                with dve.Fori(2 * PAIRS, GROUPS - 1) as g:
                    group(g, [])
            group(GROUPS - 1, [], last=True)

        @block.tensor
        def _(pe):
            for a in range(HALF):
                last = nc.tensor.transpose(psum[4][:, a * P:(a + 1) * P], kmax[:, a * P:(a + 1) * P], ident[:])
            last.then_inc(s_pprep, 1)
            pe.wait_ge(s_prep, 2)
            for a in range(HALF):
                last = nc.tensor.matmul(psum[5][0:1, a * P:(a + 1) * P], kcol[:, a:a + 1], ident[:], start=True, stop=True)
            last.then_inc(s_pprep, 1)
            pe.wait_ge(s_w, WEIGHTS)
            pe.wait_ge(s_prep, 4)
            for a in range(HALF):
                nc.tensor.matmul(psum[6][:, 0:GH], lnb_all[:, a, :], wg1[:, a, :], start=(a == 0), stop=False)
            nc.tensor.matmul(psum[6][:, 0:GH], ones[0:1, :], bg1[:], start=False, stop=True)
            for a in range(HALF):
                for b in range(HALF):
                    last = nc.tensor.transpose(psum[7][:, a * D + b * P:a * D + (b + 1) * P],
                                               wq[:, b, a * P:(a + 1) * P], ident[:])
            last.then_inc(s_pprep, 1)
            pe.wait_ge(s_prep, 7)

            def spread(g, j):
                n = CHUNK_GROUP * g + j
                pe.wait_ge(s_scol, n + 1)
                if not (first(g) and j < 2):
                    pe.wait_ge(s_E, n - 1)
                nc.tensor.matmul(B[j % 2][:, 0:P], scol[:, j:j + 1].to_broadcast([P, P]), ident[:],
                                 start=True, stop=True).then_inc(s_B, 1)

            def message(g, j):
                n = CHUNK_GROUP * g + j
                pe.wait_ge(s_rows[j], 16 * (g + 1))
                pe.wait_ge(s_E, n + 1)
                if not (first(g) and j < 2):
                    pe.wait_ge(s_msg, n - 1)
                nc.tensor.matmul(M[j % 2][:, 0:D], Emat[:, j % 2, :], rows[:, j, :],
                                 start=True, stop=True).then_inc(s_sum, 1)

            def keys(i, s):
                n = 2 * i + s
                pe.wait_ge(s_x2[s], 32 * (i + 1))
                if not (first(i) and s == 0):
                    pe.wait_ge(s_ek, n)
                for a in range(HALF):
                    nc.tensor.matmul(psum[4][:, 0:D], xT[:, s, a, :], wk[:, a, :], start=(a == 0), stop=False)
                nc.tensor.matmul(psum[4][:, 0:D], ones[0:1, :], nmax[:], start=False, stop=True).then_inc(s_k, 1)

            def context(i, s, rws=P):
                n = 2 * i + s
                start, stop = first(i) and s == 0, rws < P
                pe.wait_ge(s_ek, n + 1)
                for a in range(HALF):
                    nc.tensor.matmul(psum[5][:, a * D:(a + 1) * D], xr[0:rws, s, a * P:(a + 1) * P], ek[0:rws, s, :],
                                     start=start and a == 0, stop=stop, skip_group_check=True)
                for a in range(HALF):
                    last = nc.tensor.matmul(psum[6][:, a:a + 1], ek[0:rws, s, a * P:(a + 1) * P], ones[0:rws, 0:1],
                                            start=start and a == 0, stop=stop, skip_group_check=True)
                last.then_inc(s_gt, 1)

            def gate_hidden(i, last):
                pe.wait_ge(s_x3, 32 * (i + 1) + 16 * last)
                if not first(i):
                    pe.wait_ge(s_hgt, i)
                for s in range(2):
                    for a in range(HALF):
                        mm = nc.tensor.matmul(psum[4][:, s * GH:(s + 1) * GH], xT[:, s, a, :], wg1s[:, a, :],
                                              start=(a == 0), stop=(a == HALF - 1))
                mm.then_inc(s_hg, 1)

            def gate_turn(i):
                pe.wait_ge(s_ge, i + 1)
                pe.nop(nofuse=True)
                for s in range(2):
                    mm = nc.tensor.transpose(psum[4][0:GH, (s + 1) * P:(s + 2) * P], hg[:, s, :], ident[:])
                mm.then_inc(s_ht, 1)

            def gate_out(i):
                pe.wait_ge(s_hgt, i + 1)
                if not first(i):
                    pe.wait_ge(s_th, i)
                for a in range(HALF):
                    mm = nc.tensor.matmul(psum[5][:, a * D:(a + 1) * D], wg2[:, a * P:(a + 1) * P],
                                          hgT[:].rearrange("p s c -> p (s c)"), start=True, stop=True)
                mm.then_inc(s_gp, 1)
                if not first(i):
                    pe.wait_ge(s_o, i)
                for a in range(HALF):
                    for b in range(HALF):
                        mm = nc.tensor.matmul(psum[6][:, a * D:(a + 1) * D], M1[:, b, a * P:(a + 1) * P], xT[:, :, b, :],
                                              start=(b == 0), stop=(b == HALF - 1))
                mm.then_inc(s_op, 1)

            def project(i):
                pe.wait_ge(s_o, i + 1)
                if not first(i):
                    pe.wait_ge(s_x1, i)
                for s in range(2):
                    bank = psum[7][:, s * D:(s + 1) * D]
                    for a in range(HALF):
                        nc.tensor.matmul(bank, oT[:, a, s * P:(s + 1) * P], wproj[:, a, :], start=(a == 0), stop=False)
                    for a in range(HALF):
                        nc.tensor.matmul(bank, xT[:, s, a, :], wr[:, a, :], start=False, stop=False)
                    mm = nc.tensor.matmul(bank, ones[0:1, :], bsum[:], start=False, stop=True)
                mm.then_inc(s_p, 1)

            def group(g, steps):
                for j in range(CHUNK_GROUP):
                    spread(g, j)
                    if j >= 1:
                        message(g, j - 1)
                    for at, what in steps:
                        if at == j:
                            what()
                message(g, CHUNK_GROUP - 1)

            def context_steps(i, last=False):
                return [(0, lambda: keys(i, 0)), (4, lambda: context(i, 0)), (5, lambda: keys(i, 1)),
                        (9, lambda: context(i, 1, LAST if last else P))]

            def mix_steps(i, last=False):
                return [(0, lambda: gate_hidden(i, last)), (4, lambda: gate_turn(i)), (8, lambda: gate_out(i)),
                        (12, lambda: project(i))]

            group(0, context_steps(0))
            with pe.Fori(1, LASTP) as g:
                group(g, context_steps(g))
            group(LASTP, context_steps(LASTP, last=True))
            pe.wait_ge(s_cv, 2)
            for a in range(HALF):
                for b in range(HALF):
                    mm = nc.tensor.matmul(psum[4][:, a * D:(a + 1) * D], GTs[:, b, a * P:(a + 1) * P], wv[:, b, :],
                                          start=(b == 0), stop=(b == HALF - 1))
            mm.then_inc(s_ctx, 1)
            pe.wait_ge(s_cv, 3)
            for a in range(HALF):
                for b in range(HALF):
                    mm = nc.tensor.matmul(psum[7][:, a * D:(a + 1) * D], wqT[:, b, a * P:(a + 1) * P], cm[:, b, :],
                                          start=(b == 0), stop=(b == HALF - 1))
            mm.then_inc(s_ctx, 1)
            pe.wait_ge(s_cv, 4)
            group(PAIRS, mix_steps(0))
            with pe.Fori(1, LASTP) as i:
                group(PAIRS + i, mix_steps(i))
            group(PAIRS + LASTP, mix_steps(LASTP, last=True))
            with pe.Fori(2 * PAIRS, GROUPS) as g:
                group(g, [])

        @block.scalar
        def _(act):
            def take(g, j):
                n = CHUNK_GROUP * g + j
                act.wait_ge(s_sum, n + 1)
                if not (first(g) and j < NACC):
                    act.wait_ge(s_add[j % NACC], 16 * ((CHUNK_GROUP // NACC) * g + j // NACC))
                nc.scalar.copy(msg[:, j % NACC, :], M[j % 2][:, 0:D]).then_inc(s_msg, 1)

            def exponential(i, s):
                n = 2 * i + s
                act.wait_ge(s_k, n + 1)
                if not first(i):
                    act.wait_ge(s_gt, n - 1)
                nc.scalar.activation(ek[:, s, :], psum[4][:, 0:D], ACT.Exp).then_inc(s_ek, 1)

            def gelu(i):
                act.wait_ge(s_hp, i + 1)
                if not first(i):
                    act.wait_ge(s_ht, i)
                nc.scalar.activation(hg[:], hp[:], ACT.Gelu).then_inc(s_ge, 1)

            def gelu_out(i):
                act.wait_ge(s_ht, i + 1)
                if not first(i):
                    act.wait_ge(s_gp, i)
                nc.scalar.copy(hgT[:].rearrange("p s c -> p (s c)"), psum[4][0:GH, P:3 * P]).then_inc(s_hgt, 1)

            def tanh(i):
                act.wait_ge(s_gp, i + 1)
                if not first(i):
                    act.wait_ge(s_o, i)
                for a in range(HALF):
                    last = nc.scalar.activation(tg[:, a, :], psum[5][:, a * D:(a + 1) * D], ACT.Tanh,
                                                bias=bg2h[:, a:a + 1], scale=0.5)
                last.then_inc(s_th, 1)

            def group(g, steps):
                for j in range(CHUNK_GROUP):
                    take(g, j)
                    for at, what in steps:
                        if at == j:
                            what()

            def mix_steps(i):
                return [(2, lambda: gelu(i)), (5, lambda: gelu_out(i)), (9, lambda: tanh(i))]

            def exp_steps(i):
                return [(2, lambda: exponential(i, 0)), (7, lambda: exponential(i, 1))]

            group(0, exp_steps(0))
            with act.Fori(1, PAIRS) as g:
                group(g, exp_steps(g))
            group(PAIRS, mix_steps(0))
            with act.Fori(1, PAIRS) as i:
                group(PAIRS + i, mix_steps(i))
            with act.Fori(2 * PAIRS, GROUPS) as g:
                group(g, [])


def over_pairs(engine, body):
    body(0, 0)
    body(0, 1)
    with engine.Fori(1, PAIRS // 2) as k:
        body(k, 0)
        body(k, 1)
    if PAIRS % 2:
        body(PAIRS // 2, 0)


def before(k, s):
    return (k, 0) if s == 1 else (k - 1, 1)


def pair_of(a, i, width=2 * P):
    return a[bass.ds(i * width, width), :].rearrange("(a p) d -> p a d", p=P)


def route_phase(nc, t, scratch, psum, ident, ones, iota8, wfull):
    with ExitStack() as ctx:
        def sb(name, shape, dt=F32):
            return ctx.enter_context(nc.sbuf_tensor(name, shape, dt))

        def sem(name):
            return ctx.enter_context(nc.semaphore(name))

        xin = sb("r_xin", [P, 2, 2, D])
        agg = [sb(f"r_agg{r}", [P, 2, 2, D]) for r in range(NACC)]
        half = sb("r_half", [P, 2, 2, D])
        x1 = sb("r_x1", [P, 2, 2, D])
        z = sb("r_z", [P, 2, 2, D])
        xf = sb("r_xf", [P, 2, HALF, 2 * P])
        stat = sb("r_stat", [P, 2, 6])
        mv = sb("r_mv", [P, 2, 2, 2])
        vs = sb("r_vs", [P, 2, 2])
        std = sb("r_std", [P, 2, 2])
        scl = sb("r_scl", [P, 2, 2])
        lg = sb("r_lg", [P, 2, NE])
        top = sb("r_top", [P, 2, NE])
        idx = sb("r_idx", [P, 2, NE], U32)
        gap = sb("r_gap", [P, TILES])
        best = sb("r_best", [P, 2, TILES])
        w12 = sb("r_w12", [P, 2, TILES])
        hit = sb("r_hit", [P, TILES, NE])
        gamma = sb("r_gamma", [P, HALF])
        beta = sb("r_beta", [P, HALF])
        wrt = sb("r_wrt", [P, HALF, NE])
        br = sb("r_br", [1, NE])
        s_w = sem("r_weights")
        s_ld = [sem(f"r_loaded{s}") for s in range(2)]
        s_ld2 = [sem(f"r_loaded_rest{s}") for s in range(2)]
        s_half = sem("r_half_sum")
        s_sum = sem("r_sum")
        s_st = sem("r_stat_step")
        s_std = sem("r_std")
        s_scl = sem("r_scale")
        s_z = sem("r_z")
        s_T = sem("r_turned")
        s_xf = sem("r_xf")
        s_L = sem("r_logits")
        s_lg = sem("r_route_step")
        s_x1st = [sem(f"r_x1_stored{s}") for s in range(2)]
        s_xfst = [sem(f"r_xf_stored{s}") for s in range(2)]
        s_fin = sem("r_fin")
        s_tanh = sem("r_tanh")
        T = [psum[0], psum[1]]
        L = [psum[2], psum[3]]
        block = ctx.enter_context(nc.Block())

        @block.sync
        def _(sp):
            for dst, src in ((gamma[:], t["L0_ffn_gamma"].rearrange("(a p) -> p a", p=P)),
                             (beta[:], t["L0_ffn_beta"].rearrange("(a p) -> p a", p=P)),
                             (wrt[:], t["L0_ffn_Wr"].rearrange("(a p) n -> p a n", p=P)),
                             (br[:], t["L0_ffn_br"].rearrange("(a n) -> a n", a=1))):
                sp.dma_start(dst, src, allow_slow_non_contiguous=True).then_inc(s_w, 16)

            def load(k, s):
                i = 2 * k + s
                if not first(k):
                    sp.wait_ge(s_sum, 3 * i - 3)
                    sp.nop(nofuse=True)
                sp.dma_start(xin[:, s], pair_of(scratch["x1"], i)).then_inc(s_ld[s], 16)
                for r in range(NACC):
                    sp.dma_start(agg[r][:, s], pair_of(scratch["agg"][r], i)).then_inc((s_ld if r < 2 else s_ld2)[s], 16)

            def store_x1(k, s):
                sp.wait_ge(s_sum, 3 * (2 * k + s) + 3)
                sp.nop(nofuse=True)
                sp.dma_start(pair_of(scratch["x1"], 2 * k + s), x1[:, s]).then_inc(s_x1st[s], 16)

            def store_xf(k, s):
                i = 2 * k + s
                sp.wait_ge(s_xf, i + 1)
                sp.nop(nofuse=True)
                sp.dma_start(scratch["xf"][bass.ds(i * P, P), :],
                             xf[:, s].rearrange("p a c -> p (a c)")).then_inc(s_xfst[s], 16)

            def body(k, s):
                if not (isinstance(k, int) and 2 * k + s == PAIRS - 1):
                    load(*((k, 1) if s == 0 else (k + 1, 0)))
                store_x1(k, s)
                if not (first(k) and s == 0):
                    store_xf(*before(k, s))

            load(0, 0)
            over_pairs(sp, body)
            store_xf(*divmod(PAIRS - 1, 2))
            for s in range(2):
                uses = (PAIRS + 1 - s) // 2
                sp.wait_ge(s_x1st[s], 16 * uses)
                sp.wait_ge(s_xfst[s], 16 * uses)
                sp.nop(nofuse=True)

        @block.gpsimd
        def _(pool):
            def body(k, s):
                i = 2 * k + s
                pool.wait_ge(s_ld2[s], 32 * k + 32)
                if not first(k):
                    pool.wait_ge(s_sum, 3 * i - 3)
                nc.gpsimd.tensor_tensor(half[:, s], agg[2][:, s], agg[3][:, s], ALU.add).then_inc(s_half, 1)
            over_pairs(pool, body)

        @block.vector
        def _(dve):
            def gather_sums(k, s):
                i = 2 * k + s
                dve.wait_ge(s_ld[s], 48 * k + 48)
                if not first(k):
                    dve.wait_ge(s_z, i - 1)
                    dve.wait_ge(s_x1st[s], 16 * k)
                nc.vector.tensor_tensor(x1[:, s], xin[:, s], agg[0][:, s], ALU.add).then_inc(s_sum, 1)
                dve.wait_ge(s_sum, 3 * i + 1)
                nc.vector.tensor_tensor(x1[:, s], x1[:, s], agg[1][:, s], ALU.add).then_inc(s_sum, 1)
                dve.wait_ge(s_sum, 3 * i + 2)
                dve.wait_ge(s_half, i + 1)
                nc.vector.tensor_tensor(x1[:, s], x1[:, s], half[:, s], ALU.add).then_inc(s_sum, 1)
                dve.wait_ge(s_sum, 3 * i + 3)
                for c in range(2):
                    last = nc.vector.bn_stats(stat[:, c, :], x1[:, s, c, :])
                last.then_inc(s_st, 1)
                dve.wait_ge(s_st, 3 * i + 1)
                dve.nop(nofuse=True)
                for c in range(2):
                    last = nc.vector.bn_aggr(mv[:, s, c, :], stat[:, c, :])
                last.then_inc(s_st, 1)
                dve.wait_ge(s_st, 3 * i + 2)
                nc.vector.tensor_scalar(vs[:, s], mv[:, s, :, 1], 1.0 + EPS, EPS * EPS, ALU.mult, ALU.add).then_inc(s_st, 1)

            def normalise(k, s):
                i = 2 * k + s
                dve.wait_ge(s_std, i + 1)
                nc.vector.reciprocal(scl[:, s], std[:, s]).then_inc(s_scl, 1)
                dve.wait_ge(s_scl, i + 1)
                if not first(k):
                    dve.wait_ge(s_T, i - 1)
                for c in range(2):
                    last = nc.vector.tensor_scalar(z[:, s, c, :], x1[:, s, c, :], mv[:, s, c, 0:1], scl[:, s, c:c + 1],
                                                   ALU.subtract, ALU.mult)
                last.then_inc(s_z, 1)

            def route(k, s):
                i = 2 * k + s
                dve.wait_ge(s_L, i + 1)
                nc.vector.tensor_copy(lg[:], L[s][:, 0:2 * NE].rearrange("p (a e) -> p a e", a=2)).then_inc(s_lg, 1)
                dve.wait_ge(s_lg, 3 * i + 1)
                dve.nop(nofuse=True)
                for c in range(2):
                    last = nc.vector.max(top[:, c, :], lg[:, c, :])
                last.then_inc(s_lg, 1)
                dve.wait_ge(s_lg, 3 * i + 2)
                dve.nop(nofuse=True)
                for c in range(2):
                    last = nc.vector.max_index(idx[:, c, :], top[:, c, :], lg[:, c, :])
                last.then_inc(s_lg, 1)
                nc.vector.tensor_tensor(gap[:, bass.ds(2 * i, 2)], top[:, :, 1], top[:, :, 0], ALU.subtract)
                dve.wait_ge(s_lg, 3 * i + 3)
                for m in range(2):
                    nc.vector.tensor_copy(best[:, m, bass.ds(2 * i, 2)], idx[:, :, m])

            def body(k, s):
                gather_sums(k, s)
                if not (first(k) and s == 0):
                    route(*before(k, s))
                normalise(k, s)

            over_pairs(dve, body)
            route(*divmod(PAIRS - 1, 2))
            nc.vector.memset(hit[:], 0.0).then_inc(s_fin, 1)
            dve.wait_ge(s_tanh, 1)
            nc.vector.tensor_scalar(w12[:, 0, :], gap[:], -0.5, 0.5, ALU.mult, ALU.add)
            nc.vector.tensor_scalar(w12[:, 1, :], gap[:], 0.5, 0.5, ALU.mult, ALU.add).then_inc(s_fin, 1)

            def spread(a):
                return a.rearrange("p (n a) -> p n a", a=1).to_broadcast([P, TILES, NE])
            every = iota8[:].rearrange("p (a e) -> p a e", a=1).to_broadcast([P, TILES, NE])
            dve.wait_ge(s_fin, 2)
            nc.vector.tensor_tensor(wfull[:], every, spread(best[:, 0, :]), ALU.is_equal).then_inc(s_fin, 1)
            nc.vector.tensor_tensor(hit[:], every, spread(best[:, 1, :]), ALU.is_equal).then_inc(s_fin, 1)
            dve.wait_ge(s_fin, 4)
            nc.vector.tensor_tensor(wfull[:], wfull[:], spread(w12[:, 0, :]), ALU.mult).then_inc(s_fin, 1)
            nc.vector.tensor_tensor(hit[:], hit[:], spread(w12[:, 1, :]), ALU.mult).then_inc(s_fin, 1)
            dve.wait_ge(s_fin, 6)
            nc.vector.tensor_tensor(wfull[:], wfull[:], hit[:], ALU.add)

        @block.tensor
        def _(pe):
            pe.wait_ge(s_w, 64)

            def turn(k, s):
                i = 2 * k + s
                pe.wait_ge(s_z, i + 1)
                if not first(k):
                    pe.wait_ge(s_xf, i - 1)
                for c in range(2):
                    for a in range(HALF):
                        mm = nc.tensor.transpose(T[s][:, a * D + c * P:a * D + (c + 1) * P],
                                                 z[:, s, c, a * P:(a + 1) * P], ident[:])
                mm.then_inc(s_T, 1)

            def logits(k, s):
                i = 2 * k + s
                pe.wait_ge(s_xf, i + 1)
                if not first(k):
                    pe.wait_ge(s_lg, 3 * i - 5)
                for c in range(2):
                    bank = L[s][:, c * NE:(c + 1) * NE]
                    for a in range(HALF):
                        nc.tensor.matmul(bank, xf[:, s, a, c * P:(c + 1) * P], wrt[:, a, :], start=(a == 0), stop=False)
                    mm = nc.tensor.matmul(bank, ones[0:1, :], br[:], start=False, stop=True)
                mm.then_inc(s_L, 1)

            def body(k, s):
                turn(k, s)
                logits(k, s)
            over_pairs(pe, body)

        @block.scalar
        def _(act):
            def body(k, s):
                i = 2 * k + s
                act.wait_ge(s_st, 3 * i + 3)
                nc.scalar.activation(std[:, s], vs[:, s], ACT.Sqrt).then_inc(s_std, 1)
                act.wait_ge(s_T, i + 1)
                if not first(k):
                    act.wait_ge(s_L, i - 1)
                    act.wait_ge(s_xfst[s], 16 * k)
                for a in range(HALF):
                    last = nc.scalar.activation(xf[:, s, a, :], T[s][:, a * D:(a + 1) * D], ACT.Identity,
                                                bias=beta[:, a:a + 1], scale=gamma[:, a:a + 1])
                last.then_inc(s_xf, 1)
            act.wait_ge(s_w, 64)
            over_pairs(act, body)
            act.wait_ge(s_fin, 1)
            nc.scalar.activation(gap[:], gap[:], ACT.Tanh, scale=0.5).then_inc(s_tanh, 1)


def expert_phase(nc, t, scratch, out, psum, ident, ones, wfull):
    with ExitStack() as ctx:
        def sb(name, shape, dt=F32):
            return ctx.enter_context(nc.sbuf_tensor(name, shape, dt))

        def sem(name):
            return ctx.enter_context(nc.semaphore(name))

        w1 = sb("w1", [P, NE, HALF, HID])
        w2 = sb("w2", [P, NE, HC, D])
        b1 = sb("b1", [P, NE, HC])
        b2 = sb("b2", [NE, D])
        xf = sb("x_xf", [P, 2, HALF, 2 * P])
        acc = sb("x_acc", [P, 2, 2, D])
        ws = sb("x_ws", [P, 2, 2, NE])
        wT = sb("x_wT", [NE, 2, P])
        hT = sb("x_hT", [P, 2, HC, 2 * P])
        H = [psum[r] for r in range(HC)]
        Y = [psum[HC], psum[HC + 1]]
        WT, YB = psum[6], psum[7]
        s_w = sem("x_weights")
        s_ld = [sem(f"x_loaded{s}") for s in range(2)]
        s_ws = sem("x_shares")
        s_wT = sem("x_shares_turned")
        s_wTs = sem("x_shares_turned_out")
        s_yb = sem("x_bias_sum")
        s_H = sem("x_hidden")
        s_g = sem("x_gelu")
        s_Y = sem("x_expert_out")
        s_acc = sem("x_sum")
        s_out = [sem(f"x_stored{s}") for s in range(2)]
        block = ctx.enter_context(nc.Block())
        STEPS = NE + 1
        END = PAIRS - 1

        @block.sync
        def _(sp):
            for e in range(NE):
                sp.dma_start(w1[:, e], t["L0_ffn_W1"][e].rearrange("(a p) n -> p a n", p=P)).then_inc(s_w, 16)
                sp.dma_start(w2[:, e], t["L0_ffn_W2"][e].rearrange("(a p) n -> p a n", p=P)).then_inc(s_w, 16)
            for e in range(NE):
                sp.dma_start(b1[:, e, :], t["L0_ffn_b1"][e].rearrange("(c p) -> p c", p=P),
                             allow_slow_non_contiguous=True).then_inc(s_w, 16)
            sp.dma_start(b2[:], t["L0_ffn_b2"]).then_inc(s_w, 16)

            def load(k, s):
                i = 2 * k + s
                if not first(k):
                    sp.wait_ge(s_H, NE * HC * (i - 1))
                    sp.nop(nofuse=True)
                    sp.wait_ge(s_out[s], 16 * k)
                    sp.nop(nofuse=True)
                sp.dma_start(xf[:, s].rearrange("p a c -> p (a c)"), scratch["xf"][bass.ds(i * P, P), :]).then_inc(s_ld[s], 16)
                sp.dma_start(acc[:, s], pair_of(scratch["x1"], i)).then_inc(s_ld[s], 16)

            def body(k, s):
                i = 2 * k + s
                final = isinstance(k, int) and i == END
                if not final:
                    load(*((k, 1) if s == 0 else (k + 1, 0)))
                sp.wait_ge(s_acc, STEPS * (i + 1))
                sp.nop(nofuse=True)
                if final:
                    sp.dma_start(out[(TILES - 2) * P:(TILES - 1) * P, :], acc[:, s, 0, :]).then_inc(s_out[s], 16)
                    sp.dma_start(out[(TILES - 1) * P:N, :], acc[0:LAST, s, 1, :]).then_inc(s_out[s], 16)
                else:
                    sp.dma_start(pair_of(out, i), acc[:, s]).then_inc(s_out[s], 16)

            load(0, 0)
            over_pairs(sp, body)
            for s in range(2):
                sp.wait_ge(s_out[s], 16 * ((PAIRS + 1 - s) // 2) + 16 * (s == END % 2))
                sp.nop(nofuse=True)

        @block.vector
        def _(dve):
            def body(k, s):
                i = 2 * k + s
                if not first(k):
                    dve.wait_ge(s_wT, i - 1)
                nc.vector.tensor_copy(ws[:, s], wfull[:, bass.ds(2 * i, 2), :]).then_inc(s_ws, 1)
                dve.wait_ge(s_ld[s], 32 * k + 32)
                dve.wait_ge(s_yb, i + 1)
                nc.vector.tensor_tensor(acc[:, s], acc[:, s], YB[:, :].rearrange("p (a d) -> p a d", a=2),
                                        ALU.add).then_inc(s_acc, 1)
                for e in range(NE):
                    dve.wait_ge(s_Y, NE * i + e + 1)
                    dve.wait_ge(s_acc, STEPS * i + e + 1)
                    for c in range(2):
                        last = nc.vector.scalar_tensor_tensor(out=acc[:, s, c, :], in0=Y[e % 2][:, c * D:(c + 1) * D],
                                                              scalar=ws[:, s, c, e:e + 1], in1=acc[:, s, c, :],
                                                              op0=ALU.mult, op1=ALU.add)
                    last.then_inc(s_acc, 1)
            over_pairs(dve, body)

        @block.tensor
        def _(pe):
            pe.wait_ge(s_w, 16 * (3 * NE + 1))

            def shares(k, s):
                i = 2 * k + s
                pe.wait_ge(s_ws, i + 1)
                if not (first(k) and s == 0):
                    pe.wait_ge(s_wTs, i)
                for c in range(2):
                    mm = nc.tensor.matmul(WT[0:NE, c * P:(c + 1) * P], ws[:, s, c, :], ident[:], start=True, stop=True)
                mm.then_inc(s_wT, 1)
                pe.wait_ge(s_wTs, i + 1)
                if not (first(k) and s == 0):
                    pe.wait_ge(s_acc, STEPS * (i - 1) + 1)
                for c in range(2):
                    mm = nc.tensor.matmul(YB[:, c * D:(c + 1) * D], wT[:, c, :], b2[:], start=True, stop=True)
                mm.then_inc(s_yb, 1)

            def hidden(k, s, e):
                i = 2 * k + s
                for c in range(HC):
                    if not (first(k) and s == 0 and e == 0):
                        pe.wait_ge(s_g, HC * (NE * i + e - 1) + c + 1)
                    for a in range(HALF):
                        mm = nc.tensor.matmul(H[c][:, 0:2 * P], w1[:, e, a, c * P:(c + 1) * P], xf[:, s, a, :],
                                              start=(a == 0), stop=(a == HALF - 1))
                    mm.then_inc(s_H, 1)

            def expert(k, s, e):
                i = 2 * k + s
                if not (first(k) and s == 0 and e < 2):
                    pe.wait_ge(s_acc, (STEPS * i + e) if e >= 2 else (STEPS * (i - 1) + NE - 2 + e + 2))
                for c in range(HC):
                    pe.wait_ge(s_g, HC * (NE * i + e) + c + 1)
                    for q in range(2):
                        mm = nc.tensor.matmul(Y[e % 2][:, q * D:(q + 1) * D], hT[:, e % 2, c, q * P:(q + 1) * P],
                                              w2[:, e, c, :], start=(c == 0 and q == 0), stop=(c == HC - 1),
                                              skip_group_check=True)
                mm.then_inc(s_Y, 1)

            def body(k, s):
                pe.wait_ge(s_ld[s], 32 * k + 32)
                hidden(k, s, 0)
                shares(k, s)
                for e in range(1, NE):
                    hidden(k, s, e)
                    expert(k, s, e - 1)
                expert(k, s, NE - 1)
            over_pairs(pe, body)

        @block.scalar
        def _(act):
            act.wait_ge(s_w, 16 * (3 * NE + 1))

            def body(k, s):
                i = 2 * k + s
                for e in range(NE):
                    for c in range(HC):
                        n = HC * (NE * i + e) + c
                        act.wait_ge(s_H, n + 1)
                        if c == 0 and not (first(k) and s == 0 and e < 2):
                            act.wait_ge(s_Y, NE * i + e - 1)
                        nc.scalar.activation(hT[:, e % 2, c, :], H[c][:, 0:2 * P], ACT.Gelu,
                                             bias=b1[:, e, c:c + 1]).then_inc(s_g, 1)
                    if e == 0:
                        act.wait_ge(s_wT, i + 1)
                        if not (first(k) and s == 0):
                            act.wait_ge(s_yb, i)
                        nc.scalar.copy(wT[:].rearrange("e c p -> e (c p)"), WT[0:NE, 0:2 * P]).then_inc(s_wTs, 1)
            over_pairs(act, body)


_INS = ['x', 'src', 'dst', 'edge_weight', 'L0_gnn_weight_l', 'L0_gnn_bias_l', 'L0_gnn_weight_r', 'L0_gnn_bias_r',
        'L0_mix_Wqkv', 'L0_mix_Wproj', 'L0_mix_bproj', 'L0_mix_ln_g', 'L0_mix_ln_b', 'L0_mix_Wg1', 'L0_mix_bg1',
        'L0_mix_Wg2', 'L0_mix_bg2', 'L0_ffn_gamma', 'L0_ffn_beta', 'L0_ffn_Wr', 'L0_ffn_br', 'L0_ffn_W1',
        'L0_ffn_b1', 'L0_ffn_W2', 'L0_ffn_b2']


def kernel(**inputs):
    import numpy as _np
    import concourse.bacc as _bacc
    from concourse import mybir as _mybir
    from concourse.bass_utils import run_bass_kernel_spmd as _run

    nc = _bacc.Bacc("TRN2", target_bir_lowering=False, num_devices=1)
    arrays, t = {}, {}
    for name in _INS:
        a = _np.ascontiguousarray(inputs[name])
        arrays[f"in_{name}_dram"] = a
        t[name] = nc.dram_tensor(f"in_{name}_dram", a.shape, _mybir.dt.from_np(a.dtype), kind="ExternalInput").ap()

    def internal(name, shape):
        return nc.dram_tensor(name, shape, _mybir.dt.float32, kind="Internal").ap()

    scratch = {"xn": internal("xn_rows", (NPAD, D)), "xnT": internal("xn_turned", (NPAD, D)),
               "h": internal("h_rows", (NPAD, D)), "x1": internal("x1_rows", (NPAD, D)),
               "xf": internal("xf_turned", (PAIRS * P, HALF * 2 * P)),
               "agg": [internal(f"agg{r}", (AGG_ROWS, D)) for r in range(NACC)]}
    out = nc.dram_tensor("out_0_dram", (N, D), _mybir.dt.float32, kind="ExternalOutput").ap()
    build(nc, t, scratch, out)
    r = _run(nc, [arrays], core_ids=[0])
    return r.results[0]["out_0_dram"]
```

```python
from contextlib import ExitStack

import numpy as np

import concourse.bass as bass
from concourse import mybir

F32 = mybir.dt.float32
BF16 = mybir.dt.bfloat16
I32 = mybir.dt.int32
U32 = mybir.dt.uint32
ALU = mybir.AluOpType
ACT = mybir.ActivationFunctionType
AX_X = mybir.AxisListType.X

P = 128
N, D = 12500, 256
E = 212500
NH, HD = 8, 32
GH = 64
NE, HID = 8, 512
EPS = 1e-5

TILES = -(-N // P)
LAST = N - (TILES - 1) * P
PAIRS = TILES // 2
NPAD = TILES * P
HALF = D // P
HC = HID // P

CHUNK_GROUP = 16
WINDOW = 8
BATCH = 4
SPAN = P // 2
EROWS = -(-E // P)
GROUPS = -(-EROWS // CHUNK_GROUP)
CHUNKS = GROUPS * CHUNK_GROUP
BTILES = -(-CHUNKS // BATCH // SPAN)
BFULL = E // (BATCH * P)
ETILES = CHUNKS // P
EFULL = E // P
NACC = 4
TRASH = NPAD
AGG_ROWS = NPAD + P
assert NPAD <= P * P
assert TILES % 2 == 0 and CHUNKS % P == 0 and CHUNK_GROUP % NACC == 0

CAP = 2 * P
BLOCKS = -(-NPAD // CAP) + NE - 1
BLOCKS += BLOCKS % 2
REGION = NPAD + CAP
ROW = D + 3
TAIL_GROUPS = GROUPS - 2 * PAIRS
assert TAIL_GROUPS >= 3


def build(nc, t, scratch, out):
    with ExitStack() as ctx:
        def sb(name, shape, dt=F32):
            return ctx.enter_context(nc.sbuf_tensor(name, shape, dt))

        def sem(name):
            return ctx.enter_context(nc.semaphore(name))

        ident = sb("ident", [P, P])
        prior = sb("prior", [P, P])
        trash = sb("trash", [P, 1])
        iota8 = sb("iota8", [P, NE])
        lower = sb("lower", [P, P])
        iotaq = sb("iotaq", [P, BLOCKS])
        nodes = sb("nodes", [P, TILES])
        base = sb("base", [P, 2 * NE])
        run = sb("run", [P, 2 * NE])
        offset = sb("offset", [1, 2, BLOCKS], I32)[:].rearrange("p m q -> p (m q)")
        expert = sb("expert", [1, 2, BLOCKS], I32)[:].rearrange("p m q -> p (m q)")
        ones = sb("ones", [P, P])
        zeros = sb("zeros", [P, 512])
        gscale = sb("gscale", [P, TILES])
        srcf = sb("srcf", [P, CHUNKS])
        packed = sb("packed", [P, BTILES, BATCH * P], BF16)
        both = sb("both", [P, SPAN], BF16)
        iotaf = sb("iotaf", [P, P])
        wtf = sb("wtf", [P, CHUNKS])
        dsti = sb("dsti", [P, CHUNKS], I32)
        locf = sb("locf", [P, CHUNKS])
        base_row = sb("window_base", [1, CHUNKS // WINDOW], I32)
        general = sb("general_group", [1, GROUPS], I32)
        psum = [ctx.enter_context(nc.psum_tensor(f"bank{i}", [P, 512], F32)) for i in range(8)]

        edges = dict(src=srcf, packed=packed, both=both, iota=iotaf, weight=wtf, dst=dsti, local=locf,
                     base=base_row, general=general)
        setup_phase(nc, ctx, t, scratch, psum, ident, prior, trash, iota8, ones, zeros,
                    lower, iotaq, nodes, base, run, edges)
        with ExitStack() as mid:
            kmax = mid.enter_context(nc.sbuf_tensor("kmax", [P, D], F32))
            wk = mid.enter_context(nc.sbuf_tensor("wk", [P, HALF, D], F32))
            norm_phase(nc, t, scratch, psum, ident, gscale, kmax, wk)
            edge_mix_phase(nc, t, scratch, psum, ident, prior, trash, ones, zeros, gscale,
                           edges, kmax, wk)
        route_phase(nc, t, scratch, psum, ident, ones, zeros, iota8, lower, run, nodes)
        plan_phase(nc, scratch, iotaq, base, run, offset, expert, trash)
        expert_phase(nc, t, scratch, out, psum, ident, offset, expert)


def setup_phase(nc, outer, t, scratch, psum, ident, prior, trash, iota8, ones, zeros,
                lower, iotaq, nodes, base, run, edges):
    with ExitStack() as ctx:
        def sem(name):
            return ctx.enter_context(nc.semaphore(name))
        raw = {k: ctx.enter_context(nc.sbuf_tensor(f"raw_{k}", [P, ETILES, P], dt))
               for k, dt in (("src", I32), ("dst", I32), ("wt", F32))}
        flt = {k: ctx.enter_context(nc.sbuf_tensor(f"flt_{k}", [P, ETILES, P], F32)) for k in ("src", "dst", "loc")}
        srcf, wtf, dsti, locf = edges["src"], edges["weight"], edges["dst"], edges["local"]

        def sb(name, shape, dt=F32):
            return ctx.enter_context(nc.sbuf_tensor(name, shape, dt))
        raw_end = sb("raw_end", [P, P], I32)
        flt_end = sb("flt_end", [P, P])
        low = sb("low", [P, P])
        high = sb("high", [P, P])
        wbase = sb("wbase", [P, P // WINDOW])
        whigh = sb("whigh", [P, P // WINDOW])
        wfit = sb("wfit", [P, P // WINDOW])
        gfit = sb("gfit", [P, P // CHUNK_GROUP])
        wbase_i = sb("wbase_i", [P, P // WINDOW], I32)
        ggen = sb("ggen", [P, P // CHUNK_GROUP], I32)
        cbase = sb("cbase", [P, P])
        cfit = sb("cfit", [P, P])
        tbase = sb("tbase", [P, P])
        tfit = sb("tfit", [P, P])
        tgen = sb("tgen", [P, P])
        wide = sb("wide", [P, BTILES, BATCH * P], I32)
        s_wide = sem("setup_wide")
        s_win = sem("setup_windows")
        s_wturn = sem("setup_windows_turned")
        s_plan = sem("setup_plan_moved")
        s_clear = sem("setup_clear")
        s_load = sem("setup_load")
        s_const = sem("setup_const")
        s_pool = sem("setup_pool")
        s_flt = sem("setup_flt")
        s_turn = sem("setup_turn")
        s_taken = sem("setup_taken")
        s_zeroed = sem("setup_zeroed")
        s_tail = sem("setup_tail")
        dram = {"src": t["src"], "dst": t["dst"], "wt": t["edge_weight"]}
        block = ctx.enter_context(nc.Block())
        full_tiles = EFULL // P
        rest_rows = EFULL - full_tiles * P
        rest = E - EFULL * P
        WSPAN, WPLAN, WLOCAL = 3, 13, 18

        @block.sync
        def _(sp):
            sp.wait_ge(s_clear, 6)
            for k, a in dram.items():
                sp.dma_start(raw[k][:, 0:full_tiles, :],
                             a[0:full_tiles * P * P].rearrange("(t c p) -> c t p", c=P, p=P)).then_inc(s_load, 16)
                sp.dma_start(raw[k][0:rest_rows, full_tiles, :],
                             a[full_tiles * P * P:EFULL * P].rearrange("(c p) -> c p", p=P)).then_inc(s_load, 16)
                sp.dma_start(raw[k][rest_rows:rest_rows + 1, full_tiles, 0:rest],
                             a[EFULL * P:E].rearrange("(a p) -> a p", a=1)).then_inc(s_load, 16)
            tiles, row = BFULL // SPAN, BATCH * P
            for half in (0, SPAN):
                sp.dma_start(wide[half:half + SPAN, 0:tiles, :],
                             t["src"][0:tiles * SPAN * row].rearrange("(t c e) -> c t e", c=SPAN, e=row)).then_inc(s_wide, 16)
                sp.dma_start(wide[half:half + BFULL % SPAN, tiles, :],
                             t["src"][tiles * SPAN * row:BFULL * row].rearrange("(c e) -> c e", e=row)).then_inc(s_wide, 16)
                at = half + BFULL % SPAN
                sp.dma_start(wide[at:at + 1, tiles, 0:E - BFULL * row],
                             t["src"][BFULL * row:E].rearrange("(a e) -> a e", a=1)).then_inc(s_wide, 16)
            sp.dma_start(raw_end[0:rest_rows, :],
                         t["dst"][full_tiles * P * P:EFULL * P].rearrange("(c p) -> c p", p=P)).then_inc(s_load, 16)
            sp.dma_start(raw_end[rest_rows:rest_rows + 1, 0:rest],
                         t["dst"][EFULL * P:E].rearrange("(a p) -> a p", a=1)).then_inc(s_load, 16)
            for acc in scratch["agg"]:
                v = acc.rearrange("(a p) d -> p a d", p=P)
                rows = AGG_ROWS // P
                for a in range(0, rows, 2):
                    n = min(2, rows - a)
                    sp.dma_start(v[:, a:a + n, :], zeros[:, 0:n * D].rearrange("p (a d) -> p a d", a=n)).then_inc(s_zeroed, 16)
            sp.wait_ge(s_win, WPLAN)
            sp.dma_start(scratch["base"].rearrange("(t w) -> t w", t=ETILES), wbase_i[0:ETILES, :]).then_inc(s_plan, 16)
            sp.dma_start(scratch["general"].rearrange("(t w) -> t w", t=ETILES), ggen[0:ETILES, :]).then_inc(s_plan, 16)
            sp.wait_ge(s_plan, 32)
            sp.dma_start(edges["base"][:], scratch["base"].rearrange("(a w) -> a w", a=1)).then_inc(s_plan, 16)
            sp.dma_start(edges["general"][:], scratch["general"].rearrange("(a w) -> a w", a=1)).then_inc(s_plan, 16)
            sp.wait_ge(s_plan, 64)
            sp.wait_ge(s_zeroed, 16 * NACC * (-(-(AGG_ROWS // P) // 2)))

        @block.vector
        def _(dve):
            nc.vector.memset(raw["src"][:, full_tiles, :], 0).then_inc(s_clear, 1)
            nc.vector.memset(raw["dst"][:, full_tiles, :], 0).then_inc(s_clear, 1)
            nc.vector.memset(raw["wt"][:, full_tiles, :], 0.0).then_inc(s_clear, 1)
            nc.vector.memset(zeros[:], 0.0).then_inc(s_clear, 1)
            nc.vector.memset(raw_end[:], NPAD).then_inc(s_clear, 1)
            nc.vector.memset(wide[:, BFULL // SPAN:BTILES, :], 0).then_inc(s_clear, 1)
            nc.vector.memset(ones[:], 1.0).then_inc(s_const, 1)
            nc.vector.memset(low[:], 0.0)
            nc.vector.memset(high[:], 0.0)
            dve.wait_ge(s_load, 16 * 11)
            nc.vector.tensor_copy(flt["src"][:], raw["src"][:]).then_inc(s_flt, 1)
            nc.vector.tensor_copy(flt["dst"][:], raw["dst"][:]).then_inc(s_flt, 1)
            nc.vector.tensor_copy(flt_end[:], raw_end[:]).then_inc(s_flt, 1)
            done = [0]

            def step(*ins):
                for i in ins:
                    i.then_inc(s_win, 1)
                done[0] += len(ins)
                dve.wait_ge(s_win, done[0])

            dve.wait_ge(s_flt, 3)
            step(nc.vector.tensor_reduce(low[:, 0:full_tiles], flt["dst"][:, 0:full_tiles, :], AX_X, ALU.min),
                 nc.vector.tensor_reduce(low[:, full_tiles:ETILES], flt_end[:].rearrange("p (a c) -> p a c", a=1), AX_X, ALU.min),
                 nc.vector.tensor_reduce(high[:, 0:ETILES], flt["dst"][:], AX_X, ALU.max))
            assert done[0] == WSPAN
            dve.wait_ge(s_wturn, 2)
            step(nc.vector.tensor_reduce(wbase[:], psum[4][:, 0:P].rearrange("p (w c) -> p w c", c=WINDOW), AX_X, ALU.min),
                 nc.vector.tensor_reduce(whigh[:], psum[5][:, 0:P].rearrange("p (w c) -> p w c", c=WINDOW), AX_X, ALU.max))
            step(nc.vector.tensor_scalar(wbase[:], wbase[:], float(NPAD - P), None, ALU.min))
            step(nc.vector.tensor_tensor(whigh[:], whigh[:], wbase[:], ALU.subtract),
                 nc.vector.tensor_copy(wbase_i[:], wbase[:]))
            step(nc.vector.tensor_scalar(wfit[:], whigh[:], float(P), None, ALU.is_lt))
            step(nc.vector.tensor_reduce(gfit[:], wfit[:].rearrange("p (g h) -> p g h", h=CHUNK_GROUP // WINDOW), AX_X, ALU.min))
            step(nc.vector.tensor_scalar(ggen[:], gfit[:], -1.0, 1.0, ALU.mult, ALU.add),
                 nc.vector.tensor_copy(cbase[:].rearrange("p (w c) -> p w c", c=WINDOW),
                                       wbase[:].rearrange("p (w a) -> p w a", a=1).to_broadcast([P, P // WINDOW, WINDOW])),
                 nc.vector.tensor_copy(cfit[:].rearrange("p (g c) -> p g c", c=CHUNK_GROUP),
                                       gfit[:].rearrange("p (g a) -> p g a", a=1).to_broadcast([P, P // CHUNK_GROUP, CHUNK_GROUP])))
            assert done[0] == WPLAN
            dve.wait_ge(s_wturn, 4)
            step(nc.vector.tensor_copy(tbase[:], psum[4][:, P:2 * P]),
                 nc.vector.tensor_copy(tfit[:], psum[5][:, P:2 * P]))
            step(nc.vector.tensor_scalar(tgen[:], tfit[:], -1.0, 1.0, ALU.mult, ALU.add))
            for i in range(ETILES):
                last = nc.vector.tensor_scalar(flt["loc"][:, i, :], flt["dst"][:, i, :], tbase[:, i:i + 1], tfit[:, i:i + 1],
                                               ALU.subtract, ALU.mult)
            step(last)
            dve.wait_ge(s_pool, 3)
            for i in range(ETILES):
                last = nc.vector.scalar_tensor_tensor(out=flt["loc"][:, i, :], in0=edges["iota"][:], scalar=tgen[:, i:i + 1],
                                                      in1=flt["loc"][:, i, :], op0=ALU.mult, op1=ALU.add)
            step(last)
            assert done[0] == WLOCAL
            n = 0
            for i in range(ETILES):
                for dst in (srcf, dsti, wtf, locf):
                    dve.wait_ge(s_turn, n + 1)
                    nc.vector.tensor_copy(dst[:, i * P:(i + 1) * P], psum[n % 4][:, 0:P]).then_inc(s_taken, 1)
                    n += 1
            dve.wait_ge(s_wide, 96)
            step(nc.vector.tensor_scalar(wide[0:SPAN], wide[0:SPAN], (P - 1) * P, None, ALU.bitwise_and),
                 nc.vector.tensor_scalar(wide[SPAN:P], wide[SPAN:P], P - 1, None, ALU.bitwise_and))
            step(nc.vector.tensor_copy(edges["packed"][:], wide[:]),
                 nc.vector.tensor_tensor(edges["both"][:], ident[:, 0:SPAN], ident[:, SPAN:P], ALU.add))

        @block.gpsimd
        def _(pool):
            nc.gpsimd.iota(edges["iota"][:], pattern=[[1, P]], base=0, channel_multiplier=0,
                           allow_small_or_imprecise_dtypes=True).then_inc(s_pool, 1)
            pool.wait_ge(s_const, 1)
            nc.gpsimd.affine_select(out=ident[:], in_=ones[:], compare_op=ALU.is_equal, fill=0.0, base=0,
                                    pattern=[[-1, P]], channel_multiplier=1).then_inc(s_const, 1)
            nc.gpsimd.iota(prior[:], pattern=[[0, P]], base=TRASH, channel_multiplier=1,
                           allow_small_or_imprecise_dtypes=True).then_inc(s_pool, 1)
            nc.gpsimd.iota(trash[:], pattern=[[0, 1]], base=TRASH, channel_multiplier=1,
                           allow_small_or_imprecise_dtypes=True)
            nc.gpsimd.affine_select(out=lower[:], in_=ones[:], compare_op=ALU.is_ge, fill=0.0, base=-1,
                                    pattern=[[1, P]], channel_multiplier=-1)
            nc.gpsimd.iota(iotaq[:], pattern=[[1, BLOCKS]], base=0, channel_multiplier=0,
                           allow_small_or_imprecise_dtypes=True)
            nc.gpsimd.iota(nodes[:], pattern=[[P, TILES]], base=0, channel_multiplier=1,
                           allow_small_or_imprecise_dtypes=True)
            for a in (base, run):
                nc.gpsimd.iota(a[:], pattern=[[0, 2], [REGION, NE]], base=0, channel_multiplier=0,
                               allow_small_or_imprecise_dtypes=True)
            nc.gpsimd.iota(iota8[:], pattern=[[1, NE]], base=0, channel_multiplier=0,
                           allow_small_or_imprecise_dtypes=True)
            pool.wait_ge(s_pool, 2)
            nc.gpsimd.affine_select(out=prior[:], in_=prior[:], compare_op=ALU.is_ge, fill=0.0, base=-1,
                                    pattern=[[-1, P]], channel_multiplier=1).then_inc(s_pool, 1)

        @block.tensor
        def _(pe):
            pe.wait_ge(s_const, 2)
            pe.wait_ge(s_flt, 2)
            pe.wait_ge(s_win, WSPAN)
            nc.tensor.transpose(psum[4][:, 0:P], low[:], ident[:]).then_inc(s_wturn, 1)
            nc.tensor.transpose(psum[5][:, 0:P], high[:], ident[:]).then_inc(s_wturn, 1)
            pe.wait_ge(s_win, WPLAN)
            nc.tensor.transpose(psum[4][:, P:2 * P], cbase[:], ident[:]).then_inc(s_wturn, 1)
            nc.tensor.transpose(psum[5][:, P:2 * P], cfit[:], ident[:]).then_inc(s_wturn, 1)
            pe.wait_ge(s_win, WLOCAL)
            n = 0
            for i in range(ETILES):
                for a in (flt["src"], flt["dst"], raw["wt"], flt["loc"]):
                    if n >= 4:
                        pe.wait_ge(s_taken, n - 3)
                    nc.tensor.transpose(psum[n % 4][:, 0:P], a[:, i, :], ident[:]).then_inc(s_turn, 1)
                    n += 1


def first(i):
    return isinstance(i, int) and i == 0


def norm_phase(nc, t, scratch, psum, ident, gscale, kmax, wk):
    with ExitStack() as ctx:
        def sb(name, shape, dt=F32):
            return ctx.enter_context(nc.sbuf_tensor(name, shape, dt))

        def sem(name):
            return ctx.enter_context(nc.semaphore(name))

        xin = sb("xin", [P, 2, D])
        xnr = sb("xnr", [P, 2, D])
        xnT = sb("xnT", [P, 2, HALF, P])
        hrow = sb("hrow", [P, 2, D])
        stat = sb("stat", [P, 2, 6])
        mv = sb("mv", [P, 2, 2])
        vare = sb("vare", [P, 2])
        std = sb("std", [P, 2])
        varall = sb("varall", [P, TILES])
        rstd = sb("rstd", [P, TILES])
        gvar = sb("gvar", [P, TILES])
        gstd = sb("gstd", [P, TILES])
        wl = sb("wl", [P, HALF, D])
        s_w = sem("n_weights")
        s_in = [sem(f"n_x_loaded{s}") for s in range(2)]
        s_step = sem("n_step")
        s_xn = sem("n_xn")
        s_T = sem("n_turned")
        s_xT = sem("n_xnT")
        s_hk = sem("n_hk")
        s_h = sem("n_h")
        s_max = sem("n_kmax")
        s_xst = [sem(f"n_xn_stored{s}") for s in range(2)]
        s_Tst = [sem(f"n_xnT_stored{s}") for s in range(2)]
        s_hst = [sem(f"n_h_stored{s}") for s in range(2)]
        s_std = sem("n_std")
        s_pad = sem("n_pad")
        s_fin = sem("n_gate_variance")
        s_gstd = sem("n_gate_std")
        T = [psum[0], psum[1]]
        H = [psum[2], psum[3]]
        K = [psum[4], psum[5]]
        block = ctx.enter_context(nc.Block())
        x = t["x"]

        @block.sync
        def _(sp):
            wkd = t["L0_mix_Wqkv"][:, D:2 * D].rearrange("(a p) n -> p a n", p=P)
            sp.dma_start(wl[:], t["L0_gnn_weight_l"].rearrange("(a p) n -> p a n", p=P)).then_inc(s_w, 16)
            sp.dma_start(wk[:], wkd).then_inc(s_w, 16)

            def load(i, s, last=False):
                if not first(i):
                    sp.wait_ge(s_xn, 2 * i + s - 1)
                if last:
                    sp.wait_ge(s_pad, 1)
                    sp.dma_start(xin[0:LAST, s, :], x[(TILES - 1) * P:N, :]).then_inc(s_in[s], 16)
                else:
                    sp.dma_start(xin[:, s, :], x[bass.ds(i * 2 * P + s * P, P), :]).then_inc(s_in[s], 16)

            load(0, 0)
            load(0, 1)
            with sp.Fori(1, PAIRS - 1) as i:
                load(i, 0)
                load(i, 1)
            load(PAIRS - 1, 0)
            load(PAIRS - 1, 1, last=True)

        @block.vector
        def _(dve):
            nc.vector.memset(kmax[:], -3.0e38).then_inc(s_max, 1)

            def normalise(i, s):
                n = 2 * i + s
                dve.wait_ge(s_in[s], 16 * i + 16)
                nc.vector.bn_stats(stat[:, s, :], xin[:, s, :]).then_inc(s_step, 1)
                dve.wait_ge(s_step, 4 * n + 1)
                dve.nop(nofuse=True)
                nc.vector.bn_aggr(mv[:, s, :], stat[:, s, :]).then_inc(s_step, 1)
                dve.wait_ge(s_step, 4 * n + 2)
                nc.vector.tensor_scalar(vare[:, s:s + 1], mv[:, s, 1:2], EPS, None, ALU.add).then_inc(s_step, 1)
                nc.vector.tensor_copy(varall[:, bass.ds(n, 1)], mv[:, s, 1:2])
                dve.wait_ge(s_std, n + 1)
                dve.nop(nofuse=True)
                nc.vector.reciprocal(rstd[:, bass.ds(n, 1)], std[:, s:s + 1]).then_inc(s_step, 1)
                dve.wait_ge(s_step, 4 * n + 4)
                if not first(i):
                    dve.wait_ge(s_T, n - 1)
                if not first(i):
                    dve.wait_ge(s_xst[s], 16 * i)
                nc.vector.tensor_scalar(xnr[:, s, :], xin[:, s, :], mv[:, s, 0:1], rstd[:, bass.ds(n, 1)],
                                        ALU.subtract, ALU.mult).then_inc(s_xn, 1)

            def maximum(i, s, rows=P):
                n = 2 * i + s
                dve.wait_ge(s_hk, n + 1)
                dve.wait_ge(s_max, n + 1)
                nc.vector.tensor_tensor(kmax[0:rows, :], kmax[0:rows, :], K[s][0:rows, 0:D],
                                        ALU.max).then_inc(s_max, 1)

            normalise(0, 0)
            normalise(0, 1)
            maximum(0, 0)
            maximum(0, 1)
            with dve.Fori(1, PAIRS - 1) as i:
                normalise(i, 0)
                normalise(i, 1)
                maximum(i, 0)
                maximum(i, 1)
            dve.wait_ge(s_xn, 2 * (PAIRS - 1))
            nc.vector.memset(xin[:, 1, :], 0.0).then_inc(s_pad, 1)
            normalise(PAIRS - 1, 0)
            normalise(PAIRS - 1, 1)
            maximum(PAIRS - 1, 0)
            maximum(PAIRS - 1, 1, rows=LAST)
            dve.wait_ge(s_xn, TILES)
            nc.vector.tensor_tensor(gvar[:], rstd[:], rstd[:], ALU.mult).then_inc(s_fin, 1)
            dve.wait_ge(s_fin, 1)
            nc.vector.tensor_tensor(gvar[:], gvar[:], varall[:], ALU.mult).then_inc(s_fin, 1)
            dve.wait_ge(s_fin, 2)
            nc.vector.tensor_scalar(gvar[:], gvar[:], EPS, None, ALU.add).then_inc(s_fin, 1)
            dve.wait_ge(s_gstd, 1)
            nc.vector.reciprocal(gscale[:], gstd[:])

        @block.gpsimd
        def _(pool):
            def store(i, s):
                n = 2 * i + s
                rows = bass.ds(i * 2 * P + s * P, P)
                for ready, src, dst, done in ((s_xn, xnr[:, s, :], scratch["xn"], s_xst),
                                              (s_xT, xnT[:, s, :, :].rearrange("p a c -> p (a c)"), scratch["xnT"], s_Tst),
                                              (s_h, hrow[:, s, :], scratch["h"], s_hst)):
                    pool.wait_ge(ready, n + 1)
                    pool.nop(nofuse=True)
                    pool.dma_start(dst[rows, :], src).then_inc(done[s], 16)
            store(0, 0)
            store(0, 1)
            with pool.Fori(1, PAIRS) as i:
                store(i, 0)
                store(i, 1)
            for done in (s_xst, s_Tst, s_hst):
                for s in range(2):
                    pool.wait_ge(done[s], 16 * PAIRS)

        @block.tensor
        def _(pe):
            pe.wait_ge(s_w, 32)

            def turn(i, s):
                n = 2 * i + s
                pe.wait_ge(s_xn, n + 1)
                if not first(i):
                    pe.wait_ge(s_xT, n - 1)
                for a in range(HALF):
                    last = nc.tensor.transpose(T[s][:, a * P:(a + 1) * P], xnr[:, s, a * P:(a + 1) * P], ident[:])
                last.then_inc(s_T, 1)

            def product(i, s):
                n = 2 * i + s
                pe.wait_ge(s_xT, n + 1)
                if not first(i):
                    pe.wait_ge(s_h, n - 1)
                if not first(i):
                    pe.wait_ge(s_max, n - 1)
                for bank, w in ((H[s], wl), (K[s], wk)):
                    for a in range(HALF):
                        last = nc.tensor.matmul(bank[:, 0:D], xnT[:, s, a, :], w[:, a, :],
                                                start=(a == 0), stop=(a == HALF - 1))
                last.then_inc(s_hk, 1)

            turn(0, 0)
            turn(0, 1)
            product(0, 0)
            product(0, 1)
            with pe.Fori(1, PAIRS) as i:
                turn(i, 0)
                turn(i, 1)
                product(i, 0)
                product(i, 1)

        @block.scalar
        def _(act):

            def unload(i, s):
                n = 2 * i + s
                act.wait_ge(s_T, n + 1)
                if not first(i):
                    act.wait_ge(s_hk, n - 1)
                if not first(i):
                    act.wait_ge(s_Tst[s], 16 * i)
                nc.scalar.copy(xnT[:, s, :, :].rearrange("p a c -> p (a c)"), T[s][:, 0:D]).then_inc(s_xT, 1)

            def emit(i, s):
                n = 2 * i + s
                act.wait_ge(s_hk, n + 1)
                if not first(i):
                    act.wait_ge(s_hst[s], 16 * i)
                nc.scalar.copy(hrow[:, s, :], H[s][:, 0:D]).then_inc(s_h, 1)

            def deviation(i, s):
                n = 2 * i + s
                act.wait_ge(s_step, 4 * n + 3)
                nc.scalar.activation(std[:, s:s + 1], vare[:, s:s + 1], ACT.Sqrt).then_inc(s_std, 1)

            deviation(0, 0)
            deviation(0, 1)
            unload(0, 0)
            unload(0, 1)
            emit(0, 0)
            emit(0, 1)
            with act.Fori(1, PAIRS) as i:
                deviation(i, 0)
                deviation(i, 1)
                unload(i, 0)
                unload(i, 1)
                emit(i, 0)
                emit(i, 1)
            act.wait_ge(s_fin, 3)
            nc.scalar.activation(gstd[:], gvar[:], ACT.Sqrt).then_inc(s_gstd, 1)


def edge_mix_phase(nc, t, scratch, psum, ident, prior, trash, ones, zeros, gscale, edges, kmax, wk):
    with ExitStack() as ctx:
        def sb(name, shape, dt=F32):
            return ctx.enter_context(nc.sbuf_tensor(name, shape, dt))

        def sem(name):
            return ctx.enter_context(nc.semaphore(name))

        srcf, wtf, dsti, locf = edges["src"], edges["weight"], edges["dst"], edges["local"]
        gidx = sb("gidx", [P, CHUNK_GROUP], I32)
        sidx = sb("sidx", [P, CHUNK_GROUP], I32)
        rows = sb("rows", [P, CHUNK_GROUP, D])
        pick = sb("pick", [P, 2, BATCH, P])
        Emat = sb("Emat", [P, 2, BATCH, P])
        seen = sb("seen", [P, BATCH, P])
        seen_sum = sb("seen_sum", [P, CHUNK_GROUP])
        Cmat = sb("Cmat", [P, 2, BATCH, P])
        msg = sb("msg", [P, 2 * BATCH, D])
        B = [psum[0], psum[7]]
        C = psum[1]
        M = [psum[2], psum[3]]
        s_gidx = sem("e_gather_rows_known")
        s_rows = [sem(f"e_rows_at_hand{h}") for h in range(2)]
        HALF_ROWS = 16 * WINDOW
        s_B = sem("e_targets_spread")
        s_E = sem("e_matrices")
        s_sidx = sem("e_add_rows_known")
        s_C = sem("e_combined")
        s_Cc = sem("e_combined_out")
        s_sum = sem("e_sums")
        s_msg = sem("e_message")
        s_add = [sem(f"e_added{r}") for r in range(NACC)]
        NB = CHUNK_GROUP // BATCH
        assert NB == 4 and BATCH == NACC and CHUNK_GROUP == 2 * WINDOW

        wq = sb("wq", [P, HALF, D])
        wqT = sb("wqT", [P, HALF, D])
        wv = sb("wv", [P, HALF, D])
        wproj = sb("wproj", [P, HALF, D])
        wr = sb("wr", [P, HALF, D])
        wg1 = sb("wg1", [P, HALF, GH])
        wg1s = sb("wg1s", [P, HALF, GH])
        wg2 = sb("wg2", [GH, D])
        lng = sb("lng", [P, HALF])
        lnb = sb("lnb", [P, HALF])
        lnb_all = sb("lnb_all", [P, HALF, P])
        bg1 = sb("bg1", [1, GH])
        bg2 = sb("bg2", [P, HALF])
        bg2h = sb("bg2h", [P, HALF])
        brows = sb("brows", [1, 3, D])
        bsum = sb("bsum", [1, D])
        hbias = sb("hbias", [P, GH])
        kcol = sb("kcol", [P, HALF])
        nmax = sb("nmax", [1, D])
        xr = sb("xr", [P, 2, 2, D])
        xT = sb("xT", [P, 2, 2, HALF, P])
        ek = sb("ek", [P, 2, D])
        GTs = sb("GTs", [P, HALF, D])
        rden = sb("rden", [P, HALF])
        cm = sb("cm", [P, HALF, D])
        M1 = sb("M1", [P, HALF, D])
        hp = sb("hp", [P, 2, GH])
        hg = sb("hg", [P, 2, GH])
        hgT = sb("hgT", [GH, 2, P])
        tg = sb("tg", [P, HALF, 2 * P])
        oT = sb("oT", [P, HALF, 2 * P])
        x1 = sb("x1", [P, 2, D])
        s_w = sem("m_weights")
        s_prep = sem("m_prep")
        s_pprep = sem("m_prep_tensor")
        s_x2 = [sem(f"m_tile_loaded{s}") for s in range(2)]
        s_k = sem("m_k")
        s_ek = sem("m_exp_k")
        s_gt = sem("m_gt")
        s_ctx = sem("m_context")
        s_cv = sem("m_context_vector")
        s_x3 = [sem(f"m_pair_loaded{u}") for u in range(2)]
        s_hg = sem("m_gate_hidden")
        s_hp = sem("m_gate_hidden_scaled")
        s_ge = sem("m_gelu")
        s_ht = sem("m_gelu_turned")
        s_hgt = sem("m_gelu_turned_out")
        s_gp = sem("m_gate")
        s_th = sem("m_tanh")
        s_op = sem("m_attention_out")
        s_o = sem("m_gated")
        s_p = sem("m_projected")
        s_x1 = sem("m_x1")
        s_x1st = sem("m_x1_stored")
        block = ctx.enter_context(nc.Block())
        LASTP = PAIRS - 1

        def over_mix_pairs(engine, body):
            body(0, 0)
            body(0, 1)
            with engine.Fori(1, PAIRS // 2) as k:
                body(k, 0)
                body(k, 1)
            body(PAIRS // 2, 0)

        assert PAIRS % 2 == 1

        def take_steps(steps, *places):
            for at, what in steps:
                if at in places:
                    what()

        def halves(a):
            return a.rearrange("(a p) n -> p a n", p=P)

        def column(a):
            return a.rearrange("(a p) -> p a", p=P)

        def row(a):
            return a.rearrange("(a n) -> a n", a=1)

        def pair_rows(a, i):
            return a[bass.ds(i * 2 * P, 2 * P), :].rearrange("(a p) d -> p a d", p=P)

        weights = [(wq[:], halves(t["L0_mix_Wqkv"][:, 0:D])), (wv[:], halves(t["L0_mix_Wqkv"][:, 2 * D:3 * D])),
                   (wproj[:], halves(t["L0_mix_Wproj"])), (wr[:], halves(t["L0_gnn_weight_r"])),
                   (wg1[:], halves(t["L0_mix_Wg1"])), (wg2[:], t["L0_mix_Wg2"]),
                   (lng[:], column(t["L0_mix_ln_g"])), (lnb[:], column(t["L0_mix_ln_b"])),
                   (bg1[:], row(t["L0_mix_bg1"])), (bg2[:], column(t["L0_mix_bg2"])),
                   (brows[:, 0, :], row(t["L0_gnn_bias_l"])), (brows[:, 1, :], row(t["L0_gnn_bias_r"])),
                   (brows[:, 2, :], row(t["L0_mix_bproj"]))]
        WEIGHTS = 16 * len(weights)

        @block.sync
        def _(sp):
            for dst, src in weights:
                sp.dma_start(dst, src, allow_slow_non_contiguous=True).then_inc(s_w, 16)

            def load_window(g, h):
                if not first(g):
                    sp.wait_ge(s_sum, 2 * NB * (g - 1) + NB * (h + 1))
                    sp.nop(nofuse=True)
                gen = sp.value_load(edges["general"][0:1, bass.ds(g, 1)], min_val=0, max_val=1)
                with sp.If(gen == 0):
                    at = sp.value_load(edges["base"][0:1, bass.ds(2 * g + h, 1)], min_val=0, max_val=NPAD - P)
                    sp.dma_start(rows[:, WINDOW * h, :], scratch["h"][bass.ds(at, P), :]).then_inc(s_rows[h], 16)
                    sp.nop(nofuse=True).then_inc(s_rows[h], HALF_ROWS - 16)

            def load_tile(i, s):
                n = 2 * i + s
                if not first(i):
                    sp.wait_ge(s_gt, n - 1)
                at = bass.ds(i * 2 * P + s * P, P)
                sp.dma_start(xr[:, 0, s, :], scratch["xn"][at, :]).then_inc(s_x2[s], 16)
                sp.dma_start(xT[:, 0, s, :, :].rearrange("p a c -> p (a c)"), scratch["xnT"][at, :]).then_inc(s_x2[s], 16)

            def load_pair(k, u, last=False):
                i = 2 * k + u
                sp.dma_start(xT[:, u].rearrange("p s a c -> p s (a c)"), pair_rows(scratch["xnT"], i)).then_inc(s_x3[u], 16)
                if last:
                    sp.dma_start(xr[:, u, 0, :], t["x"][(TILES - 2) * P:(TILES - 1) * P, :]).then_inc(s_x3[u], 16)
                    sp.dma_start(xr[0:LAST, u, 1, :], t["x"][(TILES - 1) * P:N, :]).then_inc(s_x3[u], 16)
                else:
                    sp.dma_start(xr[:, u], pair_rows(t["x"], i)).then_inc(s_x3[u], 16)

            def store_pair(k, u):
                i = 2 * k + u
                sp.wait_ge(s_x1, i + 1)
                sp.nop(nofuse=True)
                sp.dma_start(pair_rows(scratch["x1"], i), x1[:]).then_inc(s_x1st, 16)

            load_window(0, 0)
            load_window(0, 1)
            load_tile(0, 0)
            load_tile(0, 1)
            with sp.Fori(1, PAIRS) as i:
                load_tile(i, 0)
                load_window(i, 0)
                load_tile(i, 1)
                load_window(i, 1)
            sp.wait_ge(s_gt, TILES)
            load_pair(0, 0)
            load_pair(0, 1)
            load_window(PAIRS, 0)
            load_window(PAIRS, 1)
            load_window(PAIRS + 1, 0)

            def mix_turn(k, u, more=True, last=False):
                load_window(PAIRS + 2 * k + u, 1)
                store_pair(*before(k, u))
                if more:
                    load_pair(*((k, 1) if u == 0 else (k + 1, 0)), last=last)
                load_window(PAIRS + 1 + 2 * k + u, 0)

            mix_turn(0, 1)
            with sp.Fori(1, PAIRS // 2 - 1) as k:
                mix_turn(k, 0)
                mix_turn(k, 1)
            mix_turn(PAIRS // 2 - 1, 0)
            mix_turn(PAIRS // 2 - 1, 1, last=True)
            mix_turn(PAIRS // 2, 0, more=False)
            store_pair(PAIRS // 2, 0)
            load_window(2 * PAIRS, 1)
            with sp.Fori(2 * PAIRS + 1, GROUPS) as g:
                load_window(g, 0)
                load_window(g, 1)
            sp.wait_ge(s_x1st, 16 * PAIRS)

        @block.gpsimd
        def _(pool):
            def gather(g, h):
                gen = pool.value_load(edges["general"][0:1, bass.ds(g, 1)], min_val=0, max_val=1)
                with pool.If(gen == 1):
                    pool.wait_ge(s_gidx, 2 * g + h + 1)
                    pool.nop(nofuse=True)
                    for j in range(WINDOW * h, WINDOW * (h + 1)):
                        pool.indirect_dma_start(rows[:, j, :], None, scratch["h"][:, :],
                                                bass.IndirectOffsetOnAxis(ap=gidx[:, j:j + 1], axis=0)).then_inc(s_rows[h], 16)

            def group(g, last=False):
                for j in range(CHUNK_GROUP):
                    b, r = j // BATCH, j % BATCH
                    if r == 0:
                        pool.wait_ge(s_sidx, NB * g + b + 1)
                    if r % 2 == 0:
                        pool.wait_ge(s_msg, 2 * (NB * g + b) + r // 2 + 1)
                    if not (first(g) and b == 0):
                        pool.wait_ge(s_add[r], 16 * (NB * g + b))
                    pool.nop(nofuse=True)
                    pool.indirect_dma_start(scratch["agg"][r][:, :],
                                            bass.IndirectOffsetOnAxis(ap=sidx[:, j:j + 1], axis=0),
                                            msg[:, j % (2 * BATCH), :], None, compute_op=ALU.add).then_inc(s_add[r], 16)
                    if not last and (j + 1) % WINDOW == 0:
                        gather(g + 1, j // WINDOW)

            gather(0, 0)
            gather(0, 1)
            group(0)
            with pool.Fori(1, GROUPS - 1) as g:
                group(g)
            group(GROUPS - 1, last=True)
            for r in range(NACC):
                pool.wait_ge(s_add[r], 16 * CHUNKS // NACC)

        @block.vector
        def _(dve):
            nc.vector.tensor_copy(gidx[:], dsti[:, 0:CHUNK_GROUP]).then_inc(s_gidx, 2)
            nc.vector.memset(cm[:], 0.0).then_inc(s_prep, 1)
            dve.wait_ge(s_pprep, 1)
            nc.vector.tensor_reduce(kcol[:], psum[4][:, 0:D].rearrange("p (a c) -> p a c", a=HALF), AX_X,
                                    ALU.max).then_inc(s_prep, 1)
            dve.wait_ge(s_w, WEIGHTS)
            for a in range(HALF):
                nc.vector.tensor_scalar(wg1s[:, a, :], wg1[:, a, :], lng[:, a:a + 1], None, ALU.mult)
                nc.vector.tensor_scalar(lnb_all[:, a, :], ones[:], lnb[:, a:a + 1], None, ALU.mult)
            nc.vector.tensor_scalar(bg2h[:], bg2[:], 0.5, None, ALU.mult)
            nc.vector.tensor_tensor(bsum[:], brows[:, 0, :], brows[:, 1, :], ALU.add).then_inc(s_prep, 1)
            dve.wait_ge(s_prep, 3)
            nc.vector.tensor_tensor(bsum[:], bsum[:], brows[:, 2, :], ALU.add).then_inc(s_prep, 1)
            dve.wait_ge(s_pprep, 2)
            nc.vector.tensor_scalar(nmax[:], psum[5][0:1, 0:D], -1.0, None, ALU.mult).then_inc(s_prep, 1)
            dve.wait_ge(s_pprep, 3)
            nc.vector.tensor_copy(hbias[:], psum[6][:, 0:GH]).then_inc(s_prep, 1)
            nc.vector.tensor_copy(wqT[:].rearrange("p a n -> p (a n)"), psum[7][:, :]).then_inc(s_prep, 1)

            def picks(g, b):
                nb = NB * g + b
                if not (first(g) and b < 2):
                    dve.wait_ge(s_C, nb - 1)
                for q in range(BATCH):
                    nc.vector.tensor_scalar(pick[:, b % 2, q, :], edges["iota"][:], locf[:, bass.ds(BATCH * nb + q, 1)],
                                            None, ALU.is_equal)

            def matrices(g, b):
                nb = NB * g + b
                dve.wait_ge(s_B, nb + 1)
                for q in range(BATCH):
                    n = bass.ds(BATCH * nb + q, 1)
                    nc.vector.tensor_scalar(Emat[:, b % 2, q, :], B[b % 2][:, q * P:(q + 1) * P], srcf[:, n], wtf[:, n],
                                            ALU.is_equal, ALU.mult)
                for q in range(BATCH):
                    last = nc.vector.scalar_tensor_tensor(out=seen[:, q, :], in0=B[b % 2][:, q * P:(q + 1) * P],
                                                          scalar=srcf[:, bass.ds(BATCH * nb + q, 1)],
                                                          in1=prior[:], op0=ALU.is_equal, op1=ALU.mult,
                                                          accum_out=seen_sum[:, BATCH * b + q:BATCH * b + q + 1])
                last.then_inc(s_E, 1)

            def add_rows(g, b, last):
                nb = NB * g + b
                dve.wait_ge(s_E, nb + 1)
                if not first(g):
                    for r in range(NACC):
                        dve.wait_ge(s_add[r], 16 * (nb - 3))
                cols = slice(BATCH * b, BATCH * (b + 1))
                nc.vector.scalar_tensor_tensor(out=sidx[:, cols], in0=seen_sum[:, cols], scalar=trash[:, 0:1],
                                               in1=srcf[:, bass.ds(BATCH * nb, BATCH)],
                                               op0=ALU.min, op1=ALU.max).then_inc(s_sidx, 1)
                if b % 2 == 1 and not last:
                    h = b // 2
                    dve.wait_ge(s_rows[h], HALF_ROWS * (g + 1))
                    nc.vector.tensor_copy(gidx[:, WINDOW * h:WINDOW * (h + 1)],
                                          dsti[:, bass.ds(CHUNK_GROUP * (g + 1) + WINDOW * h, WINDOW)]).then_inc(s_gidx, 1)

            def gate_scale(k, u):
                i = 2 * k + u
                dve.wait_ge(s_hg, i + 1)
                if not (first(k) and u == 0):
                    dve.wait_ge(s_ge, i)
                for s in range(2):
                    last = nc.vector.scalar_tensor_tensor(out=hp[:, s, :], in0=psum[4][:, s * GH:(s + 1) * GH],
                                                          scalar=gscale[:, bass.ds(2 * i + s, 1)], in1=hbias[:],
                                                          op0=ALU.mult, op1=ALU.add)
                last.then_inc(s_hp, 1)

            def gate_apply(k, u):
                i = 2 * k + u
                dve.wait_ge(s_th, i + 1)
                dve.wait_ge(s_op, i + 1)
                if not (first(k) and u == 0):
                    dve.wait_ge(s_p, i)
                nc.vector.scalar_tensor_tensor(out=oT[:].rearrange("p a c -> p (a c)"),
                                               in0=tg[:].rearrange("p a c -> p (a c)"), scalar=1.0,
                                               in1=psum[6][:, :], op0=ALU.add, op1=ALU.mult).then_inc(s_o, 1)

            def residual(k, u, last=False):
                i = 2 * k + u
                dve.wait_ge(s_p, i + 1)
                dve.wait_ge(s_x3[u], 32 * (k + 1) + 16 * last)
                if not (first(k) and u == 0):
                    dve.wait_ge(s_x1st, 16 * i)
                nc.vector.tensor_tensor(x1[:].rearrange("p a d -> p (a d)"), xr[:, u].rearrange("p a d -> p (a d)"),
                                        psum[5][:, :], ALU.add).then_inc(s_x1, 1)

            def group(g, steps, last=False):
                for b in range(NB):
                    picks(g, b)
                    take_steps(steps, 4 * b)
                    matrices(g, b)
                    add_rows(g, b, last)
                    take_steps(steps, 4 * b + 1, 4 * b + 2, 4 * b + 3)

            def mix_steps(k, u, last=False):
                steps = [(11, lambda: gate_scale(k, u))]
                if not (first(k) and u == 0):
                    steps += end_steps(*before(k, u))
                return steps

            def end_steps(k, u, last=False):
                return [(3, lambda: gate_apply(k, u)), (10, lambda: residual(k, u, last))]

            group(0, [])
            with dve.Fori(1, PAIRS) as g:
                group(g, [])
            dve.wait_ge(s_gt, TILES)
            nc.vector.tensor_copy(GTs[:].rearrange("p a n -> p (a n)"), psum[5][:, :]).then_inc(s_cv, 1)
            nc.vector.reciprocal(rden[:], psum[6][:, 0:HALF]).then_inc(s_cv, 1)
            dve.wait_ge(s_cv, 2)
            dve.wait_ge(s_ctx, 1)
            for a in range(HALF):
                for q in range(P // HD):
                    v = a * P + q * HD
                    blk = slice(q * HD, (q + 1) * HD)
                    last = nc.vector.tensor_scalar(cm[blk, a, v:v + HD], psum[4][blk, a * D + v:a * D + v + HD],
                                                   rden[blk, a:a + 1], 0.5, ALU.mult, ALU.mult)
            last.then_inc(s_cv, 1)
            dve.wait_ge(s_ctx, 2)
            nc.vector.tensor_copy(M1[:].rearrange("p a n -> p (a n)"), psum[6][:, :]).then_inc(s_cv, 1)
            over_mix_pairs(dve, lambda k, u: group(PAIRS + 2 * k + u, mix_steps(k, u)))
            group(2 * PAIRS, end_steps(PAIRS // 2, 0, last=True))
            with dve.Fori(2 * PAIRS + 1, GROUPS - 1) as g:
                group(g, [])
            group(GROUPS - 1, [], last=True)

        @block.tensor
        def _(pe):
            for a in range(HALF):
                last = nc.tensor.transpose(psum[4][:, a * P:(a + 1) * P], kmax[:, a * P:(a + 1) * P], ident[:])
            last.then_inc(s_pprep, 1)
            pe.wait_ge(s_prep, 2)
            for a in range(HALF):
                last = nc.tensor.matmul(psum[5][0:1, a * P:(a + 1) * P], kcol[:, a:a + 1], ident[:], start=True, stop=True)
            last.then_inc(s_pprep, 1)
            pe.wait_ge(s_w, WEIGHTS)
            pe.wait_ge(s_prep, 4)
            for a in range(HALF):
                nc.tensor.matmul(psum[6][:, 0:GH], lnb_all[:, a, :], wg1[:, a, :], start=(a == 0), stop=False)
            nc.tensor.matmul(psum[6][:, 0:GH], ones[0:1, :], bg1[:], start=False, stop=True)
            for a in range(HALF):
                for b in range(HALF):
                    last = nc.tensor.transpose(psum[7][:, a * D + b * P:a * D + (b + 1) * P],
                                               wq[:, b, a * P:(a + 1) * P], ident[:])
            last.then_inc(s_pprep, 1)
            pe.wait_ge(s_prep, 7)

            def spread(g, b):
                nb = NB * g + b
                if not (first(g) and b < 2):
                    pe.wait_ge(s_E, nb - 1)
                per = SPAN // NB
                nc.tensor.matmul(B[b % 2][:, :], edges["both"][:, bass.ds(NB * (g % per) + b, 1)].to_broadcast([P, P]),
                                 edges["packed"][:, bass.ds(g // per, 1), :], start=True, stop=True).then_inc(s_B, 1)

            def combine(g, b):
                nb = NB * g + b
                pe.wait_ge(s_E, nb + 1)
                if not (first(g) and b == 0):
                    pe.wait_ge(s_Cc, nb)
                for q in range(BATCH):
                    mm = nc.tensor.matmul(C[:, q * P:(q + 1) * P], pick[:, b % 2, q, :], Emat[:, b % 2, q, :],
                                          start=True, stop=True)
                mm.then_inc(s_C, 1)

            def message(g, b, p, gen):
                nb = NB * g + b
                h = b // 2
                if p == 0:
                    pe.wait_ge(s_rows[h], HALF_ROWS * (g + 1))
                    pe.wait_ge(s_Cc, nb + 1)
                if not (first(g) and b == 0):
                    pe.wait_ge(s_msg, 2 * nb - 1 + p)
                for q in (2 * p, 2 * p + 1):
                    slot = WINDOW * h + gen * (BATCH * b + q - WINDOW * h)
                    mm = nc.tensor.matmul(M[p][:, (q % 2) * D:(q % 2 + 1) * D], Cmat[:, b % 2, q, :],
                                          rows[:, bass.ds(slot, 1), :], start=True, stop=True)
                mm.then_inc(s_sum, 1)

            def keys(i, s):
                n = 2 * i + s
                pe.wait_ge(s_x2[s], 32 * (i + 1))
                if not (first(i) and s == 0):
                    pe.wait_ge(s_ek, n)
                for a in range(HALF):
                    nc.tensor.matmul(psum[4][:, 0:D], xT[:, 0, s, a, :], wk[:, a, :], start=(a == 0), stop=False)
                nc.tensor.matmul(psum[4][:, 0:D], ones[0:1, :], nmax[:], start=False, stop=True).then_inc(s_k, 1)

            def context(i, s, rws=P):
                n = 2 * i + s
                start, stop = first(i) and s == 0, rws < P
                pe.wait_ge(s_ek, n + 1)
                for a in range(HALF):
                    nc.tensor.matmul(psum[5][:, a * D:(a + 1) * D], xr[0:rws, 0, s, a * P:(a + 1) * P], ek[0:rws, s, :],
                                     start=start and a == 0, stop=stop, skip_group_check=True)
                for a in range(HALF):
                    last = nc.tensor.matmul(psum[6][:, a:a + 1], ek[0:rws, s, a * P:(a + 1) * P], ones[0:rws, 0:1],
                                            start=start and a == 0, stop=stop, skip_group_check=True)
                last.then_inc(s_gt, 1)

            def gate_hidden(k, u, last=False):
                i = 2 * k + u
                pe.wait_ge(s_x3[u], 32 * (k + 1) + 16 * last)
                if not (first(k) and u == 0):
                    pe.wait_ge(s_hgt, i)
                for s in range(2):
                    for a in range(HALF):
                        mm = nc.tensor.matmul(psum[4][:, s * GH:(s + 1) * GH], xT[:, u, s, a, :], wg1s[:, a, :],
                                              start=(a == 0), stop=(a == HALF - 1))
                mm.then_inc(s_hg, 1)

            def gate_turn(k, u):
                pe.wait_ge(s_ge, 2 * k + u + 1)
                pe.nop(nofuse=True)
                for s in range(2):
                    mm = nc.tensor.transpose(psum[4][0:GH, (s + 1) * P:(s + 2) * P], hg[:, s, :], ident[:])
                mm.then_inc(s_ht, 1)

            def gate_out(k, u):
                i = 2 * k + u
                pe.wait_ge(s_hgt, i + 1)
                if not (first(k) and u == 0):
                    pe.wait_ge(s_x1, i)
                for a in range(HALF):
                    mm = nc.tensor.matmul(psum[5][:, a * D:(a + 1) * D], wg2[:, a * P:(a + 1) * P],
                                          hgT[:].rearrange("p s c -> p (s c)"), start=True, stop=True)
                mm.then_inc(s_gp, 1)

            def attend(k, u):
                i = 2 * k + u
                if not (first(k) and u == 0):
                    pe.wait_ge(s_o, i)
                for a in range(HALF):
                    for b in range(HALF):
                        mm = nc.tensor.matmul(psum[6][:, a * D:(a + 1) * D], M1[:, b, a * P:(a + 1) * P], xT[:, u, :, b, :],
                                              start=(b == 0), stop=(b == HALF - 1))
                mm.then_inc(s_op, 1)

            def project(k, u, s):
                i = 2 * k + u
                if s == 0:
                    pe.wait_ge(s_o, i + 1)
                bank = psum[5][:, s * D:(s + 1) * D]
                for a in range(HALF):
                    nc.tensor.matmul(bank, oT[:, a, s * P:(s + 1) * P], wproj[:, a, :], start=(a == 0), stop=False)
                for a in range(HALF):
                    nc.tensor.matmul(bank, xT[:, u, s, a, :], wr[:, a, :], start=False, stop=False)
                mm = nc.tensor.matmul(bank, ones[0:1, :], bsum[:], start=False, stop=True)
                if s == 1:
                    mm.then_inc(s_p, 1)

            def gathered(g):
                return pe.value_load(edges["general"][0:1, bass.ds(g, 1)], min_val=0, max_val=1)

            def group(g, steps, last=False):
                gen = gathered(g)
                for b in range(NB):
                    if b + 2 < NB:
                        spread(g, b + 2)
                    elif not last:
                        spread(g + 1, b + 2 - NB)
                    combine(g, b)
                    take_steps(steps, 4 * b)
                    back = (g, b - 1, gen) if b else None if first(g) else (g - 1, NB - 1, gathered(g - 1))
                    for p in range(2):
                        if back:
                            message(back[0], back[1], p, back[2])
                        take_steps(steps, *((4 * b + 1, 4 * b + 2) if p == 0 else (4 * b + 3,)))

            def context_steps(i, last=False):
                return [(0, lambda: keys(i, 0)), (4, lambda: context(i, 0)), (5, lambda: keys(i, 1)),
                        (9, lambda: context(i, 1, LAST if last else P))]

            def mix_steps(k, u):
                steps = [(3, lambda: gate_hidden(k, u, last=isinstance(k, int) and k > 0)), (9, lambda: attend(k, u)),
                         (11, lambda: gate_turn(k, u)), (12, lambda: gate_out(k, u))]
                if not (first(k) and u == 0):
                    steps += projections(*before(k, u))
                return steps

            def projections(k, u):
                return [(4, lambda: project(k, u, 0)), (7, lambda: project(k, u, 1))]

            spread(0, 0)
            spread(0, 1)
            group(0, context_steps(0))
            with pe.Fori(1, LASTP) as g:
                group(g, context_steps(g))
            group(LASTP, context_steps(LASTP, last=True))
            pe.wait_ge(s_cv, 2)
            for a in range(HALF):
                for b in range(HALF):
                    mm = nc.tensor.matmul(psum[4][:, a * D:(a + 1) * D], GTs[:, b, a * P:(a + 1) * P], wv[:, b, :],
                                          start=(b == 0), stop=(b == HALF - 1))
            mm.then_inc(s_ctx, 1)
            pe.wait_ge(s_cv, 3)
            for a in range(HALF):
                for b in range(HALF):
                    mm = nc.tensor.matmul(psum[6][:, a * D:(a + 1) * D], wqT[:, b, a * P:(a + 1) * P], cm[:, b, :],
                                          start=(b == 0), stop=(b == HALF - 1))
            mm.then_inc(s_ctx, 1)
            pe.wait_ge(s_cv, 4)
            over_mix_pairs(pe, lambda k, u: group(PAIRS + 2 * k + u, mix_steps(k, u)))
            group(2 * PAIRS, projections(PAIRS // 2, 0))
            with pe.Fori(2 * PAIRS + 1, GROUPS - 1) as g:
                group(g, [])
            group(GROUPS - 1, [], last=True)
            for p in range(2):
                message(GROUPS - 1, NB - 1, p, gathered(GROUPS - 1))

        @block.scalar
        def _(act):
            def combined(g, b):
                nb = NB * g + b
                act.wait_ge(s_C, nb + 1)
                if not (first(g) and b < 2):
                    act.wait_ge(s_sum, 2 * nb - 2)
                nc.scalar.copy(Cmat[:, b % 2].rearrange("p q c -> p (q c)"), C[:, :]).then_inc(s_Cc, 1)

            def take(g, b, p):
                nb = NB * g + b
                act.wait_ge(s_sum, 2 * nb + p + 1)
                if not (first(g) and b < 2):
                    for r in (2 * p, 2 * p + 1):
                        act.wait_ge(s_add[r], 16 * (nb - 1))
                at = BATCH * (b % 2) + 2 * p
                nc.scalar.copy(msg[:, at:at + 2, :].rearrange("p q c -> p (q c)"), M[p][:, :]).then_inc(s_msg, 1)

            def exponential(i, s):
                n = 2 * i + s
                act.wait_ge(s_k, n + 1)
                if not first(i):
                    act.wait_ge(s_gt, n - 1)
                nc.scalar.activation(ek[:, s, :], psum[4][:, 0:D], ACT.Exp).then_inc(s_ek, 1)

            def gelu(k, u):
                i = 2 * k + u
                act.wait_ge(s_hp, i + 1)
                if not (first(k) and u == 0):
                    act.wait_ge(s_ht, i)
                nc.scalar.activation(hg[:], hp[:], ACT.Gelu).then_inc(s_ge, 1)

            def gelu_out(k, u):
                i = 2 * k + u
                act.wait_ge(s_ht, i + 1)
                if not (first(k) and u == 0):
                    act.wait_ge(s_gp, i)
                nc.scalar.copy(hgT[:].rearrange("p s c -> p (s c)"), psum[4][0:GH, P:3 * P]).then_inc(s_hgt, 1)

            def tanh(k, u):
                i = 2 * k + u
                act.wait_ge(s_gp, i + 1)
                if not (first(k) and u == 0):
                    act.wait_ge(s_o, i)
                for a in range(HALF):
                    last = nc.scalar.activation(tg[:, a, :], psum[5][:, a * D:(a + 1) * D], ACT.Tanh,
                                                bias=bg2h[:, a:a + 1], scale=0.5)
                last.then_inc(s_th, 1)

            def group(g, steps):
                for b in range(NB):
                    combined(g, b)
                    take_steps(steps, 4 * b)
                    back = (g, b - 1) if b else None if first(g) else (g - 1, NB - 1)
                    for p in range(2):
                        if back:
                            take(back[0], back[1], p)
                        take_steps(steps, *((4 * b + 1, 4 * b + 2) if p == 0 else (4 * b + 3,)))

            def mix_steps(k, u):
                return [(8, lambda: gelu(k, u)), (11, lambda: gelu_out(k, u)), (14, lambda: tanh(k, u))]

            def exp_steps(i):
                return [(2, lambda: exponential(i, 0)), (7, lambda: exponential(i, 1))]

            group(0, exp_steps(0))
            with act.Fori(1, PAIRS) as g:
                group(g, exp_steps(g))
            over_mix_pairs(act, lambda k, u: group(PAIRS + 2 * k + u, mix_steps(k, u)))
            with act.Fori(2 * PAIRS, GROUPS) as g:
                group(g, [])
            for p in range(2):
                take(GROUPS - 1, NB - 1, p)


def over_pairs(engine, body):
    body(0, 0)
    body(0, 1)
    body(1, 0)
    body(1, 1)
    with engine.Fori(2, PAIRS // 2) as k:
        body(k, 0)
        body(k, 1)
    if PAIRS % 2:
        body(PAIRS // 2, 0)


def before(k, s):
    return (k, 0) if s == 1 else (k - 1, 1)


def pair_of(a, i, width=2 * P):
    return a[bass.ds(i * width, width), :].rearrange("(a p) d -> p a d", p=P)


def route_phase(nc, t, scratch, psum, ident, ones, zeros, iota8, lower, run, nodes):
    with ExitStack() as ctx:
        def sb(name, shape, dt=F32):
            return ctx.enter_context(nc.sbuf_tensor(name, shape, dt))

        def sem(name):
            return ctx.enter_context(nc.semaphore(name))

        xin = sb("r_xin", [P, 2, 2, D])
        agg = [sb(f"r_agg{r}", [P, 2, 2, D]) for r in range(NACC)]
        half = sb("r_half", [P, 2, 2, D])
        x1 = sb("r_x1", [P, 2, 2, D])
        z = sb("r_z", [P, 2, 2, ROW])
        xf = sb("r_xf", [P, 2, HALF, 2 * P])
        pos = sb("r_pos", [P, 2, 2, 2], I32)
        posf = sb("r_posf", [P, 4])
        idxf = sb("r_idxf", [P, 2, 2])
        hot = sb("r_hot", [P, 2, 2, NE])
        place = sb("r_place", [P, 2, 2, NE])
        b1c = sb("r_b1c", [P, NE, HC])
        stat = sb("r_stat", [P, 2, 6])
        mv = sb("r_mv", [P, 2, 2, 2])
        vs = sb("r_vs", [P, 2, 2])
        std = sb("r_std", [P, 2, 2])
        scl = sb("r_scl", [P, 2, 2])
        lg = sb("r_lg", [P, 2, NE])
        top = sb("r_top", [P, 2, NE])
        idx = sb("r_idx", [P, 2, NE], U32)
        gamma = sb("r_gamma", [P, HALF])
        beta = sb("r_beta", [P, HALF])
        wrt = sb("r_wrt", [P, HALF, NE])
        br = sb("r_br", [1, NE])
        s_w = sem("r_weights")
        s_ld = [sem(f"r_loaded{s}") for s in range(2)]
        s_ld2 = [sem(f"r_loaded_rest{s}") for s in range(2)]
        s_half = sem("r_half_sum")
        s_sum = sem("r_sum")
        s_st = sem("r_stat_step")
        s_std = sem("r_std")
        s_scl = sem("r_scale")
        s_z = sem("r_z")
        s_T = sem("r_turned")
        s_xf = sem("r_xf")
        s_L = sem("r_logits")
        s_lg = sem("r_route_step")
        s_hot = sem("r_one_hots")
        s_rank = sem("r_ranks")
        s_pos = sem("r_positions")
        s_sent = [sem(f"r_sent{m}") for m in range(2)]
        s_aux = sem("r_aux")
        s_x1st = [sem(f"r_x1_stored{s}") for s in range(2)]
        T = [psum[0], psum[1]]
        L = [psum[2], psum[3]]
        R = [psum[4], psum[5]]
        block = ctx.enter_context(nc.Block())

        @block.sync
        def _(sp):
            for dst, src in ((gamma[:], t["L0_ffn_gamma"].rearrange("(a p) -> p a", p=P)),
                             (beta[:], t["L0_ffn_beta"].rearrange("(a p) -> p a", p=P)),
                             (wrt[:], t["L0_ffn_Wr"].rearrange("(a p) n -> p a n", p=P)),
                             (br[:], t["L0_ffn_br"].rearrange("(a n) -> a n", a=1))):
                sp.dma_start(dst, src, allow_slow_non_contiguous=True).then_inc(s_w, 16)

            def load(k, s):
                i = 2 * k + s
                if not first(k):
                    sp.wait_ge(s_sum, 3 * i - 3)
                    sp.nop(nofuse=True)
                sp.dma_start(xin[:, s], pair_of(scratch["x1"], i)).then_inc(s_ld[s], 16)
                for r in range(NACC):
                    sp.dma_start(agg[r][:, s], pair_of(scratch["agg"][r], i)).then_inc((s_ld if r < 2 else s_ld2)[s], 16)

            def store_x1(k, s):
                sp.wait_ge(s_sum, 3 * (2 * k + s) + 3)
                sp.nop(nofuse=True)
                sp.dma_start(pair_of(scratch["x1"], 2 * k + s), x1[:, s]).then_inc(s_x1st[s], 16)

            def body(k, s):
                if not (isinstance(k, int) and 2 * k + s == PAIRS - 1):
                    load(*((k, 1) if s == 0 else (k + 1, 0)))
                store_x1(k, s)

            load(0, 0)
            for e in range(NE):
                sp.dma_start(b1c[:, e, :], t["L0_ffn_b1"][e].rearrange("(c p) -> p c", p=P),
                             allow_slow_non_contiguous=True).then_inc(s_aux, 16)
            sp.dma_start(scratch["x1"][TRASH:TRASH + P, :], zeros[:, 0:D]).then_inc(s_aux, 16)
            sp.wait_ge(s_aux, 16 * (NE + 1))
            sp.dma_start(scratch["b1"].rearrange("e p c -> p e c"), b1c[:]).then_inc(s_aux, 16)
            over_pairs(sp, body)
            sp.wait_ge(s_aux, 16 * (NE + 2))
            for s in range(2):
                sp.wait_ge(s_x1st[s], 16 * ((PAIRS + 1 - s) // 2))
                sp.nop(nofuse=True)

        @block.gpsimd
        def _(pool):
            def body(k, s):
                i = 2 * k + s
                pool.wait_ge(s_ld2[s], 32 * k + 32)
                if not first(k):
                    pool.wait_ge(s_sum, 3 * i - 3)
                nc.gpsimd.tensor_tensor(half[:, s], agg[2][:, s], agg[3][:, s], ALU.add).then_inc(s_half, 1)
                if not (first(k) and s == 0):
                    send(*before(k, s))

            def send(k, s):
                i = 2 * k + s
                pool.wait_ge(s_pos, 5 * i + 5)
                for c in range(2):
                    for m in range(2):
                        if not (first(k) and s == 0 and c == 0):
                            pool.wait_ge(s_sent[m], 16 * (2 * i + c))
                        pool.nop(nofuse=True)
                        pool.indirect_dma_start(scratch["table"][m][:, :],
                                                bass.IndirectOffsetOnAxis(ap=pos[:, s, c, m:m + 1], axis=0),
                                                z[:, s, c, :], None).then_inc(s_sent[m], 16)
            over_pairs(pool, body)
            send(*divmod(PAIRS - 1, 2))
            for m in range(2):
                pool.wait_ge(s_sent[m], 16 * TILES)

        @block.vector
        def _(dve):
            def gather_sums(k, s):
                i = 2 * k + s
                dve.wait_ge(s_ld[s], 48 * k + 48)
                if not first(k):
                    dve.wait_ge(s_z, i - 1)
                    dve.wait_ge(s_x1st[s], 16 * k)
                nc.vector.tensor_tensor(x1[:, s], xin[:, s], agg[0][:, s], ALU.add).then_inc(s_sum, 1)
                dve.wait_ge(s_sum, 3 * i + 1)
                nc.vector.tensor_tensor(x1[:, s], x1[:, s], agg[1][:, s], ALU.add).then_inc(s_sum, 1)
                dve.wait_ge(s_sum, 3 * i + 2)
                dve.wait_ge(s_half, i + 1)
                nc.vector.tensor_tensor(x1[:, s], x1[:, s], half[:, s], ALU.add).then_inc(s_sum, 1)
                dve.wait_ge(s_sum, 3 * i + 3)
                for c in range(2):
                    last = nc.vector.bn_stats(stat[:, c, :], x1[:, s, c, :])
                last.then_inc(s_st, 1)
                dve.wait_ge(s_st, 3 * i + 1)
                dve.nop(nofuse=True)
                for c in range(2):
                    last = nc.vector.bn_aggr(mv[:, s, c, :], stat[:, c, :])
                last.then_inc(s_st, 1)
                dve.wait_ge(s_st, 3 * i + 2)
                nc.vector.tensor_scalar(vs[:, s], mv[:, s, :, 1], 1.0 + EPS, EPS * EPS, ALU.mult, ALU.add).then_inc(s_st, 1)

            def normalise(k, s):
                i = 2 * k + s
                dve.wait_ge(s_std, i + 1)
                nc.vector.reciprocal(scl[:, s], std[:, s]).then_inc(s_scl, 1)
                dve.wait_ge(s_scl, i + 1)
                if not first(k):
                    dve.wait_ge(s_T, i - 1)
                    dve.wait_ge(s_sent[0], 16 * (2 * i - 2))
                    dve.wait_ge(s_sent[1], 16 * (2 * i - 2))
                nc.vector.tensor_copy(z[:, s, :, D], nodes[:, bass.ds(2 * i, 2)])
                for c in range(2):
                    last = nc.vector.tensor_scalar(z[:, s, c, 0:D], x1[:, s, c, :], mv[:, s, c, 0:1], scl[:, s, c:c + 1],
                                                   ALU.subtract, ALU.mult)
                last.then_inc(s_z, 1)

            def route(k, s):
                i = 2 * k + s
                dve.wait_ge(s_L, i + 1)
                nc.vector.tensor_copy(lg[:], L[s][:, 0:2 * NE].rearrange("p (a e) -> p a e", a=2)).then_inc(s_lg, 1)
                dve.wait_ge(s_lg, 5 * i + 1)
                dve.nop(nofuse=True)
                for c in range(2):
                    last = nc.vector.max(top[:, c, :], lg[:, c, :])
                last.then_inc(s_lg, 1)
                dve.wait_ge(s_lg, 5 * i + 2)
                dve.nop(nofuse=True)
                for c in range(2):
                    last = nc.vector.max_index(idx[:, c, :], top[:, c, :], lg[:, c, :])
                last.then_inc(s_lg, 1)
                nc.vector.tensor_tensor(z[:, s, :, D + 1], top[:, :, 0], top[:, :, 1], ALU.subtract)
                nc.vector.tensor_tensor(z[:, s, :, D + 2], top[:, :, 1], top[:, :, 0], ALU.subtract).then_inc(s_lg, 1)
                dve.wait_ge(s_lg, 5 * i + 4)
                nc.vector.tensor_copy(idxf[:], idx[:, :, 0:2]).then_inc(s_lg, 1)
                dve.wait_ge(s_lg, 5 * i + 5)
                if not (first(k) and s == 0):
                    dve.wait_ge(s_rank, i)
                hot_rows = hot[:].rearrange("p c m e -> p (c m) e")
                nc.vector.tensor_tensor(hot_rows, idxf[:].rearrange("p c (m a) -> p (c m) a", a=1).to_broadcast([P, 4, NE]),
                                        iota8[:].rearrange("p (a e) -> p a e", a=1).to_broadcast([P, 4, NE]),
                                        ALU.is_equal).then_inc(s_hot, 1)

            def position(k, s):
                i = 2 * k + s
                dve.wait_ge(s_rank, i + 1)
                for c in range(2):
                    last = nc.vector.tensor_tensor(place[:, c].rearrange("p m e -> p (m e)"),
                                                   R[s][:, c * 2 * NE:(c + 1) * 2 * NE], run[:], ALU.add)
                last.then_inc(s_pos, 1)
                dve.wait_ge(s_pos, 5 * i + 1)
                nc.vector.tensor_tensor(run[:], run[:], R[s][:, 4 * NE:6 * NE], ALU.add).then_inc(s_pos, 1)
                nc.vector.tensor_tensor(place[:], place[:], hot[:], ALU.mult).then_inc(s_pos, 1)
                dve.wait_ge(s_pos, 5 * i + 3)
                nc.vector.tensor_reduce(posf[:], place[:].rearrange("p c m e -> p (c m) e"), AX_X, ALU.add).then_inc(s_pos, 1)
                dve.wait_ge(s_pos, 5 * i + 4)
                if not first(k):
                    dve.wait_ge(s_sent[0], 16 * (2 * i - 2))
                    dve.wait_ge(s_sent[1], 16 * (2 * i - 2))
                nc.vector.tensor_copy(pos[:, s].rearrange("p c m -> p (c m)"), posf[:]).then_inc(s_pos, 1)

            def body(k, s):
                gather_sums(k, s)
                if not (first(k) and s == 0):
                    route(*before(k, s))
                normalise(k, s)
                if not (first(k) and s == 0):
                    position(*before(k, s))

            over_pairs(dve, body)
            route(*divmod(PAIRS - 1, 2))
            position(*divmod(PAIRS - 1, 2))

        @block.tensor
        def _(pe):
            pe.wait_ge(s_w, 64)

            def turn(k, s):
                i = 2 * k + s
                pe.wait_ge(s_z, i + 1)
                if not first(k):
                    pe.wait_ge(s_xf, i - 1)
                for c in range(2):
                    for a in range(HALF):
                        mm = nc.tensor.transpose(T[s][:, a * D + c * P:a * D + (c + 1) * P],
                                                 z[:, s, c, a * P:(a + 1) * P], ident[:])
                mm.then_inc(s_T, 1)

            def logits(k, s):
                i = 2 * k + s
                pe.wait_ge(s_xf, i + 1)
                if not first(k):
                    pe.wait_ge(s_lg, 5 * i - 9)
                for c in range(2):
                    bank = L[s][:, c * NE:(c + 1) * NE]
                    for a in range(HALF):
                        nc.tensor.matmul(bank, xf[:, s, a, c * P:(c + 1) * P], wrt[:, a, :], start=(a == 0), stop=False)
                    mm = nc.tensor.matmul(bank, ones[0:1, :], br[:], start=False, stop=True)
                mm.then_inc(s_L, 1)

            def rank(k, s):
                i = 2 * k + s
                pe.wait_ge(s_hot, i + 1)
                if not first(k):
                    pe.wait_ge(s_pos, 5 * i - 6)
                ohs = [hot[:, c].rearrange("p m e -> p (m e)") for c in range(2)]
                w = 2 * NE
                nc.tensor.matmul(R[s][:, 0:w], lower[:], ohs[0], start=True, stop=True)
                nc.tensor.matmul(R[s][:, w:2 * w], lower[:], ohs[1], start=True, stop=False)
                nc.tensor.matmul(R[s][:, w:2 * w], ones[:], ohs[0], start=False, stop=True)
                nc.tensor.matmul(R[s][:, 2 * w:3 * w], ones[:], ohs[0], start=True, stop=False)
                nc.tensor.matmul(R[s][:, 2 * w:3 * w], ones[:], ohs[1], start=False, stop=True).then_inc(s_rank, 1)

            def body(k, s):
                turn(k, s)
                if not (first(k) and s == 0):
                    rank(*before(k, s))
                logits(k, s)
            over_pairs(pe, body)
            rank(*divmod(PAIRS - 1, 2))

        @block.scalar
        def _(act):
            def body(k, s):
                i = 2 * k + s
                act.wait_ge(s_st, 3 * i + 3)
                nc.scalar.activation(std[:, s], vs[:, s], ACT.Sqrt).then_inc(s_std, 1)
                act.wait_ge(s_T, i + 1)
                if not first(k):
                    act.wait_ge(s_L, i - 1)
                for a in range(HALF):
                    last = nc.scalar.activation(xf[:, s, a, :], T[s][:, a * D:(a + 1) * D], ACT.Identity,
                                                bias=beta[:, a:a + 1], scale=gamma[:, a:a + 1])
                last.then_inc(s_xf, 1)
            act.wait_ge(s_w, 64)
            over_pairs(act, body)


def plan_phase(nc, scratch, iotaq, base, run, offset, expert, trash):
    with ExitStack() as ctx:
        def sb(name, shape, dt=F32):
            return ctx.enter_context(nc.sbuf_tensor(name, shape, dt))

        def sem(name):
            return ctx.enter_context(nc.semaphore(name))

        fill = sb("p_fill", [P, 2, ROW])
        ends = sb("p_ends", [1, 2 * NE], I32)
        count = sb("p_count", [1, 2 * NE])
        whole = sb("p_whole", [1, 2 * NE], I32)
        blocks = sb("p_blocks", [1, 2, NE])
        upto = sb("p_upto", [1, 2, NE])
        past = sb("p_past", [1, 2, BLOCKS, NE])
        taken = sb("p_taken", [1, 2, BLOCKS, NE])
        pe_ = sb("p_expert", [1, 2, BLOCKS])
        po = sb("p_offset", [1, 2, BLOCKS])
        pt = sb("p_blocks_before", [1, 2, BLOCKS])
        s_v = sem("p_step")
        s_fill = sem("p_fill_ready")
        s_st = sem("p_filled")
        block = ctx.enter_context(nc.Block())

        @block.vector
        def _(dve):
            done = [0]

            def step(ins):
                done[0] += 1
                ins.then_inc(s_v, 1)
                dve.wait_ge(s_v, done[0])

            nc.vector.memset(fill[:], 0.0).then_inc(s_fill, 1)
            dve.wait_ge(s_fill, 1)
            for c in range(2):
                last = nc.vector.tensor_copy(fill[:, c, D:D + 1], trash[:, 0:1])
            last.then_inc(s_fill, 1)
            nc.vector.tensor_copy(ends[:], run[0:1, :]).then_inc(s_fill, 1)
            step(nc.vector.tensor_tensor(count[:], run[0:1, :], base[0:1, :], ALU.subtract))
            step(nc.vector.tensor_scalar(whole[:], count[:], float(CAP - 1), None, ALU.add))
            step(nc.vector.tensor_scalar(whole[:], whole[:], CAP.bit_length() - 1, None, ALU.arith_shift_right))
            step(nc.vector.tensor_copy(blocks[:].rearrange("p m e -> p (m e)"), whole[:]))
            step(nc.vector.tensor_copy(upto[:], blocks[:]))
            for e in range(1, NE):
                step(nc.vector.tensor_tensor(upto[:, :, e], upto[:, :, e], upto[:, :, e - 1], ALU.add))
            turns = iotaq[0:1, :].rearrange("p (q a) -> p q a", a=1).to_broadcast([1, BLOCKS, NE])
            for m in range(2):
                ends_m = upto[:, m:m + 1, :].to_broadcast([1, BLOCKS, NE])
                have_m = blocks[:, m:m + 1, :].to_broadcast([1, BLOCKS, NE])
                step(nc.vector.tensor_tensor(past[:, m], turns, ends_m, ALU.is_ge))
                step(nc.vector.tensor_tensor(taken[:, m], past[:, m], have_m, ALU.mult))
                step(nc.vector.tensor_reduce(pe_[:, m], past[:, m], AX_X, ALU.add))
                step(nc.vector.tensor_reduce(pt[:, m], taken[:, m], AX_X, ALU.add))
                step(nc.vector.tensor_tensor(pt[:, m], iotaq[0:1, :], pt[:, m], ALU.subtract))
                step(nc.vector.tensor_scalar(pt[:, m], pt[:, m], float(CAP), None, ALU.mult))
                step(nc.vector.tensor_scalar(po[:, m], pe_[:, m], float(REGION), None, ALU.mult))
                step(nc.vector.tensor_tensor(po[:, m], po[:, m], pt[:, m], ALU.add))
                step(nc.vector.tensor_scalar(offset[:, m * BLOCKS:(m + 1) * BLOCKS], po[:, m], float(NE * REGION), None, ALU.min))
                step(nc.vector.tensor_scalar(expert[:, m * BLOCKS:(m + 1) * BLOCKS], pe_[:, m], float(NE - 1), None, ALU.min))

        @block.sync
        def _(sp):
            sp.wait_ge(s_fill, 3)
            sp.nop(nofuse=True)
            n = 0
            for m in range(2):
                table = scratch["table"][m]
                for e in range(NE):
                    at = sp.value_load(ends[0:1, m * NE + e:m * NE + e + 1], min_val=0, max_val=NE * REGION - CAP)
                    sp.dma_start(table[bass.ds(at, CAP), :].rearrange("(a p) d -> p a d", p=P), fill[:]).then_inc(s_st, 16)
                    n += 1
                sp.dma_start(table[NE * REGION:NE * REGION + CAP, :].rearrange("(a p) d -> p a d", p=P), fill[:]).then_inc(s_st, 16)
                n += 1
            sp.wait_ge(s_st, 16 * n)


def expert_phase(nc, t, scratch, out, psum, ident, offset, expert):
    with ExitStack() as ctx:
        def sb(name, shape, dt=F32):
            return ctx.enter_context(nc.sbuf_tensor(name, shape, dt))

        def sem(name):
            return ctx.enter_context(nc.semaphore(name))

        zin = sb("x_zin", [P, 2, 2, ROW])
        w1 = sb("x_w1", [P, 2, HALF, HID])
        w2 = sb("x_w2", [P, 2, HC, D])
        b1 = sb("x_b1", [P, 2, HC])
        b2 = sb("x_b2", [P, 2, D])
        xf = sb("x_xf", [P, 2, HALF, CAP])
        hT = sb("x_hT", [P, 2, HC, CAP])
        th = sb("x_tanh", [P, 2, 2])
        share = sb("x_share", [P, 2, 2])
        node = sb("x_node", [P, 2, 2], I32)
        y = sb("x_y", [P, 2, 2, D])
        gamma = sb("x_gamma", [P, HALF])
        beta = sb("x_beta", [P, HALF])
        H = [psum[r] for r in range(HC)]
        Y = [psum[HC], psum[HC + 1]]
        T = [psum[6], psum[7]]
        s_w = sem("x_norm_weights")
        s_z = [sem(f"x_rows_loaded{s}") for s in range(2)]
        s_ld = [sem(f"x_weights_loaded{s}") for s in range(2)]
        s_T = sem("x_turned")
        s_xf = sem("x_xf")
        s_th = sem("x_tanh")
        s_share = sem("x_share")
        s_H = sem("x_hidden")
        s_g = sem("x_gelu")
        s_Y = sem("x_expert_out")
        s_yb = sem("x_out_biased")
        s_y = sem("x_out_weighted")
        s_add = sem("x_added")
        s_out = sem("x_out_stored")
        block = ctx.enter_context(nc.Block())
        TOTAL = 2 * BLOCKS

        def over_blocks(engine, body):
            body(0, 0, 0)
            body(0, 1, 0)
            with engine.Fori(1, BLOCKS // 2) as k:
                body(k, 0, 0)
                body(k, 1, 0)
            with engine.Fori(BLOCKS // 2, BLOCKS - 1) as k:
                body(k, 0, 1)
                body(k, 1, 1)
            body(BLOCKS - 1, 0, 1)
            body(BLOCKS - 1, 1, 1)

        @block.sync
        def _(sp):
            for dst, src in ((gamma[:], t["L0_ffn_gamma"]), (beta[:], t["L0_ffn_beta"])):
                sp.dma_start(dst, src.rearrange("(a p) -> p a", p=P), allow_slow_non_contiguous=True).then_inc(s_w, 16)

            def body(k, s, m):
                q = 2 * k + s
                at = sp.value_load(offset[0:1, bass.ds(q, 1)], min_val=0, max_val=NE * REGION)
                e = sp.value_load(expert[0:1, bass.ds(q, 1)], min_val=0, max_val=NE - 1)
                if not first(k):
                    sp.wait_ge(s_T, q - 1)
                    sp.nop(nofuse=True)
                    sp.wait_ge(s_share, q - 1)
                    sp.nop(nofuse=True)
                sp.dma_start(zin[:, s], scratch["table"][m][bass.ds(at, CAP), :].rearrange("(a p) d -> p a d", p=P)).then_inc(s_z[s], 16)
                if not first(k):
                    sp.wait_ge(s_yb, q - 1)
                    sp.nop(nofuse=True)
                sp.dma_start(w1[:, s], t["L0_ffn_W1"][bass.ds(e, 1)].rearrange("e (a p) n -> p (e a) n", p=P)).then_inc(s_ld[s], 16)
                sp.dma_start(w2[:, s], t["L0_ffn_W2"][bass.ds(e, 1)].rearrange("e (a p) n -> p (e a) n", p=P)).then_inc(s_ld[s], 16)
                sp.dma_start(b1[:, s], scratch["b1"][bass.ds(e, 1)].rearrange("e p c -> p (e c)")).then_inc(s_ld[s], 16)
                sp.dma_start(b2[:, s], t["L0_ffn_b2"][bass.ds(e, 1)].to_broadcast([P, D])).then_inc(s_ld[s], 16)

            over_blocks(sp, body)
            sp.wait_ge(s_add, 16 * 2 * TOTAL)
            whole = N // 16 * 16
            lines = 16 * (whole // 16 // 11)
            sp.dma_start(out[0:lines * 11, :].rearrange("(a b) d -> a (b d)", b=11),
                         scratch["x1"][0:lines * 11, :].rearrange("(a b) d -> a (b d)", b=11)).then_inc(s_out, 16)
            sp.dma_start(out[lines * 11:N, :], scratch["x1"][lines * 11:N, :]).then_inc(s_out, 16)
            sp.wait_ge(s_out, 32)

        @block.tensor
        def _(pe):
            def turn(k, s):
                q = 2 * k + s
                pe.wait_ge(s_z[s], 16 * k + 16)
                if not first(k):
                    pe.wait_ge(s_xf, q - 1)
                for c in range(2):
                    for a in range(HALF):
                        mm = nc.tensor.transpose(T[s][:, a * D + c * P:a * D + (c + 1) * P],
                                                 zin[:, s, c, a * P:(a + 1) * P], ident[:])
                mm.then_inc(s_T, 1)

            def body(k, s, m):
                q = 2 * k + s
                pe.wait_ge(s_ld[s], 64 * k + 64)
                pe.wait_ge(s_xf, q + 1)
                for c in range(HC):
                    if not (first(k) and s == 0):
                        pe.wait_ge(s_g, HC * (q - 1) + c + 1)
                    for a in range(HALF):
                        mm = nc.tensor.matmul(H[c][:, 0:CAP], w1[:, s, a, c * P:(c + 1) * P], xf[:, s, a, :],
                                              start=(a == 0), stop=(a == HALF - 1))
                    mm.then_inc(s_H, 1)
                if not (isinstance(k, int) and q == TOTAL - 1):
                    turn(*((k, 1) if s == 0 else (k + 1, 0)))
                if not first(k):
                    pe.wait_ge(s_yb, q - 1)
                for c in range(HC):
                    pe.wait_ge(s_g, HC * q + c + 1)
                    for h in range(2):
                        mm = nc.tensor.matmul(Y[s][:, h * D:(h + 1) * D], hT[:, s, c, h * P:(h + 1) * P],
                                              w2[:, s, c, :], start=(c == 0 and h == 0), stop=(c == HC - 1),
                                              skip_group_check=True)
                mm.then_inc(s_Y, 1)

            turn(0, 0)
            over_blocks(pe, body)

        @block.scalar
        def _(act):
            act.wait_ge(s_w, 32)

            def features(k, s):
                q = 2 * k + s
                act.wait_ge(s_T, q + 1)
                if not first(k):
                    act.wait_ge(s_H, HC * (q - 1))
                for a in range(HALF):
                    last = nc.scalar.activation(xf[:, s, a, :], T[s][:, a * D:(a + 1) * D], ACT.Identity,
                                                bias=beta[:, a:a + 1], scale=gamma[:, a:a + 1])
                last.then_inc(s_xf, 1)

            def body(k, s, m):
                q = 2 * k + s
                act.wait_ge(s_z[s], 16 * k + 16)
                if not first(k):
                    act.wait_ge(s_share, q - 1)
                nc.scalar.activation(th[:, s], zin[:, s, :, D + 1 + m], ACT.Tanh, scale=0.5).then_inc(s_th, 1)
                act.wait_ge(s_ld[s], 64 * k + 64)
                for c in range(HC):
                    act.wait_ge(s_H, HC * q + c + 1)
                    if c == 0 and not first(k):
                        act.wait_ge(s_Y, q - 1)
                    nc.scalar.activation(hT[:, s, c, :], H[c][:, 0:CAP], ACT.Gelu, bias=b1[:, s, c:c + 1]).then_inc(s_g, 1)
                if not (isinstance(k, int) and q == TOTAL - 1):
                    features(*((k, 1) if s == 0 else (k + 1, 0)))

            features(0, 0)
            over_blocks(act, body)

        @block.vector
        def _(dve):
            def body(k, s, m):
                q = 2 * k + s
                dve.wait_ge(s_th, q + 1)
                if not first(k):
                    dve.wait_ge(s_add, 32 * (q - 1))
                nc.vector.tensor_copy(node[:, s], zin[:, s, :, D])
                nc.vector.tensor_scalar(share[:, s], th[:, s], 0.5, 0.5, ALU.mult, ALU.add).then_inc(s_share, 1)
                dve.wait_ge(s_ld[s], 64 * k + 64)
                dve.wait_ge(s_Y, q + 1)
                for c in range(2):
                    last = nc.vector.tensor_tensor(y[:, s, c, :], Y[s][:, c * D:(c + 1) * D], b2[:, s], ALU.add)
                last.then_inc(s_yb, 1)
                dve.wait_ge(s_yb, q + 1)
                dve.wait_ge(s_share, q + 1)
                for c in range(2):
                    nc.vector.tensor_scalar(y[:, s, c, :], y[:, s, c, :], share[:, s, c:c + 1], None,
                                            ALU.mult).then_inc(s_y, 1)
            over_blocks(dve, body)

        @block.gpsimd
        def _(pool):
            def body(k, s, m):
                q = 2 * k + s
                for c in range(2):
                    pool.wait_ge(s_y, 2 * q + c + 1)
                    if not (first(k) and s == 0 and c == 0):
                        pool.wait_ge(s_add, 16 * (2 * q + c))
                    pool.nop(nofuse=True)
                    pool.indirect_dma_start(scratch["x1"][:, :],
                                            bass.IndirectOffsetOnAxis(ap=node[:, s, c:c + 1], axis=0),
                                            y[:, s, c, :], None, compute_op=ALU.add).then_inc(s_add, 16)
            over_blocks(pool, body)


_INS = ['x', 'src', 'dst', 'edge_weight', 'L0_gnn_weight_l', 'L0_gnn_bias_l', 'L0_gnn_weight_r', 'L0_gnn_bias_r',
        'L0_mix_Wqkv', 'L0_mix_Wproj', 'L0_mix_bproj', 'L0_mix_ln_g', 'L0_mix_ln_b', 'L0_mix_Wg1', 'L0_mix_bg1',
        'L0_mix_Wg2', 'L0_mix_bg2', 'L0_ffn_gamma', 'L0_ffn_beta', 'L0_ffn_Wr', 'L0_ffn_br', 'L0_ffn_W1',
        'L0_ffn_b1', 'L0_ffn_W2', 'L0_ffn_b2']


def kernel(**inputs):
    import numpy as _np
    import concourse.bacc as _bacc
    from concourse import mybir as _mybir
    from concourse.bass_utils import run_bass_kernel_spmd as _run

    nc = _bacc.Bacc("TRN2", target_bir_lowering=False, num_devices=1)
    arrays, t = {}, {}
    for name in _INS:
        a = _np.ascontiguousarray(inputs[name])
        arrays[f"in_{name}_dram"] = a
        t[name] = nc.dram_tensor(f"in_{name}_dram", a.shape, _mybir.dt.from_np(a.dtype), kind="ExternalInput").ap()

    def internal(name, shape, dtype=_mybir.dt.float32):
        return nc.dram_tensor(name, shape, dtype, kind="Internal").ap()

    scratch = {"xn": internal("xn_rows", (NPAD, D)), "xnT": internal("xn_turned", (NPAD, D)),
               "h": internal("h_rows", (NPAD, D)), "x1": internal("x1_rows", (AGG_ROWS, D)),
               "base": internal("window_bases", (CHUNKS // WINDOW,), _mybir.dt.int32),
               "general": internal("general_groups", (GROUPS,), _mybir.dt.int32),
               "b1": internal("b1_turned", (NE, P, HC)),
               "table": [internal(f"table{m}", (NE * REGION + CAP, ROW)) for m in range(2)],
               "agg": [internal(f"agg{r}", (AGG_ROWS, D)) for r in range(NACC)]}
    out = nc.dram_tensor("out_0_dram", (N, D), _mybir.dt.float32, kind="ExternalOutput").ap()
    build(nc, t, scratch, out)
    r = _run(nc, [arrays], core_ids=[0])
    return r.results[0]["out_0_dram"]
```

```python
from contextlib import ExitStack

import numpy as np

import concourse.bass as bass
from concourse import mybir

F32 = mybir.dt.float32
BF16 = mybir.dt.bfloat16
I32 = mybir.dt.int32
U32 = mybir.dt.uint32
ALU = mybir.AluOpType
ACT = mybir.ActivationFunctionType
AX_X = mybir.AxisListType.X

P = 128
N, D = 12500, 256
E = 212500
NH, HD = 8, 32
GH = 64
NE, HID = 8, 512
EPS = 1e-5

TILES = -(-N // P)
LAST = N - (TILES - 1) * P
PAIRS = TILES // 2
NPAD = TILES * P
HALF = D // P
HC = HID // P

CHUNK_GROUP = 16
WINDOW = 8
BATCH = 4
SPAN = P // 2
EROWS = -(-E // P)
GROUPS = -(-EROWS // CHUNK_GROUP)
CHUNKS = GROUPS * CHUNK_GROUP
BTILES = -(-CHUNKS // BATCH // SPAN)
BFULL = E // (BATCH * P)
ETILES = CHUNKS // P
EFULL = E // P
NACC = 4
TRASH = NPAD
AGG_ROWS = NPAD + P
assert NPAD <= P * P
assert TILES % 2 == 0 and CHUNKS % P == 0 and CHUNK_GROUP % NACC == 0

CAP = 2 * P
BLOCKS = -(-NPAD // CAP) + NE - 1
BLOCKS += BLOCKS % 2
REGION = NPAD + CAP
ROW = D + 3
TAIL_GROUPS = GROUPS - 2 * PAIRS
assert TAIL_GROUPS >= 3


def build(nc, t, scratch, out):
    with ExitStack() as ctx:
        def sb(name, shape, dt=F32):
            return ctx.enter_context(nc.sbuf_tensor(name, shape, dt))

        def sem(name):
            return ctx.enter_context(nc.semaphore(name))

        ident = sb("ident", [P, P])
        prior = sb("prior", [P, P])
        trash = sb("trash", [P, 1])
        iota8 = sb("iota8", [P, NE])
        lower = sb("lower", [P, P])
        iotaq = sb("iotaq", [P, BLOCKS])
        nodes = sb("nodes", [P, TILES])
        base = sb("base", [P, 2 * NE])
        run = sb("run", [P, 2 * NE])
        offset = sb("offset", [1, 2, BLOCKS], I32)[:].rearrange("p m q -> p (m q)")
        expert = sb("expert", [1, 2, BLOCKS], I32)[:].rearrange("p m q -> p (m q)")
        ones = sb("ones", [P, P])
        zeros = sb("zeros", [P, 512])
        gscale = sb("gscale", [P, TILES])
        srcf = sb("srcf", [P, CHUNKS])
        packed = sb("packed", [P, BTILES, BATCH * P], BF16)
        both = sb("both", [P, SPAN], BF16)
        iotaf = sb("iotaf", [P, P])
        wtf = sb("wtf", [P, CHUNKS])
        dsti = sb("dsti", [P, CHUNKS], I32)
        locf = sb("locf", [P, CHUNKS])
        base_row = sb("window_base", [1, CHUNKS // WINDOW], I32)
        general = sb("general_group", [1, GROUPS], I32)
        psum = [ctx.enter_context(nc.psum_tensor(f"bank{i}", [P, 512], F32)) for i in range(8)]

        edges = dict(src=srcf, packed=packed, both=both, iota=iotaf, weight=wtf, dst=dsti, local=locf,
                     base=base_row, general=general)
        setup_phase(nc, ctx, t, scratch, psum, ident, prior, trash, iota8, ones, zeros,
                    lower, iotaq, nodes, base, run, edges)
        with ExitStack() as mid:
            kmax = mid.enter_context(nc.sbuf_tensor("kmax", [P, D], F32))
            wk = mid.enter_context(nc.sbuf_tensor("wk", [P, HALF, D], F32))
            norm_phase(nc, t, scratch, psum, ident, zeros, gscale, kmax, wk)
            edge_mix_phase(nc, t, scratch, psum, ident, prior, trash, ones, zeros, gscale,
                           edges, kmax, wk)
        route_phase(nc, t, scratch, psum, ident, ones, zeros, iota8, lower, run, nodes)
        plan_phase(nc, scratch, iotaq, base, run, offset, expert, trash)
        expert_phase(nc, t, scratch, out, psum, ident, offset, expert)


def setup_phase(nc, outer, t, scratch, psum, ident, prior, trash, iota8, ones, zeros,
                lower, iotaq, nodes, base, run, edges):
    with ExitStack() as ctx:
        def sem(name):
            return ctx.enter_context(nc.semaphore(name))
        raw = {k: ctx.enter_context(nc.sbuf_tensor(f"raw_{k}", [P, ETILES, P], dt))
               for k, dt in (("src", I32), ("dst", I32), ("wt", F32))}
        flt = {k: ctx.enter_context(nc.sbuf_tensor(f"flt_{k}", [P, ETILES, P], F32)) for k in ("src", "dst", "loc")}
        srcf, wtf, dsti, locf = edges["src"], edges["weight"], edges["dst"], edges["local"]

        def sb(name, shape, dt=F32):
            return ctx.enter_context(nc.sbuf_tensor(name, shape, dt))
        raw_end = sb("raw_end", [P, P], I32)
        flt_end = sb("flt_end", [P, P])
        low = sb("low", [P, P])
        high = sb("high", [P, P])
        wbase = sb("wbase", [P, P // WINDOW])
        whigh = sb("whigh", [P, P // WINDOW])
        wfit = sb("wfit", [P, P // WINDOW])
        wbad = sb("wbad", [P, 1])
        gfit = sb("gfit", [P, P // CHUNK_GROUP])
        wbase_i = sb("wbase_i", [P, P // WINDOW], I32)
        ggen = sb("ggen", [P, P // CHUNK_GROUP], I32)
        cbase = sb("cbase", [P, P])
        cfit = sb("cfit", [P, P])
        tbase = sb("tbase", [P, P])
        tfit = sb("tfit", [P, P])
        tgen = sb("tgen", [P, P])
        wide = sb("wide", [P, BTILES, BATCH * P], I32)
        s_wide = sem("setup_wide")
        s_win = sem("setup_windows")
        s_wturn = sem("setup_windows_turned")
        s_plan = sem("setup_plan_moved")
        s_clear = sem("setup_clear")
        s_load = sem("setup_load")
        s_const = sem("setup_const")
        s_pool = sem("setup_pool")
        s_flt = sem("setup_flt")
        s_turn = sem("setup_turn")
        s_taken = sem("setup_taken")
        dram = {"src": t["src"], "dst": t["dst"], "wt": t["edge_weight"]}
        block = ctx.enter_context(nc.Block())
        full_tiles = EFULL // P
        rest_rows = EFULL - full_tiles * P
        rest = E - EFULL * P
        WSPAN, WBAD, WPLAN, WLOCAL = 3, 11, 16, 21

        @block.sync
        def _(sp):
            sp.wait_ge(s_clear, 6)
            for k, a in dram.items():
                sp.dma_start(raw[k][:, 0:full_tiles, :],
                             a[0:full_tiles * P * P].rearrange("(t c p) -> c t p", c=P, p=P)).then_inc(s_load, 16)
                sp.dma_start(raw[k][0:rest_rows, full_tiles, :],
                             a[full_tiles * P * P:EFULL * P].rearrange("(c p) -> c p", p=P)).then_inc(s_load, 16)
                sp.dma_start(raw[k][rest_rows:rest_rows + 1, full_tiles, 0:rest],
                             a[EFULL * P:E].rearrange("(a p) -> a p", a=1)).then_inc(s_load, 16)
            tiles, row = BFULL // SPAN, BATCH * P
            for half in (0, SPAN):
                sp.dma_start(wide[half:half + SPAN, 0:tiles, :],
                             t["src"][0:tiles * SPAN * row].rearrange("(t c e) -> c t e", c=SPAN, e=row)).then_inc(s_wide, 16)
                sp.dma_start(wide[half:half + BFULL % SPAN, tiles, :],
                             t["src"][tiles * SPAN * row:BFULL * row].rearrange("(c e) -> c e", e=row)).then_inc(s_wide, 16)
                at = half + BFULL % SPAN
                sp.dma_start(wide[at:at + 1, tiles, 0:E - BFULL * row],
                             t["src"][BFULL * row:E].rearrange("(a e) -> a e", a=1)).then_inc(s_wide, 16)
            sp.dma_start(raw_end[0:rest_rows, :],
                         t["dst"][full_tiles * P * P:EFULL * P].rearrange("(c p) -> c p", p=P)).then_inc(s_load, 16)
            sp.dma_start(raw_end[rest_rows:rest_rows + 1, 0:rest],
                         t["dst"][EFULL * P:E].rearrange("(a p) -> a p", a=1)).then_inc(s_load, 16)
            sp.wait_ge(s_win, WPLAN)
            sp.dma_start(scratch["base"].rearrange("(t w) -> t w", t=ETILES), wbase_i[0:ETILES, :]).then_inc(s_plan, 16)
            sp.dma_start(scratch["general"].rearrange("(t w) -> t w", t=ETILES), ggen[0:ETILES, :]).then_inc(s_plan, 16)
            sp.wait_ge(s_plan, 32)
            sp.dma_start(edges["base"][:], scratch["base"].rearrange("(a w) -> a w", a=1)).then_inc(s_plan, 16)
            sp.dma_start(edges["general"][:], scratch["general"].rearrange("(a w) -> a w", a=1)).then_inc(s_plan, 16)
            sp.wait_ge(s_plan, 64)

        @block.vector
        def _(dve):
            nc.vector.memset(raw["src"][:, full_tiles, :], 0).then_inc(s_clear, 1)
            nc.vector.memset(raw["dst"][:, full_tiles, :], 0).then_inc(s_clear, 1)
            nc.vector.memset(raw["wt"][:, full_tiles, :], 0.0).then_inc(s_clear, 1)
            nc.vector.memset(zeros[:], 0.0).then_inc(s_clear, 1)
            nc.vector.memset(raw_end[:], NPAD).then_inc(s_clear, 1)
            nc.vector.memset(wide[:, BFULL // SPAN:BTILES, :], 0).then_inc(s_clear, 1)
            nc.vector.memset(ones[:], 1.0).then_inc(s_const, 1)
            nc.vector.memset(low[:], 0.0)
            nc.vector.memset(high[:], 0.0)
            dve.wait_ge(s_load, 16 * 11)
            nc.vector.tensor_copy(flt["src"][:], raw["src"][:]).then_inc(s_flt, 1)
            nc.vector.tensor_copy(flt["dst"][:], raw["dst"][:]).then_inc(s_flt, 1)
            nc.vector.tensor_copy(flt_end[:], raw_end[:]).then_inc(s_flt, 1)
            done = [0]

            def step(*ins):
                for i in ins:
                    i.then_inc(s_win, 1)
                done[0] += len(ins)
                dve.wait_ge(s_win, done[0])

            dve.wait_ge(s_flt, 3)
            step(nc.vector.tensor_reduce(low[:, 0:full_tiles], flt["dst"][:, 0:full_tiles, :], AX_X, ALU.min),
                 nc.vector.tensor_reduce(low[:, full_tiles:ETILES], flt_end[:].rearrange("p (a c) -> p a c", a=1), AX_X, ALU.min),
                 nc.vector.tensor_reduce(high[:, 0:ETILES], flt["dst"][:], AX_X, ALU.max))
            assert done[0] == WSPAN
            dve.wait_ge(s_wturn, 2)
            step(nc.vector.tensor_reduce(wbase[:], psum[4][:, 0:P].rearrange("p (w c) -> p w c", c=WINDOW), AX_X, ALU.min),
                 nc.vector.tensor_reduce(whigh[:], psum[5][:, 0:P].rearrange("p (w c) -> p w c", c=WINDOW), AX_X, ALU.max))
            step(nc.vector.tensor_scalar(wbase[:], wbase[:], float(NPAD - P), None, ALU.min))
            step(nc.vector.tensor_tensor(whigh[:], whigh[:], wbase[:], ALU.subtract),
                 nc.vector.tensor_copy(wbase_i[:], wbase[:]))
            step(nc.vector.tensor_scalar(wfit[:], whigh[:], float(P), None, ALU.is_lt))
            step(nc.vector.tensor_reduce(wbad[:], wfit[:], AX_X, ALU.min))
            step(nc.vector.tensor_scalar(wbad[:], wbad[:], -1.0, 1.0, ALU.mult, ALU.add))
            assert done[0] == WBAD
            dve.wait_ge(s_wturn, 3)
            step(nc.vector.tensor_scalar(wbad[:], psum[6][:, 0:1], 0.5, None, ALU.is_lt))
            step(nc.vector.tensor_copy(gfit[:], wbad[:].to_broadcast([P, P // CHUNK_GROUP])))
            step(nc.vector.tensor_scalar(ggen[:], gfit[:], -1.0, 1.0, ALU.mult, ALU.add),
                 nc.vector.tensor_copy(cbase[:].rearrange("p (w c) -> p w c", c=WINDOW),
                                       wbase[:].rearrange("p (w a) -> p w a", a=1).to_broadcast([P, P // WINDOW, WINDOW])),
                 nc.vector.tensor_copy(cfit[:].rearrange("p (g c) -> p g c", c=CHUNK_GROUP),
                                       gfit[:].rearrange("p (g a) -> p g a", a=1).to_broadcast([P, P // CHUNK_GROUP, CHUNK_GROUP])))
            assert done[0] == WPLAN
            dve.wait_ge(s_wturn, 5)
            step(nc.vector.tensor_copy(tbase[:], psum[4][:, P:2 * P]),
                 nc.vector.tensor_copy(tfit[:], psum[5][:, P:2 * P]))
            step(nc.vector.tensor_scalar(tgen[:], tfit[:], -1.0, 1.0, ALU.mult, ALU.add))
            for i in range(ETILES):
                last = nc.vector.tensor_scalar(flt["loc"][:, i, :], flt["dst"][:, i, :], tbase[:, i:i + 1], tfit[:, i:i + 1],
                                               ALU.subtract, ALU.mult)
            step(last)
            dve.wait_ge(s_pool, 3)
            for i in range(ETILES):
                last = nc.vector.scalar_tensor_tensor(out=flt["loc"][:, i, :], in0=edges["iota"][:], scalar=tgen[:, i:i + 1],
                                                      in1=flt["loc"][:, i, :], op0=ALU.mult, op1=ALU.add)
            step(last)
            assert done[0] == WLOCAL
            n = 0
            for i in range(ETILES):
                for dst in (srcf, dsti, wtf, locf):
                    dve.wait_ge(s_turn, n + 1)
                    nc.vector.tensor_copy(dst[:, i * P:(i + 1) * P], psum[n % 4][:, 0:P]).then_inc(s_taken, 1)
                    n += 1
            dve.wait_ge(s_wide, 96)
            step(nc.vector.tensor_scalar(wide[0:SPAN], wide[0:SPAN], (P - 1) * P, None, ALU.bitwise_and),
                 nc.vector.tensor_scalar(wide[SPAN:P], wide[SPAN:P], P - 1, None, ALU.bitwise_and))
            step(nc.vector.tensor_copy(edges["packed"][:], wide[:]),
                 nc.vector.tensor_tensor(edges["both"][:], ident[:, 0:SPAN], ident[:, SPAN:P], ALU.add))

        @block.gpsimd
        def _(pool):
            nc.gpsimd.iota(edges["iota"][:], pattern=[[1, P]], base=0, channel_multiplier=0,
                           allow_small_or_imprecise_dtypes=True).then_inc(s_pool, 1)
            pool.wait_ge(s_const, 1)
            nc.gpsimd.affine_select(out=ident[:], in_=ones[:], compare_op=ALU.is_equal, fill=0.0, base=0,
                                    pattern=[[-1, P]], channel_multiplier=1).then_inc(s_const, 1)
            nc.gpsimd.iota(prior[:], pattern=[[0, P]], base=TRASH, channel_multiplier=1,
                           allow_small_or_imprecise_dtypes=True).then_inc(s_pool, 1)
            nc.gpsimd.iota(trash[:], pattern=[[0, 1]], base=TRASH, channel_multiplier=1,
                           allow_small_or_imprecise_dtypes=True)
            nc.gpsimd.affine_select(out=lower[:], in_=ones[:], compare_op=ALU.is_ge, fill=0.0, base=-1,
                                    pattern=[[1, P]], channel_multiplier=-1)
            nc.gpsimd.iota(iotaq[:], pattern=[[1, BLOCKS]], base=0, channel_multiplier=0,
                           allow_small_or_imprecise_dtypes=True)
            nc.gpsimd.iota(nodes[:], pattern=[[P, TILES]], base=0, channel_multiplier=1,
                           allow_small_or_imprecise_dtypes=True)
            for a in (base, run):
                nc.gpsimd.iota(a[:], pattern=[[0, 2], [REGION, NE]], base=0, channel_multiplier=0,
                               allow_small_or_imprecise_dtypes=True)
            nc.gpsimd.iota(iota8[:], pattern=[[1, NE]], base=0, channel_multiplier=0,
                           allow_small_or_imprecise_dtypes=True)
            pool.wait_ge(s_pool, 2)
            nc.gpsimd.affine_select(out=prior[:], in_=prior[:], compare_op=ALU.is_ge, fill=0.0, base=-1,
                                    pattern=[[-1, P]], channel_multiplier=1).then_inc(s_pool, 1)

        @block.tensor
        def _(pe):
            pe.wait_ge(s_const, 2)
            pe.wait_ge(s_flt, 2)
            pe.wait_ge(s_win, WSPAN)
            nc.tensor.transpose(psum[4][:, 0:P], low[:], ident[:]).then_inc(s_wturn, 1)
            nc.tensor.transpose(psum[5][:, 0:P], high[:], ident[:]).then_inc(s_wturn, 1)
            pe.wait_ge(s_win, WBAD)
            nc.tensor.matmul(psum[6][:, 0:1], ones[:], wbad[:], start=True, stop=True).then_inc(s_wturn, 1)
            pe.wait_ge(s_win, WPLAN)
            nc.tensor.transpose(psum[4][:, P:2 * P], cbase[:], ident[:]).then_inc(s_wturn, 1)
            nc.tensor.transpose(psum[5][:, P:2 * P], cfit[:], ident[:]).then_inc(s_wturn, 1)
            pe.wait_ge(s_win, WLOCAL)
            n = 0
            for i in range(ETILES):
                for a in (flt["src"], flt["dst"], raw["wt"], flt["loc"]):
                    if n >= 4:
                        pe.wait_ge(s_taken, n - 3)
                    nc.tensor.transpose(psum[n % 4][:, 0:P], a[:, i, :], ident[:]).then_inc(s_turn, 1)
                    n += 1


def first(i):
    return isinstance(i, int) and i == 0


def norm_phase(nc, t, scratch, psum, ident, zeros, gscale, kmax, wk):
    with ExitStack() as ctx:
        def sb(name, shape, dt=F32):
            return ctx.enter_context(nc.sbuf_tensor(name, shape, dt))

        def sem(name):
            return ctx.enter_context(nc.semaphore(name))

        xin = sb("xin", [P, 2, 2, D])
        xnr = sb("xnr", [P, 2, 2, D])
        xnT = sb("xnT", [P, 2, 2, HALF, P])
        hrow = sb("hrow", [P, 2, 2, D])
        stat = sb("stat", [P, 2, 6])
        mv = sb("mv", [P, 2, 2, 2])
        vare = sb("vare", [P, 2, 2])
        std = sb("std", [P, 2, 2])
        kmax2 = sb("kmax2", [P, 2, D])
        varall = sb("varall", [P, TILES])
        rstd = sb("rstd", [P, TILES])
        gvar = sb("gvar", [P, TILES])
        gstd = sb("gstd", [P, TILES])
        wl = sb("wl", [P, HALF, D])
        s_w = sem("n_weights")
        s_in = [sem(f"n_x_loaded{u}") for u in range(2)]
        s_step = sem("n_step")
        s_xn = sem("n_xn")
        s_T = sem("n_turned")
        s_xT = sem("n_xnT")
        s_hk = sem("n_hk")
        s_h = sem("n_h")
        s_max = sem("n_kmax")
        s_xst = [sem(f"n_xn_stored{u}") for u in range(2)]
        s_Tst = [sem(f"n_xnT_stored{u}") for u in range(2)]
        s_hst = [sem(f"n_h_stored{u}") for u in range(2)]
        s_std = sem("n_std")
        s_pad = sem("n_pad")
        s_fin = sem("n_gate_variance")
        s_zeroed = sem("n_accumulators_cleared")
        s_gstd = sem("n_gate_std")
        T = [psum[0], psum[1]]
        H = [psum[2], psum[3]]
        K = [psum[4], psum[5]]
        block = ctx.enter_context(nc.Block())
        x = t["x"]
        LASTK = PAIRS // 2
        assert PAIRS % 2 == 1

        def flat(a):
            return a.rearrange("p c d -> p (c d)")

        @block.sync
        def _(sp):
            wkd = t["L0_mix_Wqkv"][:, D:2 * D].rearrange("(a p) n -> p a n", p=P)
            sp.dma_start(wl[:], t["L0_gnn_weight_l"].rearrange("(a p) n -> p a n", p=P)).then_inc(s_w, 16)
            sp.dma_start(wk[:], wkd).then_inc(s_w, 16)

            def load(k, u):
                i = 2 * k + u
                if not first(k):
                    sp.wait_ge(s_xn, i - 1)
                    sp.nop(nofuse=True)
                if isinstance(k, int) and k == LASTK:
                    sp.wait_ge(s_pad, 1)
                    sp.dma_start(xin[:, u, 0, :], x[(TILES - 2) * P:(TILES - 1) * P, :]).then_inc(s_in[u], 16)
                    sp.dma_start(xin[0:LAST, u, 1, :], x[(TILES - 1) * P:N, :]).then_inc(s_in[u], 16)
                else:
                    sp.dma_start(xin[:, u], pair_of(x, i)).then_inc(s_in[u], 16)

            def clear(i, tiles=2):
                for acc in scratch["agg"]:
                    sp.dma_start(acc[bass.ds(i * 2 * P, tiles * P), :].rearrange("(a p) d -> p a d", p=P),
                                 zeros[:, 0:tiles * D].rearrange("p (a d) -> p a d", a=tiles)).then_inc(s_zeroed, 16)

            def body(k, u):
                load(k, u)
                clear(2 * k + u)

            over_pairs(sp, body)
            clear(PAIRS, tiles=(AGG_ROWS - NPAD) // P)
            sp.wait_ge(s_zeroed, 16 * NACC * (PAIRS + 1))

        @block.vector
        def _(dve):
            nc.vector.memset(kmax2[:], -3.0e38).then_inc(s_max, 1)

            def normalise(k, u):
                i = 2 * k + u
                if isinstance(k, int) and k == LASTK:
                    dve.wait_ge(s_xn, i - 1)
                    nc.vector.memset(xin[:, u, 1, :], 0.0).then_inc(s_pad, 1)
                    dve.wait_ge(s_in[u], 16 * k + 32)
                else:
                    dve.wait_ge(s_in[u], 16 * k + 16)
                for c in range(2):
                    last = nc.vector.bn_stats(stat[:, c, :], xin[:, u, c, :])
                last.then_inc(s_step, 1)
                dve.wait_ge(s_step, 4 * i + 1)
                dve.nop(nofuse=True)
                for c in range(2):
                    last = nc.vector.bn_aggr(mv[:, u, c, :], stat[:, c, :])
                last.then_inc(s_step, 1)
                dve.wait_ge(s_step, 4 * i + 2)
                nc.vector.tensor_scalar(vare[:, u], mv[:, u, :, 1], EPS, None, ALU.add).then_inc(s_step, 1)
                nc.vector.tensor_copy(varall[:, bass.ds(2 * i, 2)], mv[:, u, :, 1])
                dve.wait_ge(s_std, i + 1)
                dve.nop(nofuse=True)
                nc.vector.reciprocal(rstd[:, bass.ds(2 * i, 2)], std[:, u]).then_inc(s_step, 1)
                dve.wait_ge(s_step, 4 * i + 4)
                if not first(k):
                    dve.wait_ge(s_T, i - 1)
                    dve.wait_ge(s_xst[u], 16 * k)
                for c in range(2):
                    last = nc.vector.tensor_scalar(xnr[:, u, c, :], xin[:, u, c, :], mv[:, u, c, 0:1],
                                                   rstd[:, bass.ds(2 * i + c, 1)], ALU.subtract, ALU.mult)
                last.then_inc(s_xn, 1)

            def maximum(k, u):
                i = 2 * k + u
                dve.wait_ge(s_hk, i + 1)
                dve.wait_ge(s_max, i + 1)
                if isinstance(k, int) and k == LASTK:
                    nc.vector.tensor_tensor(kmax2[:, 0, :], kmax2[:, 0, :], K[u][:, 0:D], ALU.max)
                    nc.vector.tensor_tensor(kmax2[0:LAST, 1, :], kmax2[0:LAST, 1, :], K[u][0:LAST, D:2 * D],
                                            ALU.max).then_inc(s_max, 1)
                else:
                    nc.vector.tensor_tensor(flat(kmax2[:]), flat(kmax2[:]), K[u][:, :], ALU.max).then_inc(s_max, 1)

            def body(k, u):
                normalise(k, u)
                if not first(k):
                    maximum(k - 1, u)

            over_pairs(dve, body)
            maximum(LASTK - 1, 1)
            maximum(LASTK, 0)
            dve.wait_ge(s_max, PAIRS + 1)
            nc.vector.tensor_tensor(kmax[:], kmax2[:, 0, :], kmax2[:, 1, :], ALU.max)
            nc.vector.tensor_tensor(gvar[:], rstd[:], rstd[:], ALU.mult).then_inc(s_fin, 1)
            dve.wait_ge(s_fin, 1)
            nc.vector.tensor_tensor(gvar[:], gvar[:], varall[:], ALU.mult).then_inc(s_fin, 1)
            dve.wait_ge(s_fin, 2)
            nc.vector.tensor_scalar(gvar[:], gvar[:], EPS, None, ALU.add).then_inc(s_fin, 1)
            dve.wait_ge(s_gstd, 1)
            nc.vector.reciprocal(gscale[:], gstd[:])

        @block.gpsimd
        def _(pool):
            def store(k, u):
                i = 2 * k + u
                for ready, src, dst, done in ((s_xn, xnr[:, u], scratch["xn"], s_xst),
                                              (s_xT, xnT[:, u].rearrange("p c a r -> p c (a r)"), scratch["xnT"], s_Tst)):
                    pool.wait_ge(ready, i + 1)
                    pool.nop(nofuse=True)
                    pool.dma_start(pair_of(dst, i), src).then_inc(done[u], 16)
                if not first(k):
                    store_h(k - 1, u)

            def store_h(k, u):
                pool.wait_ge(s_h, 2 * k + u + 1)
                pool.nop(nofuse=True)
                pool.dma_start(pair_of(scratch["h"], 2 * k + u), hrow[:, u]).then_inc(s_hst[u], 16)

            over_pairs(pool, store)
            store_h(LASTK - 1, 1)
            store_h(LASTK, 0)
            for done in (s_xst, s_Tst, s_hst):
                for u in range(2):
                    pool.wait_ge(done[u], 16 * ((PAIRS + 1 - u) // 2))

        @block.tensor
        def _(pe):
            pe.wait_ge(s_w, 32)

            def turn(k, u):
                i = 2 * k + u
                pe.wait_ge(s_xn, i + 1)
                if not first(k):
                    pe.wait_ge(s_xT, i - 1)
                for c in range(2):
                    for a in range(HALF):
                        last = nc.tensor.transpose(T[u][:, (HALF * c + a) * P:(HALF * c + a + 1) * P],
                                                   xnr[:, u, c, a * P:(a + 1) * P], ident[:])
                last.then_inc(s_T, 1)

            def product(k, u):
                i = 2 * k + u
                pe.wait_ge(s_xT, i + 1)
                if not first(k):
                    pe.wait_ge(s_h, i - 1)
                    pe.wait_ge(s_max, i)
                for c in range(2):
                    for bank, w in ((H[u], wl), (K[u], wk)):
                        for a in range(HALF):
                            last = nc.tensor.matmul(bank[:, c * D:(c + 1) * D], xnT[:, u, c, a, :], w[:, a, :],
                                                    start=(a == 0), stop=(a == HALF - 1))
                last.then_inc(s_hk, 1)

            def body(k, u):
                turn(k, u)
                if not (first(k) and u == 0):
                    product(*before(k, u))
            over_pairs(pe, body)
            product(LASTK, 0)

        @block.scalar
        def _(act):
            def unload(k, u):
                i = 2 * k + u
                act.wait_ge(s_T, i + 1)
                if not first(k):
                    act.wait_ge(s_hk, i - 1)
                    act.wait_ge(s_Tst[u], 16 * k)
                nc.scalar.copy(xnT[:, u].rearrange("p c a r -> p (c a r)"), T[u][:, :]).then_inc(s_xT, 1)

            def emit(k, u):
                i = 2 * k + u
                act.wait_ge(s_hk, i + 1)
                if not first(k):
                    act.wait_ge(s_hst[u], 16 * k)
                nc.scalar.copy(flat(hrow[:, u]), H[u][:, :]).then_inc(s_h, 1)

            def body(k, u):
                i = 2 * k + u
                act.wait_ge(s_step, 4 * i + 3)
                nc.scalar.activation(std[:, u], vare[:, u], ACT.Sqrt).then_inc(s_std, 1)
                unload(k, u)
                if not first(k):
                    emit(k - 1, u)

            over_pairs(act, body)
            emit(LASTK - 1, 1)
            emit(LASTK, 0)
            act.wait_ge(s_fin, 3)
            nc.scalar.activation(gstd[:], gvar[:], ACT.Sqrt).then_inc(s_gstd, 1)


def edge_mix_phase(nc, t, scratch, psum, ident, prior, trash, ones, zeros, gscale, edges, kmax, wk):
    with ExitStack() as ctx:
        def sb(name, shape, dt=F32):
            return ctx.enter_context(nc.sbuf_tensor(name, shape, dt))

        def sem(name):
            return ctx.enter_context(nc.semaphore(name))

        srcf, wtf, dsti, locf = edges["src"], edges["weight"], edges["dst"], edges["local"]
        gidx = sb("gidx", [P, CHUNK_GROUP], I32)
        sidx = sb("sidx", [P, CHUNK_GROUP], I32)
        rows = sb("rows", [P, CHUNK_GROUP, D])
        pick = sb("pick", [P, 2, BATCH, P])
        Emat = sb("Emat", [P, 2, BATCH, P])
        seen = sb("seen", [P, BATCH, P])
        seen_sum = sb("seen_sum", [P, CHUNK_GROUP])
        Cmat = sb("Cmat", [P, 2, BATCH, P])
        msg = sb("msg", [P, 2 * BATCH, D])
        B = [psum[0], psum[7]]
        C = psum[1]
        M = [psum[2], psum[3]]
        s_gidx = sem("e_gather_rows_known")
        s_rows = [sem(f"e_rows_at_hand{h}") for h in range(2)]
        HALF_ROWS = 16 * WINDOW
        s_B = sem("e_targets_spread")
        s_E = sem("e_matrices")
        s_sidx = sem("e_add_rows_known")
        s_C = sem("e_combined")
        s_Cc = sem("e_combined_out")
        s_sum = sem("e_sums")
        s_msg = sem("e_message")
        s_add = [sem(f"e_added{r}") for r in range(NACC)]
        NB = CHUNK_GROUP // BATCH
        assert NB == 4 and BATCH == NACC and CHUNK_GROUP == 2 * WINDOW

        wq = sb("wq", [P, HALF, D])
        wqT = sb("wqT", [P, HALF, D])
        wv = sb("wv", [P, HALF, D])
        wproj = sb("wproj", [P, HALF, D])
        wg1 = sb("wg1", [P, HALF, GH])
        wg1s = sb("wg1s", [P, HALF, GH])
        wg2 = sb("wg2", [GH, D])
        lng = sb("lng", [P, HALF])
        lnb = sb("lnb", [P, HALF])
        lnb_all = sb("lnb_all", [P, HALF, P])
        bg1 = sb("bg1", [1, GH])
        bg2 = sb("bg2", [P, HALF])
        bg2h = sb("bg2h", [P, HALF])
        hbias = sb("hbias", [P, GH])
        kcol = sb("kcol", [P, HALF])
        nmax = sb("nmax", [1, D])
        xr = sb("xr", [P, 2, 2, D])
        xT = sb("xT", [P, 2, 2, HALF, P])
        ek = sb("ek", [P, 2, D])
        GTs = sb("GTs", [P, HALF, D])
        rden = sb("rden", [P, HALF])
        cm = sb("cm", [P, HALF, D])
        M1 = sb("M1", [P, HALF, D])
        hp = sb("hp", [P, 2, GH])
        hg = sb("hg", [P, 2, GH])
        hgT = sb("hgT", [GH, 2, P])
        tg = sb("tg", [P, HALF, 2 * P])
        oT = sb("oT", [P, HALF, 2 * P])
        x1 = sb("x1", [P, 2, D])
        s_w = sem("m_weights")
        s_prep = sem("m_prep")
        s_pprep = sem("m_prep_tensor")
        s_x2 = [sem(f"m_tile_loaded{s}") for s in range(2)]
        s_k = sem("m_k")
        s_ek = sem("m_exp_k")
        s_gt = sem("m_gt")
        s_ctx = sem("m_context")
        s_cv = sem("m_context_vector")
        s_x3 = [sem(f"m_pair_loaded{u}") for u in range(2)]
        s_hg = sem("m_gate_hidden")
        s_hp = sem("m_gate_hidden_scaled")
        s_ge = sem("m_gelu")
        s_ht = sem("m_gelu_turned")
        s_hgt = sem("m_gelu_turned_out")
        s_gp = sem("m_gate")
        s_th = sem("m_tanh")
        s_op = sem("m_attention_out")
        s_o = sem("m_gated")
        s_p = sem("m_projected")
        s_x1 = sem("m_x1")
        s_x1st = sem("m_x1_stored")
        block = ctx.enter_context(nc.Block())
        LASTP = PAIRS - 1

        def over_mix_pairs(engine, body):
            body(0, 0)
            body(0, 1)
            with engine.Fori(1, PAIRS // 2) as k:
                body(k, 0)
                body(k, 1)
            body(PAIRS // 2, 0)

        assert PAIRS % 2 == 1

        def take_steps(steps, *places):
            for at, what in steps:
                if at in places:
                    what()

        def halves(a):
            return a.rearrange("(a p) n -> p a n", p=P)

        def column(a):
            return a.rearrange("(a p) -> p a", p=P)

        def row(a):
            return a.rearrange("(a n) -> a n", a=1)

        def pair_rows(a, i):
            return a[bass.ds(i * 2 * P, 2 * P), :].rearrange("(a p) d -> p a d", p=P)

        weights = [(wq[:], halves(t["L0_mix_Wqkv"][:, 0:D])), (wv[:], halves(t["L0_mix_Wqkv"][:, 2 * D:3 * D])),
                   (wproj[:], halves(t["L0_mix_Wproj"])),
                   (wg1[:], halves(t["L0_mix_Wg1"])), (wg2[:], t["L0_mix_Wg2"]),
                   (lng[:], column(t["L0_mix_ln_g"])), (lnb[:], column(t["L0_mix_ln_b"])),
                   (bg1[:], row(t["L0_mix_bg1"])), (bg2[:], column(t["L0_mix_bg2"]))]
        WEIGHTS = 16 * len(weights)

        @block.sync
        def _(sp):
            for dst, src in weights:
                sp.dma_start(dst, src, allow_slow_non_contiguous=True).then_inc(s_w, 16)

            def load_window(g, h):
                if not first(g):
                    sp.wait_ge(s_sum, 2 * NB * (g - 1) + NB * (h + 1))
                    sp.nop(nofuse=True)
                gen = sp.value_load(edges["general"][0:1, bass.ds(g, 1)], min_val=0, max_val=1)
                with sp.If(gen == 0):
                    at = sp.value_load(edges["base"][0:1, bass.ds(2 * g + h, 1)], min_val=0, max_val=NPAD - P)
                    sp.dma_start(rows[:, WINDOW * h, :], scratch["h"][bass.ds(at, P), :]).then_inc(s_rows[h], 16)
                    sp.nop(nofuse=True).then_inc(s_rows[h], HALF_ROWS - 16)

            def load_tile(i, s):
                n = 2 * i + s
                if not first(i):
                    sp.wait_ge(s_gt, n - 1)
                at = bass.ds(i * 2 * P + s * P, P)
                sp.dma_start(xr[:, 0, s, :], scratch["xn"][at, :]).then_inc(s_x2[s], 16)
                sp.dma_start(xT[:, 0, s, :, :].rearrange("p a c -> p (a c)"), scratch["xnT"][at, :]).then_inc(s_x2[s], 16)

            def load_pair(k, u, last=False):
                i = 2 * k + u
                sp.dma_start(xT[:, u].rearrange("p s a c -> p s (a c)"), pair_rows(scratch["xnT"], i)).then_inc(s_x3[u], 16)
                if last:
                    sp.dma_start(xr[:, u, 0, :], t["x"][(TILES - 2) * P:(TILES - 1) * P, :]).then_inc(s_x3[u], 16)
                    sp.dma_start(xr[0:LAST, u, 1, :], t["x"][(TILES - 1) * P:N, :]).then_inc(s_x3[u], 16)
                else:
                    sp.dma_start(xr[:, u], pair_rows(t["x"], i)).then_inc(s_x3[u], 16)

            def store_pair(k, u):
                i = 2 * k + u
                sp.wait_ge(s_x1, i + 1)
                sp.nop(nofuse=True)
                sp.dma_start(pair_rows(scratch["x1"], i), x1[:]).then_inc(s_x1st, 16)

            load_window(0, 0)
            load_window(0, 1)
            load_tile(0, 0)
            load_tile(0, 1)
            with sp.Fori(1, PAIRS) as i:
                load_tile(i, 0)
                load_window(i, 0)
                load_tile(i, 1)
                load_window(i, 1)
            sp.wait_ge(s_gt, TILES)
            load_pair(0, 0)
            load_pair(0, 1)
            load_window(PAIRS, 0)
            load_window(PAIRS, 1)
            load_window(PAIRS + 1, 0)

            def mix_turn(k, u, more=True, last=False):
                load_window(PAIRS + 2 * k + u, 1)
                store_pair(*before(k, u))
                if more:
                    load_pair(*((k, 1) if u == 0 else (k + 1, 0)), last=last)
                load_window(PAIRS + 1 + 2 * k + u, 0)

            mix_turn(0, 1)
            with sp.Fori(1, PAIRS // 2 - 1) as k:
                mix_turn(k, 0)
                mix_turn(k, 1)
            mix_turn(PAIRS // 2 - 1, 0)
            mix_turn(PAIRS // 2 - 1, 1, last=True)
            mix_turn(PAIRS // 2, 0, more=False)
            store_pair(PAIRS // 2, 0)
            load_window(2 * PAIRS, 1)
            with sp.Fori(2 * PAIRS + 1, GROUPS) as g:
                load_window(g, 0)
                load_window(g, 1)
            sp.wait_ge(s_x1st, 16 * PAIRS)

        @block.gpsimd
        def _(pool):
            def gather(g, h):
                gen = pool.value_load(edges["general"][0:1, bass.ds(g, 1)], min_val=0, max_val=1)
                with pool.If(gen == 1):
                    pool.wait_ge(s_gidx, 2 * g + h + 1)
                    pool.nop(nofuse=True)
                    for j in range(WINDOW * h, WINDOW * (h + 1)):
                        pool.indirect_dma_start(rows[:, j, :], None, scratch["h"][:, :],
                                                bass.IndirectOffsetOnAxis(ap=gidx[:, j:j + 1], axis=0)).then_inc(s_rows[h], 16)

            def group(g, last=False):
                for j in range(CHUNK_GROUP):
                    b, r = j // BATCH, j % BATCH
                    if r == 0:
                        pool.wait_ge(s_sidx, NB * g + b + 1)
                    if r % 2 == 0:
                        pool.wait_ge(s_msg, 2 * (NB * g + b) + r // 2 + 1)
                    if not (first(g) and b == 0):
                        pool.wait_ge(s_add[r], 16 * (NB * g + b))
                    pool.nop(nofuse=True)
                    pool.indirect_dma_start(scratch["agg"][r][:, :],
                                            bass.IndirectOffsetOnAxis(ap=sidx[:, j:j + 1], axis=0),
                                            msg[:, j % (2 * BATCH), :], None, compute_op=ALU.add).then_inc(s_add[r], 16)
                    if not last and (j + 1) % WINDOW == 0:
                        gather(g + 1, j // WINDOW)

            gather(0, 0)
            gather(0, 1)
            group(0)
            with pool.Fori(1, GROUPS - 1) as g:
                group(g)
            group(GROUPS - 1, last=True)
            for r in range(NACC):
                pool.wait_ge(s_add[r], 16 * CHUNKS // NACC)

        @block.vector
        def _(dve):
            nc.vector.tensor_copy(gidx[:], dsti[:, 0:CHUNK_GROUP]).then_inc(s_gidx, 2)
            nc.vector.memset(cm[:], 0.0).then_inc(s_prep, 1)
            dve.wait_ge(s_pprep, 1)
            nc.vector.tensor_reduce(kcol[:], psum[4][:, 0:D].rearrange("p (a c) -> p a c", a=HALF), AX_X,
                                    ALU.max).then_inc(s_prep, 1)
            dve.wait_ge(s_w, WEIGHTS)
            for a in range(HALF):
                nc.vector.tensor_scalar(wg1s[:, a, :], wg1[:, a, :], lng[:, a:a + 1], None, ALU.mult)
                nc.vector.tensor_scalar(lnb_all[:, a, :], ones[:], lnb[:, a:a + 1], None, ALU.mult)
            nc.vector.tensor_scalar(bg2h[:], bg2[:], 0.5, None, ALU.mult).then_inc(s_prep, 1)
            dve.wait_ge(s_pprep, 2)
            nc.vector.tensor_scalar(nmax[:], psum[5][0:1, 0:D], -1.0, None, ALU.mult).then_inc(s_prep, 1)
            dve.wait_ge(s_pprep, 3)
            nc.vector.tensor_copy(hbias[:], psum[6][:, 0:GH]).then_inc(s_prep, 1)
            nc.vector.tensor_copy(wqT[:].rearrange("p a n -> p (a n)"), psum[7][:, :]).then_inc(s_prep, 1)

            def picks(g, b):
                nb = NB * g + b
                if not (first(g) and b < 2):
                    dve.wait_ge(s_C, nb - 1)
                for q in range(BATCH):
                    nc.vector.tensor_scalar(pick[:, b % 2, q, :], edges["iota"][:], locf[:, bass.ds(BATCH * nb + q, 1)],
                                            None, ALU.is_equal)

            def matrices(g, b):
                nb = NB * g + b
                dve.wait_ge(s_B, nb + 1)
                for q in range(BATCH):
                    n = bass.ds(BATCH * nb + q, 1)
                    nc.vector.tensor_scalar(Emat[:, b % 2, q, :], B[b % 2][:, q * P:(q + 1) * P], srcf[:, n], wtf[:, n],
                                            ALU.is_equal, ALU.mult)
                for q in range(BATCH):
                    last = nc.vector.scalar_tensor_tensor(out=seen[:, q, :], in0=B[b % 2][:, q * P:(q + 1) * P],
                                                          scalar=srcf[:, bass.ds(BATCH * nb + q, 1)],
                                                          in1=prior[:], op0=ALU.is_equal, op1=ALU.mult,
                                                          accum_out=seen_sum[:, BATCH * b + q:BATCH * b + q + 1])
                last.then_inc(s_E, 1)

            def add_rows(g, b, last):
                nb = NB * g + b
                dve.wait_ge(s_E, nb + 1)
                if not first(g):
                    for r in range(NACC):
                        dve.wait_ge(s_add[r], 16 * (nb - 3))
                cols = slice(BATCH * b, BATCH * (b + 1))
                nc.vector.scalar_tensor_tensor(out=sidx[:, cols], in0=seen_sum[:, cols], scalar=trash[:, 0:1],
                                               in1=srcf[:, bass.ds(BATCH * nb, BATCH)],
                                               op0=ALU.min, op1=ALU.max).then_inc(s_sidx, 1)
                if b % 2 == 1 and not last:
                    h = b // 2
                    dve.wait_ge(s_rows[h], HALF_ROWS * (g + 1))
                    nc.vector.tensor_copy(gidx[:, WINDOW * h:WINDOW * (h + 1)],
                                          dsti[:, bass.ds(CHUNK_GROUP * (g + 1) + WINDOW * h, WINDOW)]).then_inc(s_gidx, 1)

            def gate_scale(k, u):
                i = 2 * k + u
                dve.wait_ge(s_hg, i + 1)
                if not (first(k) and u == 0):
                    dve.wait_ge(s_ge, i)
                for s in range(2):
                    last = nc.vector.scalar_tensor_tensor(out=hp[:, s, :], in0=psum[4][:, s * GH:(s + 1) * GH],
                                                          scalar=gscale[:, bass.ds(2 * i + s, 1)], in1=hbias[:],
                                                          op0=ALU.mult, op1=ALU.add)
                last.then_inc(s_hp, 1)

            def gate_apply(k, u):
                i = 2 * k + u
                dve.wait_ge(s_th, i + 1)
                dve.wait_ge(s_op, i + 1)
                if not (first(k) and u == 0):
                    dve.wait_ge(s_p, i)
                nc.vector.scalar_tensor_tensor(out=oT[:].rearrange("p a c -> p (a c)"),
                                               in0=tg[:].rearrange("p a c -> p (a c)"), scalar=1.0,
                                               in1=psum[6][:, :], op0=ALU.add, op1=ALU.mult).then_inc(s_o, 1)

            def residual(k, u, last=False):
                i = 2 * k + u
                dve.wait_ge(s_p, i + 1)
                dve.wait_ge(s_x3[u], 32 * (k + 1) + 16 * last)
                if not (first(k) and u == 0):
                    dve.wait_ge(s_x1st, 16 * i)
                nc.vector.tensor_tensor(x1[:].rearrange("p a d -> p (a d)"), xr[:, u].rearrange("p a d -> p (a d)"),
                                        psum[5][:, :], ALU.add).then_inc(s_x1, 1)

            def group(g, steps, last=False):
                for b in range(NB):
                    picks(g, b)
                    take_steps(steps, 4 * b)
                    matrices(g, b)
                    add_rows(g, b, last)
                    take_steps(steps, 4 * b + 1, 4 * b + 2, 4 * b + 3)

            def mix_steps(k, u, last=False):
                steps = [(11, lambda: gate_scale(k, u))]
                if not (first(k) and u == 0):
                    steps += end_steps(*before(k, u))
                return steps

            def end_steps(k, u, last=False):
                return [(3, lambda: gate_apply(k, u)), (10, lambda: residual(k, u, last))]

            group(0, [])
            with dve.Fori(1, PAIRS) as g:
                group(g, [])
            dve.wait_ge(s_gt, TILES)
            nc.vector.tensor_copy(GTs[:].rearrange("p a n -> p (a n)"), psum[5][:, :]).then_inc(s_cv, 1)
            nc.vector.reciprocal(rden[:], psum[6][:, 0:HALF]).then_inc(s_cv, 1)
            dve.wait_ge(s_cv, 2)
            dve.wait_ge(s_ctx, 1)
            for a in range(HALF):
                for q in range(P // HD):
                    v = a * P + q * HD
                    blk = slice(q * HD, (q + 1) * HD)
                    last = nc.vector.tensor_scalar(cm[blk, a, v:v + HD], psum[4][blk, a * D + v:a * D + v + HD],
                                                   rden[blk, a:a + 1], 0.5, ALU.mult, ALU.mult)
            last.then_inc(s_cv, 1)
            dve.wait_ge(s_ctx, 2)
            nc.vector.tensor_copy(M1[:].rearrange("p a n -> p (a n)"), psum[6][:, :]).then_inc(s_cv, 1)
            over_mix_pairs(dve, lambda k, u: group(PAIRS + 2 * k + u, mix_steps(k, u)))
            group(2 * PAIRS, end_steps(PAIRS // 2, 0, last=True))
            with dve.Fori(2 * PAIRS + 1, GROUPS - 1) as g:
                group(g, [])
            group(GROUPS - 1, [], last=True)

        @block.tensor
        def _(pe):
            for a in range(HALF):
                last = nc.tensor.transpose(psum[4][:, a * P:(a + 1) * P], kmax[:, a * P:(a + 1) * P], ident[:])
            last.then_inc(s_pprep, 1)
            pe.wait_ge(s_prep, 2)
            for a in range(HALF):
                last = nc.tensor.matmul(psum[5][0:1, a * P:(a + 1) * P], kcol[:, a:a + 1], ident[:], start=True, stop=True)
            last.then_inc(s_pprep, 1)
            pe.wait_ge(s_w, WEIGHTS)
            pe.wait_ge(s_prep, 3)
            for a in range(HALF):
                nc.tensor.matmul(psum[6][:, 0:GH], lnb_all[:, a, :], wg1[:, a, :], start=(a == 0), stop=False)
            nc.tensor.matmul(psum[6][:, 0:GH], ones[0:1, :], bg1[:], start=False, stop=True)
            for a in range(HALF):
                for b in range(HALF):
                    last = nc.tensor.transpose(psum[7][:, a * D + b * P:a * D + (b + 1) * P],
                                               wq[:, b, a * P:(a + 1) * P], ident[:])
            last.then_inc(s_pprep, 1)
            pe.wait_ge(s_prep, 6)

            def spread(g, b):
                nb = NB * g + b
                if not (first(g) and b < 2):
                    pe.wait_ge(s_E, nb - 1)
                per = SPAN // NB
                nc.tensor.matmul(B[b % 2][:, :], edges["both"][:, bass.ds(NB * (g % per) + b, 1)].to_broadcast([P, P]),
                                 edges["packed"][:, bass.ds(g // per, 1), :], start=True, stop=True).then_inc(s_B, 1)

            def combine(g, b):
                nb = NB * g + b
                pe.wait_ge(s_E, nb + 1)
                if not (first(g) and b == 0):
                    pe.wait_ge(s_Cc, nb)
                for q in range(BATCH):
                    mm = nc.tensor.matmul(C[:, q * P:(q + 1) * P], pick[:, b % 2, q, :], Emat[:, b % 2, q, :],
                                          start=True, stop=True)
                mm.then_inc(s_C, 1)

            def message(g, b, p, gen):
                nb = NB * g + b
                h = b // 2
                if p == 0:
                    pe.wait_ge(s_rows[h], HALF_ROWS * (g + 1))
                    pe.wait_ge(s_Cc, nb + 1)
                if not (first(g) and b == 0):
                    pe.wait_ge(s_msg, 2 * nb - 1 + p)
                for q in (2 * p, 2 * p + 1):
                    slot = WINDOW * h + gen * (BATCH * b + q - WINDOW * h)
                    mm = nc.tensor.matmul(M[p][:, (q % 2) * D:(q % 2 + 1) * D], Cmat[:, b % 2, q, :],
                                          rows[:, bass.ds(slot, 1), :], start=True, stop=True)
                mm.then_inc(s_sum, 1)

            def keys(i, s):
                n = 2 * i + s
                pe.wait_ge(s_x2[s], 32 * (i + 1))
                if not (first(i) and s == 0):
                    pe.wait_ge(s_ek, n)
                for a in range(HALF):
                    nc.tensor.matmul(psum[4][:, 0:D], xT[:, 0, s, a, :], wk[:, a, :], start=(a == 0), stop=False)
                nc.tensor.matmul(psum[4][:, 0:D], ones[0:1, :], nmax[:], start=False, stop=True).then_inc(s_k, 1)

            def context(i, s, rws=P):
                n = 2 * i + s
                start, stop = first(i) and s == 0, rws < P
                pe.wait_ge(s_ek, n + 1)
                for a in range(HALF):
                    nc.tensor.matmul(psum[5][:, a * D:(a + 1) * D], xr[0:rws, 0, s, a * P:(a + 1) * P], ek[0:rws, s, :],
                                     start=start and a == 0, stop=stop, skip_group_check=True)
                for a in range(HALF):
                    last = nc.tensor.matmul(psum[6][:, a:a + 1], ek[0:rws, s, a * P:(a + 1) * P], ones[0:rws, 0:1],
                                            start=start and a == 0, stop=stop, skip_group_check=True)
                last.then_inc(s_gt, 1)

            def gate_hidden(k, u, last=False):
                i = 2 * k + u
                pe.wait_ge(s_x3[u], 32 * (k + 1) + 16 * last)
                if not (first(k) and u == 0):
                    pe.wait_ge(s_hgt, i)
                for s in range(2):
                    for a in range(HALF):
                        mm = nc.tensor.matmul(psum[4][:, s * GH:(s + 1) * GH], xT[:, u, s, a, :], wg1s[:, a, :],
                                              start=(a == 0), stop=(a == HALF - 1))
                mm.then_inc(s_hg, 1)

            def gate_turn(k, u):
                pe.wait_ge(s_ge, 2 * k + u + 1)
                pe.nop(nofuse=True)
                for s in range(2):
                    mm = nc.tensor.transpose(psum[4][0:GH, (s + 1) * P:(s + 2) * P], hg[:, s, :], ident[:])
                mm.then_inc(s_ht, 1)

            def gate_out(k, u):
                i = 2 * k + u
                pe.wait_ge(s_hgt, i + 1)
                if not (first(k) and u == 0):
                    pe.wait_ge(s_x1, i)
                for a in range(HALF):
                    mm = nc.tensor.matmul(psum[5][:, a * D:(a + 1) * D], wg2[:, a * P:(a + 1) * P],
                                          hgT[:].rearrange("p s c -> p (s c)"), start=True, stop=True)
                mm.then_inc(s_gp, 1)

            def attend(k, u):
                i = 2 * k + u
                if not (first(k) and u == 0):
                    pe.wait_ge(s_o, i)
                for a in range(HALF):
                    for b in range(HALF):
                        mm = nc.tensor.matmul(psum[6][:, a * D:(a + 1) * D], M1[:, b, a * P:(a + 1) * P], xT[:, u, :, b, :],
                                              start=(b == 0), stop=(b == HALF - 1))
                mm.then_inc(s_op, 1)

            def project(k, u, s):
                i = 2 * k + u
                if s == 0:
                    pe.wait_ge(s_o, i + 1)
                bank = psum[5][:, s * D:(s + 1) * D]
                for a in range(HALF):
                    mm = nc.tensor.matmul(bank, oT[:, a, s * P:(s + 1) * P], wproj[:, a, :], start=(a == 0),
                                          stop=(a == HALF - 1))
                if s == 1:
                    mm.then_inc(s_p, 1)

            def gathered(g):
                return pe.value_load(edges["general"][0:1, bass.ds(g, 1)], min_val=0, max_val=1)

            def group(g, steps, last=False):
                gen = gathered(g)
                for b in range(NB):
                    if b + 2 < NB:
                        spread(g, b + 2)
                    elif not last:
                        spread(g + 1, b + 2 - NB)
                    combine(g, b)
                    take_steps(steps, 4 * b)
                    back = (g, b - 1, gen) if b else None if first(g) else (g - 1, NB - 1, gathered(g - 1))
                    for p in range(2):
                        if back:
                            message(back[0], back[1], p, back[2])
                        take_steps(steps, *((4 * b + 1, 4 * b + 2) if p == 0 else (4 * b + 3,)))

            def context_steps(i, last=False):
                return [(0, lambda: keys(i, 0)), (4, lambda: context(i, 0)), (5, lambda: keys(i, 1)),
                        (9, lambda: context(i, 1, LAST if last else P))]

            def mix_steps(k, u):
                steps = [(3, lambda: gate_hidden(k, u, last=isinstance(k, int) and k > 0)), (9, lambda: attend(k, u)),
                         (11, lambda: gate_turn(k, u)), (12, lambda: gate_out(k, u))]
                if not (first(k) and u == 0):
                    steps += projections(*before(k, u))
                return steps

            def projections(k, u):
                return [(4, lambda: project(k, u, 0)), (7, lambda: project(k, u, 1))]

            spread(0, 0)
            spread(0, 1)
            group(0, context_steps(0))
            with pe.Fori(1, LASTP) as g:
                group(g, context_steps(g))
            group(LASTP, context_steps(LASTP, last=True))
            pe.wait_ge(s_cv, 2)
            for a in range(HALF):
                for b in range(HALF):
                    mm = nc.tensor.matmul(psum[4][:, a * D:(a + 1) * D], GTs[:, b, a * P:(a + 1) * P], wv[:, b, :],
                                          start=(b == 0), stop=(b == HALF - 1))
            mm.then_inc(s_ctx, 1)
            pe.wait_ge(s_cv, 3)
            for a in range(HALF):
                for b in range(HALF):
                    mm = nc.tensor.matmul(psum[6][:, a * D:(a + 1) * D], wqT[:, b, a * P:(a + 1) * P], cm[:, b, :],
                                          start=(b == 0), stop=(b == HALF - 1))
            mm.then_inc(s_ctx, 1)
            pe.wait_ge(s_cv, 4)
            over_mix_pairs(pe, lambda k, u: group(PAIRS + 2 * k + u, mix_steps(k, u)))
            group(2 * PAIRS, projections(PAIRS // 2, 0))
            with pe.Fori(2 * PAIRS + 1, GROUPS - 1) as g:
                group(g, [])
            group(GROUPS - 1, [], last=True)
            for p in range(2):
                message(GROUPS - 1, NB - 1, p, gathered(GROUPS - 1))

        @block.scalar
        def _(act):
            def combined(g, b):
                nb = NB * g + b
                act.wait_ge(s_C, nb + 1)
                if not (first(g) and b < 2):
                    act.wait_ge(s_sum, 2 * nb - 2)
                nc.scalar.copy(Cmat[:, b % 2].rearrange("p q c -> p (q c)"), C[:, :]).then_inc(s_Cc, 1)

            def take(g, b, p):
                nb = NB * g + b
                act.wait_ge(s_sum, 2 * nb + p + 1)
                if not (first(g) and b < 2):
                    for r in (2 * p, 2 * p + 1):
                        act.wait_ge(s_add[r], 16 * (nb - 1))
                at = BATCH * (b % 2) + 2 * p
                nc.scalar.copy(msg[:, at:at + 2, :].rearrange("p q c -> p (q c)"), M[p][:, :]).then_inc(s_msg, 1)

            def exponential(i, s):
                n = 2 * i + s
                act.wait_ge(s_k, n + 1)
                if not first(i):
                    act.wait_ge(s_gt, n - 1)
                nc.scalar.activation(ek[:, s, :], psum[4][:, 0:D], ACT.Exp).then_inc(s_ek, 1)

            def gelu(k, u):
                i = 2 * k + u
                act.wait_ge(s_hp, i + 1)
                if not (first(k) and u == 0):
                    act.wait_ge(s_ht, i)
                nc.scalar.activation(hg[:], hp[:], ACT.Gelu).then_inc(s_ge, 1)

            def gelu_out(k, u):
                i = 2 * k + u
                act.wait_ge(s_ht, i + 1)
                if not (first(k) and u == 0):
                    act.wait_ge(s_gp, i)
                nc.scalar.copy(hgT[:].rearrange("p s c -> p (s c)"), psum[4][0:GH, P:3 * P]).then_inc(s_hgt, 1)

            def tanh(k, u):
                i = 2 * k + u
                act.wait_ge(s_gp, i + 1)
                if not (first(k) and u == 0):
                    act.wait_ge(s_o, i)
                for a in range(HALF):
                    last = nc.scalar.activation(tg[:, a, :], psum[5][:, a * D:(a + 1) * D], ACT.Tanh,
                                                bias=bg2h[:, a:a + 1], scale=0.5)
                last.then_inc(s_th, 1)

            def group(g, steps):
                for b in range(NB):
                    combined(g, b)
                    take_steps(steps, 4 * b)
                    back = (g, b - 1) if b else None if first(g) else (g - 1, NB - 1)
                    for p in range(2):
                        if back:
                            take(back[0], back[1], p)
                        take_steps(steps, *((4 * b + 1, 4 * b + 2) if p == 0 else (4 * b + 3,)))

            def mix_steps(k, u):
                return [(8, lambda: gelu(k, u)), (11, lambda: gelu_out(k, u)), (14, lambda: tanh(k, u))]

            def exp_steps(i):
                return [(2, lambda: exponential(i, 0)), (7, lambda: exponential(i, 1))]

            group(0, exp_steps(0))
            with act.Fori(1, PAIRS) as g:
                group(g, exp_steps(g))
            over_mix_pairs(act, lambda k, u: group(PAIRS + 2 * k + u, mix_steps(k, u)))
            with act.Fori(2 * PAIRS, GROUPS) as g:
                group(g, [])
            for p in range(2):
                take(GROUPS - 1, NB - 1, p)


def over_pairs(engine, body):
    body(0, 0)
    body(0, 1)
    body(1, 0)
    body(1, 1)
    with engine.Fori(2, PAIRS // 2) as k:
        body(k, 0)
        body(k, 1)
    if PAIRS % 2:
        body(PAIRS // 2, 0)


def before(k, s):
    return (k, 0) if s == 1 else (k - 1, 1)


def pair_of(a, i, width=2 * P):
    return a[bass.ds(i * width, width), :].rearrange("(a p) d -> p a d", p=P)


def route_phase(nc, t, scratch, psum, ident, ones, zeros, iota8, lower, run, nodes):
    with ExitStack() as ctx:
        def sb(name, shape, dt=F32):
            return ctx.enter_context(nc.sbuf_tensor(name, shape, dt))

        def sem(name):
            return ctx.enter_context(nc.semaphore(name))

        xin = sb("r_xin", [P, 2, 2, D])
        agg = [sb(f"r_agg{r}", [P, 2, 2, D]) for r in range(NACC)]
        half = sb("r_half", [P, 2, 2, D])
        x1 = sb("r_x1", [P, 2, 2, D])
        z = sb("r_z", [P, 2, 2, ROW])
        xf = sb("r_xf", [P, 2, HALF, 2 * P])
        pos = sb("r_pos", [P, 2, 2, 2], I32)
        posf = sb("r_posf", [P, 4])
        idxf = sb("r_idxf", [P, 2, 2])
        hot = sb("r_hot", [P, 2, 2, NE], BF16)
        lowerb = sb("r_lower", [P, P], BF16)
        onesb = sb("r_ones", [P, P], BF16)
        place = sb("r_place", [P, 2, 2, NE])
        b1c = sb("r_b1c", [P, NE, HC])
        stat = sb("r_stat", [P, 2, 6])
        mv = sb("r_mv", [P, 2, 2, 2])
        vs = sb("r_vs", [P, 2, 2])
        std = sb("r_std", [P, 2, 2])
        scl = sb("r_scl", [P, 2, 2])
        lg = sb("r_lg", [P, 2, NE])
        top = sb("r_top", [P, 2, NE])
        idx = sb("r_idx", [P, 2, NE], U32)
        gamma = sb("r_gamma", [P, HALF])
        beta = sb("r_beta", [P, HALF])
        wrt = sb("r_wrt", [P, HALF, NE])
        br = sb("r_br", [1, NE])
        xT = sb("r_xT", [P, 2, 2, HALF, P])
        wr = sb("r_wr", [P, HALF, D])
        brows = sb("r_brows", [1, 3, D])
        bsum = sb("r_bsum", [1, D])
        s_w = sem("r_weights")
        s_bias = sem("r_bias_sum")
        s_ldT = [sem(f"r_xnT_loaded{s}") for s in range(2)]
        s_lin = sem("r_linear")
        LIN = [psum[6], psum[7]]
        s_ld = [sem(f"r_loaded{s}") for s in range(2)]
        s_ld2 = [sem(f"r_loaded_rest{s}") for s in range(2)]
        s_half = sem("r_half_sum")
        s_sum = sem("r_sum")
        s_st = sem("r_stat_step")
        s_std = sem("r_std")
        s_scl = sem("r_scale")
        s_z = sem("r_z")
        s_T = sem("r_turned")
        s_xf = sem("r_xf")
        s_L = sem("r_logits")
        s_lg = sem("r_route_step")
        s_hot = sem("r_one_hots")
        s_bits = sem("r_bit_matrices")
        s_rank = sem("r_ranks")
        s_pos = sem("r_positions")
        s_sent = [sem(f"r_sent{m}") for m in range(2)]
        s_aux = sem("r_aux")
        s_x1st = [sem(f"r_x1_stored{s}") for s in range(2)]
        T = [psum[0], psum[1]]
        L = [psum[2], psum[3]]
        R = [psum[4], psum[5]]
        block = ctx.enter_context(nc.Block())

        @block.sync
        def _(sp):
            for dst, src in ((gamma[:], t["L0_ffn_gamma"].rearrange("(a p) -> p a", p=P)),
                             (beta[:], t["L0_ffn_beta"].rearrange("(a p) -> p a", p=P)),
                             (wrt[:], t["L0_ffn_Wr"].rearrange("(a p) n -> p a n", p=P)),
                             (br[:], t["L0_ffn_br"].rearrange("(a n) -> a n", a=1)),
                             (wr[:], t["L0_gnn_weight_r"].rearrange("(a p) n -> p a n", p=P)),
                             (brows[:, 0, :], t["L0_gnn_bias_l"].rearrange("(a n) -> a n", a=1)),
                             (brows[:, 1, :], t["L0_gnn_bias_r"].rearrange("(a n) -> a n", a=1)),
                             (brows[:, 2, :], t["L0_mix_bproj"].rearrange("(a n) -> a n", a=1))):
                sp.dma_start(dst, src, allow_slow_non_contiguous=True).then_inc(s_w, 16)

            def load(k, s):
                i = 2 * k + s
                if not first(k):
                    sp.wait_ge(s_sum, 4 * i - 4)
                    sp.nop(nofuse=True)
                sp.dma_start(xT[:, s].rearrange("p c a r -> p c (a r)"), pair_of(scratch["xnT"], i)).then_inc(s_ldT[s], 16)
                sp.dma_start(xin[:, s], pair_of(scratch["x1"], i)).then_inc(s_ld[s], 16)
                for r in range(NACC):
                    sp.dma_start(agg[r][:, s], pair_of(scratch["agg"][r], i)).then_inc((s_ld if r < 2 else s_ld2)[s], 16)

            def store_x1(k, s):
                sp.wait_ge(s_sum, 4 * (2 * k + s) + 4)
                sp.nop(nofuse=True)
                sp.dma_start(pair_of(scratch["x1"], 2 * k + s), x1[:, s]).then_inc(s_x1st[s], 16)

            def body(k, s):
                if not (isinstance(k, int) and 2 * k + s == PAIRS - 1):
                    load(*((k, 1) if s == 0 else (k + 1, 0)))
                store_x1(k, s)

            load(0, 0)
            for e in range(NE):
                sp.dma_start(b1c[:, e, :], t["L0_ffn_b1"][e].rearrange("(c p) -> p c", p=P),
                             allow_slow_non_contiguous=True).then_inc(s_aux, 16)
            sp.dma_start(scratch["x1"][TRASH:TRASH + P, :], zeros[:, 0:D]).then_inc(s_aux, 16)
            sp.wait_ge(s_aux, 16 * (NE + 1))
            sp.dma_start(scratch["b1"].rearrange("e p c -> p e c"), b1c[:]).then_inc(s_aux, 16)
            over_pairs(sp, body)
            sp.wait_ge(s_aux, 16 * (NE + 2))
            for s in range(2):
                sp.wait_ge(s_x1st[s], 16 * ((PAIRS + 1 - s) // 2))
                sp.nop(nofuse=True)

        @block.gpsimd
        def _(pool):
            def add_half(k, s):
                i = 2 * k + s
                pool.wait_ge(s_ld2[s], 32 * k + 32)
                if not first(k):
                    pool.wait_ge(s_sum, 4 * i - 4)
                nc.gpsimd.tensor_tensor(half[:, s], agg[2][:, s], agg[3][:, s], ALU.add).then_inc(s_half, 1)

            def body(k, s):
                if not (isinstance(k, int) and 2 * k + s == PAIRS - 1):
                    add_half(*((k, 1) if s == 0 else (k + 1, 0)))
                if not (first(k) and s == 0):
                    send(*before(k, s))

            def send(k, s):
                i = 2 * k + s
                pool.wait_ge(s_pos, 5 * i + 5)
                for c in range(2):
                    for m in range(2):
                        if not (first(k) and s == 0 and c == 0):
                            pool.wait_ge(s_sent[m], 16 * (2 * i + c))
                        pool.nop(nofuse=True)
                        pool.indirect_dma_start(scratch["table"][m][:, :],
                                                bass.IndirectOffsetOnAxis(ap=pos[:, s, c, m:m + 1], axis=0),
                                                z[:, s, c, :], None).then_inc(s_sent[m], 16)
            add_half(0, 0)
            over_pairs(pool, body)
            send(*divmod(PAIRS - 1, 2))
            for m in range(2):
                pool.wait_ge(s_sent[m], 16 * TILES)

        @block.vector
        def _(dve):
            nc.vector.tensor_copy(lowerb[:], lower[:])
            nc.vector.tensor_copy(onesb[:], ones[:]).then_inc(s_bits, 1)
            dve.wait_ge(s_w, 128)
            nc.vector.tensor_tensor(bsum[:], brows[:, 0, :], brows[:, 1, :], ALU.add).then_inc(s_bias, 1)
            dve.wait_ge(s_bias, 1)
            nc.vector.tensor_tensor(bsum[:], bsum[:], brows[:, 2, :], ALU.add).then_inc(s_bias, 1)

            def gather_sums(k, s):
                i = 2 * k + s
                dve.wait_ge(s_ld[s], 48 * k + 48)
                if not first(k):
                    dve.wait_ge(s_z, i - 1)
                    dve.wait_ge(s_x1st[s], 16 * k)
                nc.vector.tensor_tensor(x1[:, s], xin[:, s], agg[0][:, s], ALU.add).then_inc(s_sum, 1)
                dve.wait_ge(s_sum, 4 * i + 1)
                nc.vector.tensor_tensor(x1[:, s], x1[:, s], agg[1][:, s], ALU.add).then_inc(s_sum, 1)
                dve.wait_ge(s_sum, 4 * i + 2)
                dve.wait_ge(s_half, i + 1)
                nc.vector.tensor_tensor(x1[:, s], x1[:, s], half[:, s], ALU.add).then_inc(s_sum, 1)
                dve.wait_ge(s_sum, 4 * i + 3)
                dve.wait_ge(s_lin, i + 1)
                flat = x1[:, s].rearrange("p c d -> p (c d)")
                nc.vector.tensor_tensor(flat, flat, LIN[s][:, :], ALU.add).then_inc(s_sum, 1)

            def statistics(k, s):
                i = 2 * k + s
                dve.wait_ge(s_sum, 4 * i + 4)
                for c in range(2):
                    last = nc.vector.bn_stats(stat[:, c, :], x1[:, s, c, :])
                last.then_inc(s_st, 1)
                dve.wait_ge(s_st, 3 * i + 1)
                dve.nop(nofuse=True)
                for c in range(2):
                    last = nc.vector.bn_aggr(mv[:, s, c, :], stat[:, c, :])
                last.then_inc(s_st, 1)
                dve.wait_ge(s_st, 3 * i + 2)
                nc.vector.tensor_scalar(vs[:, s], mv[:, s, :, 1], 1.0 + EPS, EPS * EPS, ALU.mult, ALU.add).then_inc(s_st, 1)

            def normalise(k, s):
                i = 2 * k + s
                dve.wait_ge(s_std, i + 1)
                nc.vector.reciprocal(scl[:, s], std[:, s]).then_inc(s_scl, 1)
                dve.wait_ge(s_scl, i + 1)
                if not first(k):
                    dve.wait_ge(s_T, i - 1)
                    dve.wait_ge(s_sent[0], 16 * (2 * i - 2))
                    dve.wait_ge(s_sent[1], 16 * (2 * i - 2))
                nc.vector.tensor_copy(z[:, s, :, D], nodes[:, bass.ds(2 * i, 2)])
                for c in range(2):
                    last = nc.vector.tensor_scalar(z[:, s, c, 0:D], x1[:, s, c, :], mv[:, s, c, 0:1], scl[:, s, c:c + 1],
                                                   ALU.subtract, ALU.mult)
                last.then_inc(s_z, 1)

            def route(k, s):
                i = 2 * k + s
                dve.wait_ge(s_L, i + 1)
                nc.vector.tensor_copy(lg[:], L[s][:, 0:2 * NE].rearrange("p (a e) -> p a e", a=2)).then_inc(s_lg, 1)
                dve.wait_ge(s_lg, 5 * i + 1)
                dve.nop(nofuse=True)
                for c in range(2):
                    last = nc.vector.max(top[:, c, :], lg[:, c, :])
                last.then_inc(s_lg, 1)
                dve.wait_ge(s_lg, 5 * i + 2)
                dve.nop(nofuse=True)
                for c in range(2):
                    last = nc.vector.max_index(idx[:, c, :], top[:, c, :], lg[:, c, :])
                last.then_inc(s_lg, 1)
                nc.vector.tensor_tensor(z[:, s, :, D + 1], top[:, :, 0], top[:, :, 1], ALU.subtract)
                nc.vector.tensor_tensor(z[:, s, :, D + 2], top[:, :, 1], top[:, :, 0], ALU.subtract).then_inc(s_lg, 1)
                dve.wait_ge(s_lg, 5 * i + 4)
                nc.vector.tensor_copy(idxf[:], idx[:, :, 0:2]).then_inc(s_lg, 1)
                dve.wait_ge(s_lg, 5 * i + 5)
                if not (first(k) and s == 0):
                    dve.wait_ge(s_rank, i)
                hot_rows = hot[:].rearrange("p c m e -> p (c m) e")
                nc.vector.tensor_tensor(hot_rows, idxf[:].rearrange("p c (m a) -> p (c m) a", a=1).to_broadcast([P, 4, NE]),
                                        iota8[:].rearrange("p (a e) -> p a e", a=1).to_broadcast([P, 4, NE]),
                                        ALU.is_equal).then_inc(s_hot, 1)

            def position(k, s):
                i = 2 * k + s
                dve.wait_ge(s_rank, i + 1)
                for c in range(2):
                    last = nc.vector.tensor_tensor(place[:, c].rearrange("p m e -> p (m e)"),
                                                   R[s][:, c * 2 * NE:(c + 1) * 2 * NE], run[:], ALU.add)
                last.then_inc(s_pos, 1)
                dve.wait_ge(s_pos, 5 * i + 1)
                nc.vector.tensor_tensor(run[:], run[:], R[s][:, 4 * NE:6 * NE], ALU.add).then_inc(s_pos, 1)
                nc.vector.tensor_tensor(place[:], place[:], hot[:], ALU.mult).then_inc(s_pos, 1)
                dve.wait_ge(s_pos, 5 * i + 3)
                nc.vector.tensor_reduce(posf[:], place[:].rearrange("p c m e -> p (c m) e"), AX_X, ALU.add).then_inc(s_pos, 1)
                dve.wait_ge(s_pos, 5 * i + 4)
                if not first(k):
                    dve.wait_ge(s_sent[0], 16 * (2 * i - 2))
                    dve.wait_ge(s_sent[1], 16 * (2 * i - 2))
                nc.vector.tensor_copy(pos[:, s].rearrange("p c m -> p (c m)"), posf[:]).then_inc(s_pos, 1)

            def body(k, s):
                gather_sums(k, s)
                statistics(k, s)
                if not (first(k) and s == 0):
                    route(*before(k, s))
                    position(*before(k, s))
                normalise(k, s)

            over_pairs(dve, body)
            route(*divmod(PAIRS - 1, 2))
            position(*divmod(PAIRS - 1, 2))

        @block.tensor
        def _(pe):
            pe.wait_ge(s_w, 128)
            pe.wait_ge(s_bits, 1)
            pe.wait_ge(s_bias, 2)

            def linear(k, s, c):
                i = 2 * k + s
                if c == 0:
                    pe.wait_ge(s_ldT[s], 16 * k + 16)
                    if not first(k):
                        pe.wait_ge(s_sum, 4 * i - 4)
                bank = LIN[s][:, c * D:(c + 1) * D]
                for a in range(HALF):
                    nc.tensor.matmul(bank, xT[:, s, c, a, :], wr[:, a, :], start=(a == 0), stop=False)
                mm = nc.tensor.matmul(bank, ones[0:1, :], bsum[:], start=False, stop=True)
                if c == 1:
                    mm.then_inc(s_lin, 1)

            def turn(k, s):
                i = 2 * k + s
                pe.wait_ge(s_z, i + 1)
                if not first(k):
                    pe.wait_ge(s_xf, i - 1)
                for c in range(2):
                    for a in range(HALF):
                        mm = nc.tensor.transpose(T[s][:, a * D + c * P:a * D + (c + 1) * P],
                                                 z[:, s, c, a * P:(a + 1) * P], ident[:])
                mm.then_inc(s_T, 1)

            def logits(k, s):
                i = 2 * k + s
                pe.wait_ge(s_xf, i + 1)
                if not first(k):
                    pe.wait_ge(s_lg, 5 * i - 9)
                for c in range(2):
                    bank = L[s][:, c * NE:(c + 1) * NE]
                    for a in range(HALF):
                        nc.tensor.matmul(bank, xf[:, s, a, c * P:(c + 1) * P], wrt[:, a, :], start=(a == 0), stop=False)
                    mm = nc.tensor.matmul(bank, ones[0:1, :], br[:], start=False, stop=True)
                mm.then_inc(s_L, 1)

            def rank(k, s):
                i = 2 * k + s
                pe.wait_ge(s_hot, i + 1)
                if not first(k):
                    pe.wait_ge(s_pos, 5 * i - 6)
                ohs = [hot[:, c].rearrange("p m e -> p (m e)") for c in range(2)]
                w = 2 * NE
                nc.tensor.matmul(R[s][:, 0:w], lowerb[:], ohs[0], start=True, stop=True)
                nc.tensor.matmul(R[s][:, w:2 * w], lowerb[:], ohs[1], start=True, stop=False)
                nc.tensor.matmul(R[s][:, w:2 * w], onesb[:], ohs[0], start=False, stop=True)
                nc.tensor.matmul(R[s][:, 2 * w:3 * w], onesb[:], ohs[0], start=True, stop=False)
                nc.tensor.matmul(R[s][:, 2 * w:3 * w], onesb[:], ohs[1], start=False, stop=True).then_inc(s_rank, 1)

            def body(k, s):
                more = not (isinstance(k, int) and 2 * k + s == PAIRS - 1)
                after = (k, 1) if s == 0 else (k + 1, 0)
                if not (first(k) and s == 0):
                    rank(*before(k, s))
                if more:
                    linear(*after, 0)
                turn(k, s)
                if more:
                    linear(*after, 1)
                logits(k, s)
            linear(0, 0, 0)
            linear(0, 0, 1)
            over_pairs(pe, body)
            rank(*divmod(PAIRS - 1, 2))

        @block.scalar
        def _(act):
            def body(k, s):
                i = 2 * k + s
                act.wait_ge(s_st, 3 * i + 3)
                nc.scalar.activation(std[:, s], vs[:, s], ACT.Sqrt).then_inc(s_std, 1)
                act.wait_ge(s_T, i + 1)
                if not first(k):
                    act.wait_ge(s_L, i - 1)
                for a in range(HALF):
                    last = nc.scalar.activation(xf[:, s, a, :], T[s][:, a * D:(a + 1) * D], ACT.Identity,
                                                bias=beta[:, a:a + 1], scale=gamma[:, a:a + 1])
                last.then_inc(s_xf, 1)
            act.wait_ge(s_w, 128)
            over_pairs(act, body)


def plan_phase(nc, scratch, iotaq, base, run, offset, expert, trash):
    with ExitStack() as ctx:
        def sb(name, shape, dt=F32):
            return ctx.enter_context(nc.sbuf_tensor(name, shape, dt))

        def sem(name):
            return ctx.enter_context(nc.semaphore(name))

        fill = sb("p_fill", [P, 2, ROW])
        ends = sb("p_ends", [1, 2 * NE], I32)
        count = sb("p_count", [1, 2 * NE])
        whole = sb("p_whole", [1, 2 * NE], I32)
        blocks = sb("p_blocks", [1, 2, NE])
        upto = sb("p_upto", [1, 2, NE])
        past = sb("p_past", [1, 2, BLOCKS, NE])
        taken = sb("p_taken", [1, 2, BLOCKS, NE])
        pe_ = sb("p_expert", [1, 2, BLOCKS])
        po = sb("p_offset", [1, 2, BLOCKS])
        pt = sb("p_blocks_before", [1, 2, BLOCKS])
        s_v = sem("p_step")
        s_fill = sem("p_fill_ready")
        s_st = [sem(f"p_filled{m}") for m in range(2)]
        block = ctx.enter_context(nc.Block())

        @block.vector
        def _(dve):
            done = [0]

            def step(*ins):
                for i in ins:
                    i.then_inc(s_v, 1)
                done[0] += len(ins)
                dve.wait_ge(s_v, done[0])

            nc.vector.memset(fill[:], 0.0).then_inc(s_fill, 1)
            dve.wait_ge(s_fill, 1)
            for c in range(2):
                last = nc.vector.tensor_copy(fill[:, c, D:D + 1], trash[:, 0:1])
            last.then_inc(s_fill, 1)
            nc.vector.tensor_copy(ends[:], run[0:1, :]).then_inc(s_fill, 1)
            step(nc.vector.tensor_tensor(count[:], run[0:1, :], base[0:1, :], ALU.subtract))
            step(nc.vector.tensor_scalar(whole[:], count[:], float(CAP - 1), None, ALU.add))
            step(nc.vector.tensor_scalar(whole[:], whole[:], CAP.bit_length() - 1, None, ALU.arith_shift_right))
            step(nc.vector.tensor_copy(blocks[:].rearrange("p m e -> p (m e)"), whole[:]))
            step(nc.vector.tensor_copy(upto[:], blocks[:]))
            for e in range(1, NE):
                step(nc.vector.tensor_tensor(upto[:, :, e], upto[:, :, e], upto[:, :, e - 1], ALU.add))
            turns = iotaq[0:1, :].rearrange("p (q a) -> p q a", a=1).to_broadcast([1, BLOCKS, NE])

            def both(what):
                step(*[what(m) for m in range(2)])

            both(lambda m: nc.vector.tensor_tensor(past[:, m], turns, upto[:, m:m + 1, :].to_broadcast([1, BLOCKS, NE]), ALU.is_ge))
            both(lambda m: nc.vector.tensor_tensor(taken[:, m], past[:, m], blocks[:, m:m + 1, :].to_broadcast([1, BLOCKS, NE]), ALU.mult))
            both(lambda m: nc.vector.tensor_reduce(pe_[:, m], past[:, m], AX_X, ALU.add))
            both(lambda m: nc.vector.tensor_reduce(pt[:, m], taken[:, m], AX_X, ALU.add))
            both(lambda m: nc.vector.tensor_tensor(pt[:, m], iotaq[0:1, :], pt[:, m], ALU.subtract))
            both(lambda m: nc.vector.tensor_scalar(pt[:, m], pt[:, m], float(CAP), None, ALU.mult))
            both(lambda m: nc.vector.tensor_scalar(po[:, m], pe_[:, m], float(REGION), None, ALU.mult))
            both(lambda m: nc.vector.tensor_tensor(po[:, m], po[:, m], pt[:, m], ALU.add))
            both(lambda m: nc.vector.tensor_scalar(offset[:, m * BLOCKS:(m + 1) * BLOCKS], po[:, m], float(NE * REGION), None, ALU.min))
            both(lambda m: nc.vector.tensor_scalar(expert[:, m * BLOCKS:(m + 1) * BLOCKS], pe_[:, m], float(NE - 1), None, ALU.min))

        def fill_up(engine, m):
            engine.wait_ge(s_fill, 3)
            engine.nop(nofuse=True)
            table = scratch["table"][m]
            for e in range(NE):
                at = engine.value_load(ends[0:1, m * NE + e:m * NE + e + 1], min_val=0, max_val=NE * REGION - CAP)
                engine.dma_start(table[bass.ds(at, CAP), :].rearrange("(a p) d -> p a d", p=P), fill[:]).then_inc(s_st[m], 16)
            engine.dma_start(table[NE * REGION:NE * REGION + CAP, :].rearrange("(a p) d -> p a d", p=P),
                             fill[:]).then_inc(s_st[m], 16)
            engine.wait_ge(s_st[m], 16 * (NE + 1))

        @block.sync
        def _(sp):
            fill_up(sp, 0)

        @block.scalar
        def _(act):
            fill_up(act, 1)


def expert_phase(nc, t, scratch, out, psum, ident, offset, expert):
    with ExitStack() as ctx:
        def sb(name, shape, dt=F32):
            return ctx.enter_context(nc.sbuf_tensor(name, shape, dt))

        def sem(name):
            return ctx.enter_context(nc.semaphore(name))

        zin = sb("x_zin", [P, 2, 2, ROW])
        w1 = sb("x_w1", [P, 2, HALF, HID])
        w2 = sb("x_w2", [P, 2, HC, D])
        b1 = sb("x_b1", [P, 2, HC])
        b2 = sb("x_b2", [P, 2, D])
        xf = sb("x_xf", [P, 2, HALF, CAP])
        hT = sb("x_hT", [P, 2, HC, CAP])
        th = sb("x_tanh", [P, 2, 2])
        share = sb("x_share", [P, 2, 2])
        node = sb("x_node", [P, 2, 2], I32)
        y = sb("x_y", [P, 2, 2, D])
        gamma = sb("x_gamma", [P, HALF])
        beta = sb("x_beta", [P, HALF])
        H = [psum[r] for r in range(HC)]
        Y = [psum[HC], psum[HC + 1]]
        T = [psum[6], psum[7]]
        s_w = sem("x_norm_weights")
        s_z = [sem(f"x_rows_loaded{s}") for s in range(2)]
        s_ld = [sem(f"x_weights_loaded{s}") for s in range(2)]
        s_T = sem("x_turned")
        s_xf = sem("x_xf")
        s_th = sem("x_tanh")
        s_share = sem("x_share")
        s_H = sem("x_hidden")
        s_g = sem("x_gelu")
        s_Y = sem("x_expert_out")
        s_yb = sem("x_out_biased")
        s_y = sem("x_out_weighted")
        s_add = sem("x_added")
        s_out = sem("x_out_stored")
        block = ctx.enter_context(nc.Block())
        TOTAL = 2 * BLOCKS

        def over_blocks(engine, body):
            body(0, 0, 0)
            body(0, 1, 0)
            with engine.Fori(1, BLOCKS // 2) as k:
                body(k, 0, 0)
                body(k, 1, 0)
            with engine.Fori(BLOCKS // 2, BLOCKS - 1) as k:
                body(k, 0, 1)
                body(k, 1, 1)
            body(BLOCKS - 1, 0, 1)
            body(BLOCKS - 1, 1, 1)

        @block.sync
        def _(sp):
            for dst, src in ((gamma[:], t["L0_ffn_gamma"]), (beta[:], t["L0_ffn_beta"])):
                sp.dma_start(dst, src.rearrange("(a p) -> p a", p=P), allow_slow_non_contiguous=True).then_inc(s_w, 16)

            def body(k, s, m):
                q = 2 * k + s
                at = sp.value_load(offset[0:1, bass.ds(q, 1)], min_val=0, max_val=NE * REGION)
                e = sp.value_load(expert[0:1, bass.ds(q, 1)], min_val=0, max_val=NE - 1)
                if not first(k):
                    sp.wait_ge(s_T, q - 1)
                    sp.nop(nofuse=True)
                    sp.wait_ge(s_share, q - 1)
                    sp.nop(nofuse=True)
                sp.dma_start(zin[:, s], scratch["table"][m][bass.ds(at, CAP), :].rearrange("(a p) d -> p a d", p=P)).then_inc(s_z[s], 16)
                if not first(k):
                    sp.wait_ge(s_yb, q - 1)
                    sp.nop(nofuse=True)
                sp.dma_start(w1[:, s], t["L0_ffn_W1"][bass.ds(e, 1)].rearrange("e (a p) n -> p (e a) n", p=P)).then_inc(s_ld[s], 16)
                sp.dma_start(w2[:, s], t["L0_ffn_W2"][bass.ds(e, 1)].rearrange("e (a p) n -> p (e a) n", p=P)).then_inc(s_ld[s], 16)
                sp.dma_start(b1[:, s], scratch["b1"][bass.ds(e, 1)].rearrange("e p c -> p (e c)")).then_inc(s_ld[s], 16)
                sp.dma_start(b2[:, s], t["L0_ffn_b2"][bass.ds(e, 1)].to_broadcast([P, D])).then_inc(s_ld[s], 16)

            over_blocks(sp, body)
            sp.wait_ge(s_add, 16 * 2 * TOTAL)
            whole = N // 16 * 16
            lines = 16 * (whole // 16 // 11)
            sp.dma_start(out[0:lines * 11, :].rearrange("(a b) d -> a (b d)", b=11),
                         scratch["x1"][0:lines * 11, :].rearrange("(a b) d -> a (b d)", b=11)).then_inc(s_out, 16)
            sp.dma_start(out[lines * 11:N, :], scratch["x1"][lines * 11:N, :]).then_inc(s_out, 16)
            sp.wait_ge(s_out, 32)

        @block.tensor
        def _(pe):
            def turn(k, s):
                q = 2 * k + s
                pe.wait_ge(s_z[s], 16 * k + 16)
                if not first(k):
                    pe.wait_ge(s_xf, q - 1)
                for c in range(2):
                    for a in range(HALF):
                        mm = nc.tensor.transpose(T[s][:, a * D + c * P:a * D + (c + 1) * P],
                                                 zin[:, s, c, a * P:(a + 1) * P], ident[:])
                mm.then_inc(s_T, 1)

            def body(k, s, m):
                q = 2 * k + s
                pe.wait_ge(s_ld[s], 64 * k + 64)
                pe.wait_ge(s_xf, q + 1)
                for c in range(HC):
                    if not (first(k) and s == 0):
                        pe.wait_ge(s_g, HC * (q - 1) + c + 1)
                    for a in range(HALF):
                        mm = nc.tensor.matmul(H[c][:, 0:CAP], w1[:, s, a, c * P:(c + 1) * P], xf[:, s, a, :],
                                              start=(a == 0), stop=(a == HALF - 1))
                    mm.then_inc(s_H, 1)
                if not (isinstance(k, int) and q == TOTAL - 1):
                    turn(*((k, 1) if s == 0 else (k + 1, 0)))
                if not first(k):
                    pe.wait_ge(s_yb, q - 1)
                for c in range(HC):
                    pe.wait_ge(s_g, HC * q + c + 1)
                    for h in range(2):
                        mm = nc.tensor.matmul(Y[s][:, h * D:(h + 1) * D], hT[:, s, c, h * P:(h + 1) * P],
                                              w2[:, s, c, :], start=(c == 0 and h == 0), stop=(c == HC - 1),
                                              skip_group_check=True)
                mm.then_inc(s_Y, 1)

            turn(0, 0)
            over_blocks(pe, body)

        @block.scalar
        def _(act):
            act.wait_ge(s_w, 32)

            def features(k, s):
                q = 2 * k + s
                act.wait_ge(s_T, q + 1)
                if not first(k):
                    act.wait_ge(s_H, HC * (q - 1))
                for a in range(HALF):
                    last = nc.scalar.activation(xf[:, s, a, :], T[s][:, a * D:(a + 1) * D], ACT.Identity,
                                                bias=beta[:, a:a + 1], scale=gamma[:, a:a + 1])
                last.then_inc(s_xf, 1)

            def body(k, s, m):
                q = 2 * k + s
                act.wait_ge(s_z[s], 16 * k + 16)
                if not first(k):
                    act.wait_ge(s_share, q - 1)
                nc.scalar.activation(th[:, s], zin[:, s, :, D + 1 + m], ACT.Tanh, scale=0.5).then_inc(s_th, 1)
                act.wait_ge(s_ld[s], 64 * k + 64)
                for c in range(HC):
                    act.wait_ge(s_H, HC * q + c + 1)
                    if c == 0 and not first(k):
                        act.wait_ge(s_Y, q - 1)
                    nc.scalar.activation(hT[:, s, c, :], H[c][:, 0:CAP], ACT.Gelu, bias=b1[:, s, c:c + 1]).then_inc(s_g, 1)
                if not (isinstance(k, int) and q == TOTAL - 1):
                    features(*((k, 1) if s == 0 else (k + 1, 0)))

            features(0, 0)
            over_blocks(act, body)

        @block.vector
        def _(dve):
            def body(k, s, m):
                q = 2 * k + s
                dve.wait_ge(s_th, q + 1)
                if not first(k):
                    dve.wait_ge(s_add, 32 * (q - 1))
                nc.vector.tensor_copy(node[:, s], zin[:, s, :, D])
                nc.vector.tensor_scalar(share[:, s], th[:, s], 0.5, 0.5, ALU.mult, ALU.add).then_inc(s_share, 1)
                dve.wait_ge(s_ld[s], 64 * k + 64)
                dve.wait_ge(s_Y, q + 1)
                for c in range(2):
                    last = nc.vector.tensor_tensor(y[:, s, c, :], Y[s][:, c * D:(c + 1) * D], b2[:, s], ALU.add)
                last.then_inc(s_yb, 1)
                dve.wait_ge(s_yb, q + 1)
                dve.wait_ge(s_share, q + 1)
                for c in range(2):
                    nc.vector.tensor_scalar(y[:, s, c, :], y[:, s, c, :], share[:, s, c:c + 1], None,
                                            ALU.mult).then_inc(s_y, 1)
            over_blocks(dve, body)

        @block.gpsimd
        def _(pool):
            def body(k, s, m):
                q = 2 * k + s
                for c in range(2):
                    pool.wait_ge(s_y, 2 * q + c + 1)
                    if not (first(k) and s == 0 and c == 0):
                        pool.wait_ge(s_add, 16 * (2 * q + c))
                    pool.nop(nofuse=True)
                    pool.indirect_dma_start(scratch["x1"][:, :],
                                            bass.IndirectOffsetOnAxis(ap=node[:, s, c:c + 1], axis=0),
                                            y[:, s, c, :], None, compute_op=ALU.add).then_inc(s_add, 16)
            over_blocks(pool, body)


_INS = ['x', 'src', 'dst', 'edge_weight', 'L0_gnn_weight_l', 'L0_gnn_bias_l', 'L0_gnn_weight_r', 'L0_gnn_bias_r',
        'L0_mix_Wqkv', 'L0_mix_Wproj', 'L0_mix_bproj', 'L0_mix_ln_g', 'L0_mix_ln_b', 'L0_mix_Wg1', 'L0_mix_bg1',
        'L0_mix_Wg2', 'L0_mix_bg2', 'L0_ffn_gamma', 'L0_ffn_beta', 'L0_ffn_Wr', 'L0_ffn_br', 'L0_ffn_W1',
        'L0_ffn_b1', 'L0_ffn_W2', 'L0_ffn_b2']


def kernel(**inputs):
    import numpy as _np
    import concourse.bacc as _bacc
    from concourse import mybir as _mybir
    from concourse.bass_utils import run_bass_kernel_spmd as _run

    nc = _bacc.Bacc("TRN2", target_bir_lowering=False, num_devices=1)
    arrays, t = {}, {}
    for name in _INS:
        a = _np.ascontiguousarray(inputs[name])
        arrays[f"in_{name}_dram"] = a
        t[name] = nc.dram_tensor(f"in_{name}_dram", a.shape, _mybir.dt.from_np(a.dtype), kind="ExternalInput").ap()

    def internal(name, shape, dtype=_mybir.dt.float32):
        return nc.dram_tensor(name, shape, dtype, kind="Internal").ap()

    scratch = {"xn": internal("xn_rows", (NPAD, D)), "xnT": internal("xn_turned", (NPAD, D)),
               "h": internal("h_rows", (NPAD, D)), "x1": internal("x1_rows", (AGG_ROWS, D)),
               "base": internal("window_bases", (CHUNKS // WINDOW,), _mybir.dt.int32),
               "general": internal("general_groups", (GROUPS,), _mybir.dt.int32),
               "b1": internal("b1_turned", (NE, P, HC)),
               "table": [internal(f"table{m}", (NE * REGION + CAP, ROW)) for m in range(2)],
               "agg": [internal(f"agg{r}", (AGG_ROWS, D)) for r in range(NACC)]}
    out = nc.dram_tensor("out_0_dram", (N, D), _mybir.dt.float32, kind="ExternalOutput").ap()
    build(nc, t, scratch, out)
    r = _run(nc, [arrays], core_ids=[0])
    return r.results[0]["out_0_dram"]
```
